# Optimizing a Trainium2 kernel written in Bass

```python
import numpy as np
import jax
import jax.numpy as jnp

def _softmax(x, axis=-1):
    return jax.nn.softmax(x, axis=axis)

def _gelu(x):
    return jax.nn.gelu(x, approximate=True)

def _silu(x):
    return jax.nn.silu(x)

def _sigmoid(x):
    return jax.nn.sigmoid(x)

def _layernorm(x, axis=-1, eps=1e-05):
    m = jnp.mean(x, axis=axis, keepdims=True)
    v = jnp.var(x, axis=axis, keepdims=True)
    return (x - m) / jnp.sqrt(v + eps)

def _scatter_add(tgt, idx, src, axis=0):
    return tgt.at[idx].add(src)

def _segment_sum(src, seg, n):
    return jax.ops.segment_sum(src, seg, n)
kernel_name = 'mk_hybrid_d1_jaxref_r8_7341fe'

def setup_inputs(seed: int=0):
    np.random.seed(seed)
    _w = jnp.asarray

    def _L0_attn_a_setup():
        import jax, jax.numpy as jnp
        import numpy as np
        D_MODEL = 128
        N_HEADS = 16
        HEAD_DIM = D_MODEL // N_HEADS
        NEG_INF = jnp.float32(-1e+30)

        def _alibi_causal_mask(S, dtype):
            q = jnp.arange(S)[:, None]
            k = jnp.arange(S)[None, :]
            return jnp.where(k <= q, -(q - k).astype(dtype), NEG_INF)
        key = jax.random.key(seed)
        ks = jax.random.split(key, 5)
        B, S, D = (4, 256, D_MODEL)
        scale = 1.0 / np.sqrt(D)
        x = jax.random.normal(ks[0], (B, S, D), dtype=jnp.float32)
        w_qkv = jax.random.normal(ks[1], (3 * D, D), dtype=jnp.float32) * scale
        b_qkv = jnp.zeros((3 * D,), dtype=jnp.float32)
        w_out = jax.random.normal(ks[2], (D, D), dtype=jnp.float32) * scale
        b_out = jnp.zeros((D,), dtype=jnp.float32)
        return {'x': x, 'w_qkv': w_qkv, 'b_qkv': b_qkv, 'w_out': w_out, 'b_out': b_out}
    _L0_attn_a_in = _L0_attn_a_setup()

    def _L0_attn_b_setup():
        import jax, jax.numpy as jnp
        import numpy as np
        HIDDEN = 128
        HEADS = 16
        HEAD_DIM = HIDDEN // HEADS
        SEQ = 256
        BATCH = 1
        HH_RATIO = 0.1
        COMP_RATIO = 8
        STREAM_WIN = 128

        def _compress_states(states, ratio):
            B, H, S, D = states.shape
            L = (S + ratio - 1) // ratio
            flat = states.reshape(B * H, S, D)
            token_imp = jax.nn.softmax(jnp.linalg.norm(flat, axis=-1), axis=-1)
            pad = L * ratio - S
            if pad > 0:
                flat = jnp.pad(flat, ((0, 0), (0, pad), (0, 0)))
                token_imp = jnp.pad(token_imp, ((0, 0), (0, pad)))
            flat = flat.reshape(B * H, L, ratio, D)
            w = token_imp.reshape(B * H, L, ratio)
            pooled = (flat * w[..., None]).sum(axis=2) / (w.sum(axis=2, keepdims=True) + 1e-08)
            return pooled.reshape(B, H, L, D)

        def _heavy_hitter_indices(scores, seq_len):
            entropy = -jnp.sum(scores * jnp.log(jnp.clip(scores, 1e-08)), axis=-1)
            max_attn = scores.max(axis=-1)
            influence = scores.sum(axis=-2)
            importance = -entropy.mean(axis=1) * 0.4 + max_attn.mean(axis=1) * 0.3 + influence.mean(axis=1) * 0.3
            k = min(128, int(seq_len * HH_RATIO))
            _, idx = jax.lax.top_k(importance, k)
            return idx
        key = jax.random.key(seed)
        ks = jax.random.split(key, 5)
        s = 0.02
        return {'x': jax.random.normal(ks[0], (BATCH, SEQ, HIDDEN), jnp.float32), 'Wq': jax.random.normal(ks[1], (HIDDEN, HIDDEN), jnp.float32) * s, 'Wk': jax.random.normal(ks[2], (HIDDEN, HIDDEN), jnp.float32) * s, 'Wv': jax.random.normal(ks[3], (HIDDEN, HIDDEN), jnp.float32) * s, 'Wo': jax.random.normal(ks[4], (HIDDEN, HIDDEN), jnp.float32) * s}
    _L0_attn_b_in = _L0_attn_b_setup()

    def _L0_ffn_setup():
        import jax, jax.numpy as jnp
        import numpy as np
        DIM = 128
        HIDDEN = 384
        SCALE = 1.0 / 127.0

        def _dequant(w_int, dtype):
            return w_int.astype(dtype) * jnp.asarray(SCALE, dtype)
        key = jax.random.key(seed)
        k_x, k_g, k_u, k_d = jax.random.split(key, 4)
        x = jax.random.normal(k_x, (4, 256, DIM), dtype=jnp.float32)
        w_gate = jax.random.randint(k_g, (HIDDEN, DIM), -127, 128, dtype=jnp.int32)
        w_up = jax.random.randint(k_u, (HIDDEN, DIM), -127, 128, dtype=jnp.int32)
        w_down = jax.random.randint(k_d, (DIM, HIDDEN), -127, 128, dtype=jnp.int32)
        return {'x': x, 'w_gate': w_gate, 'w_up': w_up, 'w_down': w_down}
    _L0_ffn_in = _L0_ffn_setup()
    _d = {'L0_attn_a_x': _L0_attn_a_in['x'], 'L0_attn_a_w_qkv': _L0_attn_a_in['w_qkv'], 'L0_attn_a_b_qkv': _L0_attn_a_in['b_qkv'], 'L0_attn_a_w_out': _L0_attn_a_in['w_out'], 'L0_attn_a_b_out': _L0_attn_a_in['b_out'], 'L0_attn_b_Wq': _L0_attn_b_in['Wq'], 'L0_attn_b_Wk': _L0_attn_b_in['Wk'], 'L0_attn_b_Wv': _L0_attn_b_in['Wv'], 'L0_attn_b_Wo': _L0_attn_b_in['Wo'], 'L0_ffn_w_gate': _L0_ffn_in['w_gate'], 'L0_ffn_w_up': _L0_ffn_in['w_up'], 'L0_ffn_w_down': _L0_ffn_in['w_down']}
    _x0 = _d['L0_attn_a_x']
    _d['L0_attn_a_x'] = jax.random.normal(jax.random.fold_in(jax.random.key(seed), 1), (8, 512, 128), dtype=_x0.dtype)
    del _x0
    return _d

def reference(L0_attn_a_x, L0_attn_a_w_qkv, L0_attn_a_b_qkv, L0_attn_a_w_out, L0_attn_a_b_out, L0_attn_b_Wq, L0_attn_b_Wk, L0_attn_b_Wv, L0_attn_b_Wo, L0_ffn_w_gate, L0_ffn_w_up, L0_ffn_w_down):

    def _L0_attn_a_ref(x, w_qkv, b_qkv, w_out, b_out):
        import jax, jax.numpy as jnp
        import numpy as np
        D_MODEL = 128
        N_HEADS = 16
        HEAD_DIM = D_MODEL // N_HEADS
        NEG_INF = jnp.float32(-1e+30)

        def _alibi_causal_mask(S, dtype):
            q = jnp.arange(S)[:, None]
            k = jnp.arange(S)[None, :]
            return jnp.where(k <= q, -(q - k).astype(dtype), NEG_INF)
        B, S, D = x.shape
        H, hd = (N_HEADS, HEAD_DIM)
        qkv = x @ w_qkv.T + b_qkv
        q, k, v = jnp.split(qkv, 3, axis=-1)
        q = q.reshape(B, S, H, hd).transpose(0, 2, 1, 3)
        k = k.reshape(B, S, H, hd).transpose(0, 2, 1, 3)
        v = v.reshape(B, S, H, hd).transpose(0, 2, 1, 3)
        scores = jnp.einsum('bhqd,bhkd->bhqk', q, k) / np.sqrt(hd)
        scores = scores + _alibi_causal_mask(S, scores.dtype)
        probs = jax.nn.softmax(scores, axis=-1)
        out = jnp.einsum('bhqk,bhkd->bhqd', probs, v)
        out = out.transpose(0, 2, 1, 3).reshape(B, S, D)
        return out @ w_out.T + b_out

    def _L0_attn_b_ref(x, Wq, Wk, Wv, Wo):
        import jax, jax.numpy as jnp
        import numpy as np
        HIDDEN = 128
        HEADS = 16
        HEAD_DIM = HIDDEN // HEADS
        SEQ = 256
        BATCH = 1
        HH_RATIO = 0.1
        COMP_RATIO = 8
        STREAM_WIN = 128

        def _compress_states(states, ratio):
            B, H, S, D = states.shape
            L = (S + ratio - 1) // ratio
            flat = states.reshape(B * H, S, D)
            token_imp = jax.nn.softmax(jnp.linalg.norm(flat, axis=-1), axis=-1)
            pad = L * ratio - S
            if pad > 0:
                flat = jnp.pad(flat, ((0, 0), (0, pad), (0, 0)))
                token_imp = jnp.pad(token_imp, ((0, 0), (0, pad)))
            flat = flat.reshape(B * H, L, ratio, D)
            w = token_imp.reshape(B * H, L, ratio)
            pooled = (flat * w[..., None]).sum(axis=2) / (w.sum(axis=2, keepdims=True) + 1e-08)
            return pooled.reshape(B, H, L, D)

        def _heavy_hitter_indices(scores, seq_len):
            entropy = -jnp.sum(scores * jnp.log(jnp.clip(scores, 1e-08)), axis=-1)
            max_attn = scores.max(axis=-1)
            influence = scores.sum(axis=-2)
            importance = -entropy.mean(axis=1) * 0.4 + max_attn.mean(axis=1) * 0.3 + influence.mean(axis=1) * 0.3
            k = min(128, int(seq_len * HH_RATIO))
            _, idx = jax.lax.top_k(importance, k)
            return idx
        B, S, _ = x.shape
        scale = 1.0 / np.sqrt(HEAD_DIM).astype(np.float32)

        def split(t):
            return t.reshape(B, S, HEADS, HEAD_DIM).transpose(0, 2, 1, 3)
        q = split(x @ Wq)
        k = split(x @ Wk)
        v = split(x @ Wv)
        scores = jax.nn.softmax(jnp.einsum('bhqd,bhkd->bhqk', q, k) * scale, axis=-1)
        hh_idx = _heavy_hitter_indices(scores, S)
        gidx = hh_idx[:, None, :, None]
        k_hh = jnp.take_along_axis(k, gidx, axis=2)
        v_hh = jnp.take_along_axis(v, gidx, axis=2)
        ratio = min(COMP_RATIO, max(1, S // 64))
        k_c = _compress_states(k, ratio)
        v_c = _compress_states(v, ratio)
        k_cat = jnp.concatenate([k_hh, k_c], axis=2)
        v_cat = jnp.concatenate([v_hh, v_c], axis=2)
        attn = jax.nn.softmax(jnp.einsum('bhqd,bhkd->bhqk', q, k_cat) * scale, axis=-1)
        out = jnp.einsum('bhqk,bhkd->bhqd', attn, v_cat)
        out = out.transpose(0, 2, 1, 3).reshape(B, S, HIDDEN)
        return out @ Wo

    def _L0_ffn_ref(x, w_gate, w_up, w_down):
        import jax, jax.numpy as jnp
        import numpy as np
        DIM = 128
        HIDDEN = 384
        SCALE = 1.0 / 127.0

        def _dequant(w_int, dtype):
            return w_int.astype(dtype) * jnp.asarray(SCALE, dtype)
        wg = _dequant(w_gate, x.dtype)
        wu = _dequant(w_up, x.dtype)
        wd = _dequant(w_down, x.dtype)
        gate = jnp.einsum('bsd,hd->bsh', x, wg)
        up = jnp.einsum('bsd,hd->bsh', x, wu)
        h = jax.nn.silu(gate) * up
        return jnp.einsum('bsh,dh->bsd', h, wd)
    x = L0_attn_a_x
    x = x + _L0_attn_a_ref(_layernorm(x, axis=-1), L0_attn_a_w_qkv, L0_attn_a_b_qkv, L0_attn_a_w_out, L0_attn_a_b_out)
    x = x + _L0_ffn_ref(_layernorm(x, axis=-1), L0_ffn_w_gate, L0_ffn_w_up, L0_ffn_w_down)
    x = x + _L0_attn_b_ref(_layernorm(x, axis=-1), L0_attn_b_Wq, L0_attn_b_Wk, L0_attn_b_Wv, L0_attn_b_Wo)
    x = x + _L0_ffn_ref(_layernorm(x, axis=-1), L0_ffn_w_gate, L0_ffn_w_up, L0_ffn_w_down)
    return x

_drawn_inputs = setup_inputs


def setup_inputs(seed=0):
    import zlib

    import numpy as np

    out = dict(_drawn_inputs(seed))
    spreads = {'L0_attn_a_b_qkv': (0.0, 0.1), 'L0_attn_a_b_out': (0.0, 0.1)}
    factors = {'L0_attn_b_Wq': 64.0, 'L0_attn_b_Wk': 64.0, 'L0_attn_b_Wv': 64.0, 'L0_attn_b_Wo': 63.727}
    for name, (base, spread) in spreads.items():
        noise = np.random.default_rng([zlib.crc32(name.encode()), seed]).standard_normal(out[name].shape)
        drawn = base * np.exp(spread * noise) if base else spread * noise
        out[name] = jnp.asarray(drawn.astype(out[name].dtype))
    for name, factor in factors.items():
        out[name] = (out[name] * factor).astype(out[name].dtype)
    return out
```

```python
import math
from contextlib import ExitStack

import concourse.bass as bass
from concourse import mybir

ALU = mybir.AluOpType
ACT = mybir.ActivationFunctionType
F32 = mybir.dt.float32
BF16 = mybir.dt.bfloat16
I32 = mybir.dt.int32
AX_X = mybir.AxisListType.X

P = 128
EPS = 1e-5
NEG = -1e30
QSCALE = 8.0 ** -0.5
CLIP = 1e-8
LOG_CLIP = math.log(CLIP)
DMA = 16


def hybrid_block(nc, x, w_qkv, b_qkv, w_out, b_out, wq_b, wk_b, wv_b, wo_b, w_gate, w_up, w_down, out):
    B, T, D = x.shape
    H, HD = 16, D // 16
    NT = T // P
    FC = w_gate.shape[0] // P
    RATIO = min(8, max(1, T // 64))
    L = T // RATIO
    GPT = P // RATIO
    HH = min(128, int(T * 0.1))
    NK = L + HH
    HPO = H // 2
    assert D == P and T == 512 and NK <= P

    Q_PART = (0, 0, 1, 1, 0, 2)
    K_PART = (0, 1, 0, 1, 2, 0)
    NPAIR = len(Q_PART)
    AL = 4
    A_SC = AL + NPAIR * HD
    A_MX = A_SC + 3
    B_SC = NPAIR * HD
    B_MX = B_SC + 3
    TILES = (((0, 0),), ((1, 0), (3, T - P)), ((2, 0),))
    WIDTH = (T, T, T - 2 * P)

    nc.disable_value_cache = True
    with ExitStack() as ctx:
        def sb(name, shape, dt=F32):
            return ctx.enter_context(nc.sbuf_tensor(name, shape, dt))

        def sem(name):
            return ctx.enter_context(nc.semaphore(name))

        bank = [ctx.enter_context(nc.psum_tensor(f"bank{i}", [P, 512], F32)) for i in range(8)]

        identf = sb("identf", [P, P])
        identb = sb("identb", [P, P], BF16)
        onesf = sb("onesf", [P, P])
        maskqk = sb("maskqk", [P, P], BF16)
        maskkq = sb("maskkq", [P, P], BF16)
        tri = sb("tri", [P, P])
        iota_i = sb("iota_i", [P, HH], I32)
        iota_f = sb("iota_f", [P, HH])
        group = sb("group", [P, NT, L])
        half = sb("half", [P, NT * H])
        neghalf = sb("neghalf", [P, NT])
        eps = sb("eps", [P, NT])
        setup = sb("setup", [P, 8 * T])
        wload = setup[:, 0:4 * P].rearrange("p (i d) -> p i d", i=4)
        wfp = setup[:, 4 * P:4 * P + 9 * P].rearrange("p (i d) -> p i d", i=3)
        wint = setup[:, 13 * P:22 * P].bitcast(I32).rearrange("p (i d) -> p i d", i=3)
        wqkvT = sb("wqkvT", [P, 3 * P])
        woutT = sb("woutT", [P, P])
        wqb = sb("wqb", [P, 4, P])
        wgT = sb("wgT", [P, FC, P])
        wuT = sb("wuT", [P, FC, P])
        wdT = sb("wdT", [P, FC, P])
        bqk = sb("bqk", [P, 2])
        bqs = sb("bqs", [P, 1])
        bv = sb("bv", [P, P])
        bo = sb("bo", [P, P])

        xs = [sb(f"x{u}", [P, NT, P]) for u in range(5)]
        xbo = sb("xbo", [P, NT, P])
        st = [sb(f"st{u}", [P, NT, 6]) for u in range(4)]
        mv = [sb(f"mv{u}", [P, NT, 2]) for u in range(4)]
        ve = [sb(f"ve{u}", [P, NT]) for u in range(4)]
        rstd = [sb(f"rstd{u}", [P, NT]) for u in range(4)]
        xn = [sb(f"xn{s}", [P, NT, P]) for s in range(2)]
        xnT = [sb(f"xnT{s}", [P, T]) for s in range(2)]
        qf = [sb(f"qf{s}", [P, 2, T]) for s in range(2)]
        rest = [sb(f"rest{s}", [P, 2, T]) for s in range(2)]
        part = [sb(f"part{s}", [P, 2, 3, T], BF16) for s in range(2)]
        q_stacks = sb("q_stacks", [P, H, T], BF16)
        k_stacks = sb("k_stacks", [P, H, T], BF16)
        qst = [q_stacks[64 * s:64 * s + 64, :, :] for s in range(2)]
        kst = [k_stacks[64 * s:64 * s + 64, :, :] for s in range(2)]
        nm = [sb(f"nm{s}", [P, NT, H]) for s in range(2)]
        nmf = [sb(f"nmf{s}", [H, T]) for s in range(2)]
        nmr = [sb(f"nmr{s}", [H, T]) for s in range(2)]
        nmp = [sb(f"nmp{s}", [H, 3, T], BF16) for s in range(2)]
        vA = sb("vA", [P, NT, H, HD + 1])
        pT = [sb(f"pT{i}", [P, sum(WIDTH)]) for i in range(2)]
        rzo = [sb(f"rzo{s}", [P, HPO, NT]) for s in range(2)]
        o = [sb(f"o{s}", [P, NT, P]) for s in range(2)]
        oT = [sb(f"oT{s}", [P, T]) for s in range(2)]
        gated = sb("gated", [P, 2, FC, T])
        sil = gated[:, 0, :, :]
        hid = gated[:, 1, :, :]
        alibi_i = gated[0:1, :, :, :].rearrange("p a c t -> p (a c t)")[:, 0:AL * T].bitcast(I32).rearrange(
            "p (a t) -> p a t", a=AL)
        ktok = sb("ktok", [P, 2, NT, P])
        sq = sb("sq", [P, NT * P])
        n2 = sb("n2", [P, 2, NT, H])
        nrm = sb("nrm", [P, 2, NT, H])
        nnm = sb("nnm", [H, 2])
        ew = sb("ew", [H, 2, T])
        zw = sb("zw", [H, 2])
        rzw = sb("rzw", [H, 2])
        wt = sb("wt", [P, 2, NT, H])
        kw = sb("kw", [P, 2, NT, P])
        wrep = sb("wrep", [P, NT, P])
        den = sb("den", [P, L])
        rden = sb("rden", [P, L])
        vden = sb("vden", [L, H])
        vrden = sb("vrden", [L, H])
        NE = 8
        E = setup[:, :].rearrange("p (n t) -> p n t", n=NE)
        alibi = sb("alibi", [1, AL + 1, T], BF16)
        junk = sb("junk", [P, T])
        spare = sb("spare", [P, 1])
        nmB = sb("nmB", [P, H, NT])
        Z = sb("Z", [P, H, NT])
        lnZ = sb("lnZ", [P, H, NT])
        thr = sb("thr", [P, H, NT])
        acc = sb("acc", [P, H, NT])
        rz = sb("rz", [P, H, NT])
        t1 = sb("t1", [P, H, NT])
        t2 = sb("t2", [P, H, NT])
        t3 = sb("t3", [P, H, NT])
        own = sb("own", [P, NT])
        infl = sb("infl", [P, NT])
        imp = sb("imp", [P, NT])
        diag = sb("diag", [P, NT, P])
        cnt = sb("cnt", [P, 3, NT])
        rank = sb("rank", [P, NT])
        rank2 = sb("rank2", [P, NT])
        sel = sb("sel", [P, NT, HH])
        kcat = sb("kcat", [P, NK])
        krest = sb("krest", [P, NK])
        kcp = sb("kcp", [P, 3, NK], BF16)
        kcst = sb("kcst", [P, H, NK], BF16)[64:P, :, :]
        vcat = sb("vcat", [P, H, HD + 1])
        p2 = [sb(f"p2_{i}", [P, T]) for i in range(2)]

        part_dram = [nc.dram_tensor(f"part_dram{s}", [P, 2, 3, T], BF16, kind="Internal").ap() for s in range(2)]
        nm_dram = [nc.dram_tensor(f"nm_dram{s}", [H, 3, T], BF16, kind="Internal").ap() for s in range(2)]
        kcp_dram = nc.dram_tensor("kcp_dram", [P, 3, NK], BF16, kind="Internal").ap()

        s_w = sem("weights_loaded")
        s_const = sem("pool_constants_made")
        s_wfp = sem("weights_scaled")
        s_wtr = sem("weights_transposed")
        s_wev = sem("weights_in_sbuf")
        s_cdve = sem("dve_constants_made")
        s_rows = sem("constant_rows_in_stacks")
        s_xin = sem("x_loaded")
        s_out = sem("out_stored")
        s_xr = [None] + [sem(f"x{u}_ready") for u in range(1, 5)]
        s_xbo = sem("x_plus_bias_ready")
        s_st = [sem(f"ln_stats{u}") for u in range(4)]
        s_mv = [sem(f"ln_moments{u}") for u in range(4)]
        s_ve = [sem(f"ln_var_eps{u}") for u in range(4)]
        s_rs = [sem(f"ln_rstd{u}") for u in range(4)]
        s_xn = [sem(f"ln_normed{u}") for u in range(4)]
        s_xt = [sem(f"ln_transposed{u}") for u in range(4)]
        s_xe = [sem(f"ln_evacuated{u}") for u in range(4)]
        s_proj = [sem(f"projected{s}") for s in range(2)]
        s_qf = [sem(f"qk_evacuated{s}") for s in range(2)]
        s_vt = [sem(f"v_evacuated{s}") for s in range(2)]
        s_hi = [sem(f"high_and_mid_parts{s}") for s in range(2)]
        s_rest = [sem(f"rests_and_low_parts{s}") for s in range(2)]
        s_stack = [sem(f"stacks_loaded{s}") for s in range(2)]
        s_s1 = [sem(f"scores_for_max{s}") for s in range(2)]
        s_pd = [sem(f"parts_in_dram{s}") for s in range(2)]
        s_nd = [sem(f"maxima_in_dram{s}") for s in range(2)]
        s_kd = sem("key_parts_in_dram")
        s_m1 = [sem(f"maxima{s}") for s in range(2)]
        s_mt = [sem(f"maxima_transposed{s}") for s in range(2)]
        s_ma = [sem(f"maxima_act_steps{s}") for s in range(2)]
        s_mp = [sem(f"maxima_pool_steps{s}") for s in range(2)]
        s_mrow = [sem(f"maxima_rows_loaded{s}") for s in range(2)]
        s_s2 = [sem(f"scores_minus_max{s}") for s in range(2)]
        s_p = [sem(f"probabilities{s}") for s in range(2)]
        s_pv = [sem(f"heads_weighted{s}") for s in range(2)]
        s_rzo = [sem(f"sums_inverted{s}") for s in range(2)]
        s_o = [sem(f"heads_normalised{s}") for s in range(2)]
        s_ot = [sem(f"o_transposed{s}") for s in range(2)]
        s_oe = [sem(f"oT_evacuated{s}") for s in range(2)]
        s_op = [sem(f"o_projected{s}") for s in range(2)]
        s_g = [sem(f"gate_up_products{s}") for s in range(2)]
        s_sil = [sem(f"silu_done{s}") for s in range(2)]
        s_hid = [sem(f"hidden_done{s}") for s in range(2)]
        s_dn = [sem(f"down_product{s}") for s in range(2)]
        s_sq = sem("squares")
        s_n2 = sem("squared_norms")
        s_nrm = sem("norms")
        s_nt = sem("norms_transposed")
        s_nnm = sem("norm_maxima")
        s_ew = sem("norm_exponentials")
        s_rzw = sem("norm_sums_inverted")
        s_wn = sem("token_weights")
        s_wt = sem("token_weights_transposed")
        s_wte = sem("token_weights_in_sbuf")
        s_kw = sem("weighted_tokens")
        s_cmp = sem("compressed_sums")
        s_den = sem("compressed_denominators")
        s_rden = sem("compressed_denominators_inverted")
        s_cat = sem("compressed_in_place")
        s_bs = sem("full_scores")
        s_bm = sem("full_maxima")
        s_be = sem("full_exponentials")
        s_bz = sem("full_log_sums")
        s_bt = sem("clip_thresholds")
        s_bn = sem("entropy_sums")
        s_brz = sem("full_sums_inverted")
        s_bi = sem("influences")
        s_imp = sem("importance_steps")
        s_dg = sem("importance_diagonals")
        s_rb = sem("importance_rows")
        s_cnt = sem("ranks_counted")
        s_sel = sem("selection_made")
        s_gat = sem("heavy_hitters_gathered")
        s_hhe = sem("heavy_hitters_in_place")
        s_ka = sem("key_parts_act")
        s_kp = sem("key_parts_pool")
        s_kc = sem("key_stack_loaded")

        block = ctx.enter_context(nc.Block())

        PT_AT = {0: 0, 1: T, 3: T + T - P, 2: 2 * T}

        def stack_rows(st_, j, base):
            return st_[base + j * HD:base + (j + 1) * HD, :, :]

        @block.sync
        def _(sp):
            for c in range(3):
                sp.dma_start(wload[:, c, :], w_qkv[c * P:(c + 1) * P, :]).then_inc(s_w, DMA)
            sp.dma_start(wload[:, 3, :], w_out).then_inc(s_w, DMA)
            for i, w in enumerate((wq_b, wk_b, wv_b, wo_b)):
                sp.dma_start(wqb[:, i, :], w).then_inc(s_w, DMA)
            sp.dma_start(wint[:, 0, :].rearrange("p (c d) -> p c d", c=FC),
                         w_gate.rearrange("(c p) d -> p c d", p=P)).then_inc(s_w, DMA)
            sp.dma_start(wint[:, 1, :].rearrange("p (c d) -> p c d", c=FC),
                         w_up.rearrange("(c p) d -> p c d", p=P)).then_inc(s_w, DMA)
            sp.dma_start(wint[:, 2, :], w_down).then_inc(s_w, DMA)
            sp.dma_start(bqk[:, :], b_qkv[0:2 * P].rearrange("(c p) -> p c", p=P),
                         allow_slow_non_contiguous=True).then_inc(s_w, DMA)
            sp.dma_start(bv[:, :], b_qkv[2 * P:3 * P].rearrange("(a n) -> a n", a=1).broadcast_to([P, P])
                         ).then_inc(s_w, DMA)
            sp.dma_start(bo[:, :], b_out.rearrange("(a n) -> a n", a=1).broadcast_to([P, P])).then_inc(s_w, DMA)
            sp.wait_ge(s_cdve, 2)
            ones_row = alibi[:, AL:AL + 1, :].broadcast_to([1, H, T])
            q_rows = (alibi[:, 0:1, :], alibi[:, AL:AL + 1, :], alibi[:, 1:2, :], alibi[:, AL:AL + 1, :])
            k_rows = (alibi[:, AL:AL + 1, :], alibi[:, 2:3, :], alibi[:, AL:AL + 1, :], alibi[:, 3:4, :])
            for r in range(AL):
                sp.dma_start(qst[0][r:r + 1, :, :], q_rows[r].broadcast_to([1, H, T])).then_inc(s_rows, DMA)
                sp.dma_start(kst[0][r:r + 1, :, :], k_rows[r].broadcast_to([1, H, T])).then_inc(s_rows, DMA)
            for r in range(3):
                sp.dma_start(kst[0][A_SC + r:A_SC + r + 1, :, :], ones_row).then_inc(s_rows, DMA)
                sp.dma_start(kcst[B_SC + r:B_SC + r + 1, :, :],
                             alibi[:, AL:AL + 1, 0:NK].broadcast_to([1, H, NK])).then_inc(s_rows, DMA)

            def stacks(s, b, base):
                sp.wait_ge(s_rest[s], b * 4 + 4)
                sp.wait_ge(s_hi[s], b * 4 + 4)
                if s == 0:
                    sp.wait_ge(s_s2[0], b * 3 * H)
                else:
                    sp.wait_ge(s_s2[1], b * H)
                sp.dma_start(part_dram[s], part[s][:, :, :, :]).then_inc(s_pd[s], DMA)
                sp.wait_ge(s_pd[s], b * DMA + DMA)
                for i, (stk, parts) in enumerate(((qst[s], Q_PART), (kst[s], K_PART))):
                    for j, pt in enumerate(parts):
                        sp.dma_start(stack_rows(stk, j, base),
                                     part_dram[s][:, i, pt, :].rearrange("(h d) t -> d h t", d=HD)
                                     ).then_inc(s_stack[s], DMA)

            def max_rows(s, b, base):
                sp.wait_ge(s_mp[s], b * 2 + 2)
                sp.dma_start(nm_dram[s], nmp[s][:, :, :]).then_inc(s_nd[s], DMA)
                sp.wait_ge(s_nd[s], b * DMA + DMA)
                sp.dma_start(qst[s][base:base + 3, :, :], nm_dram[s].rearrange("h r t -> r h t")
                             ).then_inc(s_mrow[s], DMA)

            with sp.Fori(1, B + 1) as b_after:
                b = b_after - 1
                sp.wait_ge(s_xr[1], b)
                sp.dma_start(xs[0][:, :, :],
                             x[bass.ds(b, 1), :, :].rearrange("a (t p) d -> p (a t) d", p=P)).then_inc(s_xin, DMA)
                stacks(0, b, AL)
                max_rows(0, b, A_SC)
                stacks(1, b, 0)
                sp.wait_ge(s_kp, b * 2 + 2)
                sp.wait_ge(s_ka, b * 2 + 2)
                sp.wait_ge(s_s2[1], b * H)
                sp.dma_start(kcp_dram, kcp[:, :, :]).then_inc(s_kd, DMA)
                sp.wait_ge(s_kd, b * DMA + DMA)
                for j, pt in enumerate(K_PART):
                    sp.dma_start(stack_rows(kcst, j, 0),
                                 kcp_dram[:, pt, :].rearrange("(h d) t -> d h t", d=HD)).then_inc(s_kc, DMA)
                max_rows(1, b, B_SC)
                sp.wait_ge(s_xr[4], b + 1)
                sp.dma_start(out[bass.ds(b, 1), :, :].rearrange("a (t p) d -> p (a t) d", p=P),
                             xs[4][:, :, :]).then_inc(s_out, DMA)
            sp.wait_ge(s_out, B * DMA)

        @block.gpsimd
        def _(pool):
            pool.memset(identf[:, :], 0.0)
            pool.memset(identb[:, :], 0.0)
            pool.memset(onesf[:, :], 1.0)
            pool.memset(maskqk[:, :], 0.0)
            pool.memset(maskkq[:, :], 0.0)
            pool.memset(tri[:, :], 1.0)
            pool.memset(half[:, :], 0.5)
            pool.memset(neghalf[:, :], -0.5)
            pool.memset(eps[:, :], EPS)
            pool.memset(vA[:, :, :, :], 1.0)
            pool.memset(vcat[:, :, :], 1.0)
            pool.memset(alibi[:, AL:AL + 1, :], 1.0)
            pool.memset(group[:, :, :], 1.0).then_inc(s_const, 1)
            pool.wait_ge(s_const, 1)
            pool.affine_select(out=identf[:, :], in_=identf[:, :], compare_op=ALU.not_equal, fill=1.0, base=0,
                               pattern=[[-1, P]], channel_multiplier=1)
            pool.affine_select(out=identb[:, :], in_=identb[:, :], compare_op=ALU.not_equal, fill=1.0, base=0,
                               pattern=[[-1, P]], channel_multiplier=1)
            pool.affine_select(out=maskqk[:, :], in_=maskqk[:, :], compare_op=ALU.is_ge, fill=NEG, base=0,
                               pattern=[[-1, P]], channel_multiplier=1)
            pool.affine_select(out=maskkq[:, :], in_=maskkq[:, :], compare_op=ALU.is_ge, fill=NEG, base=0,
                               pattern=[[1, P]], channel_multiplier=-1)
            pool.affine_select(out=tri[:, :], in_=tri[:, :], compare_op=ALU.is_gt, fill=0.0, base=0,
                               pattern=[[-1, P]], channel_multiplier=1)
            pool.affine_select(out=group[:, :, :], in_=group[:, :, :], compare_op=ALU.is_ge, fill=0.0, base=0,
                               pattern=[[P, NT], [-RATIO, L]], channel_multiplier=1).then_inc(s_const, 1)
            pool.wait_ge(s_const, 2)
            pool.affine_select(out=group[:, :, :], in_=group[:, :, :], compare_op=ALU.is_ge, fill=0.0,
                               base=RATIO - 1, pattern=[[-P, NT], [RATIO, L]], channel_multiplier=-1)
            pool.iota(iota_i[:, :], pattern=[[1, HH]], base=0, channel_multiplier=0)
            pool.iota(alibi_i[:, 0, :], pattern=[[-256, T // 256], [0, 256]], base=0, channel_multiplier=0)
            pool.iota(alibi_i[:, 1, :], pattern=[[0, T // 256], [-1, 256]], base=0, channel_multiplier=0)
            pool.iota(alibi_i[:, 2, :], pattern=[[256, T // 256], [0, 256]], base=0, channel_multiplier=0)
            pool.iota(alibi_i[:, 3, :], pattern=[[0, T // 256], [1, 256]], base=0, channel_multiplier=0
                      ).then_inc(s_const, 1)

            def ln(u, b):
                pool.wait_ge(s_mv[u], b + 1)
                pool.wait_ge(s_xn[u], b)
                pool.tensor_tensor(ve[u][:, :], mv[u][:, :, 1], eps[:, :], ALU.add).then_inc(s_ve[u], 1)
                pool.wait_ge(s_ve[u], b + 1)
                pool.tensor_tensor(rstd[u][:, :], ve[u][:, :], neghalf[:, :], ALU.pow).then_inc(s_rs[u], 1)

            def split(s, b):
                for i in range(2):
                    pool.wait_ge(s_hi[s], b * 4 + 2 * i + 1)
                    pool.tensor_tensor(rest[s][:, i, :], qf[s][:, i, :], part[s][:, i, 0, :], ALU.subtract
                                       ).then_inc(s_rest[s], 1)
                    pool.wait_ge(s_hi[s], b * 4 + 2 * i + 2)
                    pool.wait_ge(s_stack[s], b * 2 * NPAIR * DMA)
                    pool.tensor_tensor(part[s][:, i, 2, :], rest[s][:, i, :], part[s][:, i, 1, :], ALU.subtract
                                       ).then_inc(s_rest[s], 1)

            def split_max(s, b):
                pool.wait_ge(s_ma[s], b * 3 + 2)
                pool.tensor_tensor(nmr[s][:, :], nmf[s][:, :], nmp[s][:, 0, :], ALU.subtract).then_inc(s_mp[s], 1)
                pool.wait_ge(s_ma[s], b * 3 + 3)
                pool.wait_ge(s_mrow[s], b * DMA)
                pool.tensor_tensor(nmp[s][:, 2, :], nmr[s][:, :], nmp[s][:, 1, :], ALU.subtract
                                   ).then_inc(s_mp[s], 1)

            with pool.Fori(0, B) as b:
                pool.wait_ge(s_xin, b * DMA + DMA)
                pool.wait_ge(s_w, 14 * DMA)
                pool.wait_ge(s_xr[1], b)
                for t in range(NT):
                    last = pool.tensor_tensor(xbo[:, t, :], xs[0][:, t, :], bo[:, :], ALU.add)
                last.then_inc(s_xbo, 1)
                ln(0, b)
                split(0, b)
                split_max(0, b)
                ln(1, b)
                ln(2, b)
                split(1, b)
                for i in range(2):
                    pool.wait_ge(s_vt[1], b * 2 + i + 1)
                    pool.wait_ge(s_n2, b * 2 + i)
                    pool.tensor_tensor(sq[:, :], ktok[:, i, :, :].rearrange("p t d -> p (t d)"),
                                       ktok[:, i, :, :].rearrange("p t d -> p (t d)"), ALU.mult).then_inc(s_sq, 1)
                    pool.wait_ge(s_n2, b * 2 + i + 1)
                    pool.tensor_tensor(nrm[:, i, :, :].rearrange("p t h -> p (t h)"),
                                       n2[:, i, :, :].rearrange("p t h -> p (t h)"), half[:, :], ALU.pow
                                       ).then_inc(s_nrm, 1)
                for n in range(NT * H):
                    h, t = n // NT, n % NT
                    pool.wait_ge(s_bz, b * NT * H + n + 1)
                    if n == 0:
                        pool.wait_ge(s_imp, b * 6)
                    pool.tensor_tensor(thr[:, h, t:t + 1], lnZ[:, h, t:t + 1], nmB[:, h, t:t + 1], ALU.subtract
                                       ).then_inc(s_bt, 1)
                pool.wait_ge(s_ka, b * 2 + 1)
                pool.tensor_tensor(krest[:, :], kcat[:, :], kcp[:, 0, :], ALU.subtract).then_inc(s_kp, 1)
                pool.wait_ge(s_ka, b * 2 + 2)
                pool.tensor_tensor(kcp[:, 2, :], krest[:, :], kcp[:, 1, :], ALU.subtract).then_inc(s_kp, 1)
                split_max(1, b)
                ln(3, b)

        @block.scalar
        def _(act):
            act.preload_act_table_set("natural_log_exp_and_others")
            for n, dst in enumerate((wqkvT[:, 0:P], wqkvT[:, P:2 * P], wqkvT[:, 2 * P:3 * P], woutT[:, :])):
                act.wait_ge(s_wtr, n + 1)
                act.activation(dst, bank[n][:, 0:P], ACT.Copy).then_inc(s_wev, 1)
            for i, w in enumerate((wgT, wuT, wdT)):
                for c in range(FC):
                    n = 4 + i * FC + c
                    act.wait_ge(s_wtr, n + 1)
                    act.activation(w[:, c, :], bank[n % 8][:, 0:P], ACT.Copy).then_inc(s_wev, 1)

            def ln(u, b, misc):
                act.wait_ge(s_xt[u], b + 1)
                act.activation(xnT[u // 2][:, :], bank[misc][:, :], ACT.Copy).then_inc(s_xe[u], 1)

            def qk(s, b, misc):
                for i in range(2):
                    act.wait_ge(s_proj[s], b * (3 + s) + i + 1)
                    if s == 0:
                        if i == 0:
                            act.wait_ge(s_cdve, 3)
                        act.activation(qf[s][:, i, :], bank[misc][:, :], ACT.Identity,
                                       bias=bqs[:, 0:1] if i == 0 else bqk[:, 1:2],
                                       scale=QSCALE if i == 0 else 1.0).then_inc(s_qf[s], 1)
                    else:
                        act.activation(qf[s][:, i, :], bank[misc][:, :], ACT.Copy,
                                       scale=QSCALE if i == 0 else 1.0).then_inc(s_qf[s], 1)
                act.wait_ge(s_stack[s], b * 2 * NPAIR * DMA)
                for i in range(2):
                    act.wait_ge(s_qf[s], b * 2 + i + 1)
                    act.activation(part[s][:, i, 0, :], qf[s][:, i, :], ACT.Copy).then_inc(s_hi[s], 1)
                    act.wait_ge(s_rest[s], b * 4 + 2 * i + 1)
                    act.activation(part[s][:, i, 1, :], rest[s][:, i, :], ACT.Copy).then_inc(s_hi[s], 1)

            def split_max(s, b, misc):
                act.wait_ge(s_mt[s], b + 1)
                act.activation(nmf[s][:, :], bank[misc][0:H, :], ACT.Copy).then_inc(s_ma[s], 1)
                act.wait_ge(s_ma[s], b * 3 + 1)
                act.wait_ge(s_mrow[s], b * DMA)
                act.activation(nmp[s][:, 0, :], nmf[s][:, :], ACT.Copy).then_inc(s_ma[s], 1)
                act.wait_ge(s_mp[s], b * 2 + 1)
                act.activation(nmp[s][:, 1, :], nmr[s][:, :], ACT.Copy).then_inc(s_ma[s], 1)

            def out_t(s, b, misc):
                act.wait_ge(s_ot[s], b + 1)
                act.activation(oT[s][:, :], bank[misc][:, :], ACT.Copy).then_inc(s_oe[s], 1)

            def ffn(s, b, misc):
                act.wait_ge(s_hid[1 - s], b * FC + (FC if s else 0))
                for c in range(FC):
                    act.wait_ge(s_g[s], b * 2 * FC + 2 * c + 1)
                    act.activation(sil[:, c, :], bank[misc][:, :], ACT.Silu).then_inc(s_sil[s], 1)
                act.preload_act_table_set("natural_log_exp_and_others")

            with act.Fori(0, B) as b:
                ln(0, b, 7)
                qk(0, b, 7)
                split_max(0, b, 7)
                for h in range(H):
                    if h < 2:
                        act.wait_ge(s_pv[0], b * H)
                    else:
                        act.wait_ge(s_pv[0], b * H + h - 1)
                    for i in range(3):
                        n = 3 * h + i
                        act.wait_ge(s_s2[0], b * 3 * H + n + 1)
                        act.activation(pT[h % 2][:, i * T:i * T + WIDTH[i]], bank[3 + n % 2][:, 0:WIDTH[i]],
                                       ACT.Exp).then_inc(s_p[0], 1)
                out_t(0, b, 7)
                ln(1, b, 7)
                ffn(0, b, 7)
                ln(2, b, 6)
                qk(1, b, 6)
                for i in range(2):
                    act.wait_ge(s_proj[1], b * 4 + 3 + i)
                    act.activation(ktok[:, i, :, :].rearrange("p t d -> p (t d)"), bank[6][:, :], ACT.Copy
                                   ).then_inc(s_vt[1], 1)
                for i in range(2):
                    act.wait_ge(s_nnm, b * 2 + i + 1)
                    act.activation(ew[:, i, :], bank[6][0:H, :], ACT.Exp, bias=nnm[:, i:i + 1],
                                   accum_out=zw[:, i:i + 1]).then_inc(s_ew, 1)
                for i in range(2):
                    act.wait_ge(s_rzw, b * 2 + i + 1)
                    act.wait_ge(s_ew, b * 2 + i + 1)
                    act.activation(ew[:, i, :], ew[:, i, :], ACT.Copy, scale=rzw[:, i:i + 1]).then_inc(s_wn, 1)
                for i in range(2):
                    act.wait_ge(s_wt, b * 2 + i + 1)
                    act.activation(wt[:, i, :, :].rearrange("p t h -> p (t h)"), bank[6][:, 0:NT * H], ACT.Copy
                                   ).then_inc(s_wte, 1)
                for n in range(NT * H):
                    h, t = n // NT, n % NT
                    act.wait_ge(s_bm, b * NT * H + n + 1)
                    if h >= 2:
                        act.wait_ge(s_bn, b * NT * H + n - NE + 1)
                        act.wait_ge(s_bi, b * H + h - 1)
                    if n == 0:
                        act.wait_ge(s_cnt, b * 3)
                    act.activation(E[:, n % NE, :], bank[n % 3][:, :], ACT.Exp, bias=nmB[:, h, t:t + 1],
                                   accum_out=Z[:, h, t:t + 1]).then_inc(s_be, 1)
                    act.wait_ge(s_be, b * NT * H + n + 1)
                    act.activation(lnZ[:, h, t:t + 1], Z[:, h, t:t + 1], ACT.Ln, scale=CLIP).then_inc(s_bz, 1)
                act.wait_ge(s_hhe, b * 2 + 1)
                act.wait_ge(s_cat, b * 2 + 1)
                act.wait_ge(s_kc, b * NPAIR * DMA)
                act.activation(kcp[:, 0, :], kcat[:, :], ACT.Copy).then_inc(s_ka, 1)
                act.wait_ge(s_kp, b * 2 + 1)
                act.activation(kcp[:, 1, :], krest[:, :], ACT.Copy).then_inc(s_ka, 1)
                split_max(1, b, 6)
                for h in range(H):
                    if h < 2:
                        act.wait_ge(s_pv[1], b * H)
                    else:
                        act.wait_ge(s_pv[1], b * H + h - 1)
                    act.wait_ge(s_s2[1], b * H + h + 1)
                    act.activation(p2[h % 2][0:NK, :], bank[h % 2][0:NK, :], ACT.Exp).then_inc(s_p[1], 1)
                out_t(1, b, 6)
                ln(3, b, 6)
                ffn(1, b, 6)

        @block.vector
        def _(dve):
            dve.wait_ge(s_const, 3)
            dve.tensor_copy(iota_f[:, :], iota_i[:, :]).then_inc(s_cdve, 1)
            dve.tensor_copy(alibi[:, 0:AL, :], alibi_i[:, :, :]).then_inc(s_cdve, 1)
            dve.wait_ge(s_w, 14 * DMA)
            dve.tensor_scalar(bqs[:, :], bqk[:, 0:1], QSCALE, None, ALU.mult).then_inc(s_cdve, 1)
            dve.tensor_scalar(wfp[:, :, :], wint[:, :, :], 1.0 / 127.0, None, ALU.mult).then_inc(s_wfp, 1)

            def ln(u, b):
                for t in range(NT):
                    last = dve.bn_stats(st[u][:, t, :], xs[u][:, t, :])
                last.then_inc(s_st[u], 1)
                dve.wait_ge(s_st[u], b + 1)
                dve.memset(spare[:, :], 0.0)
                for t in range(NT):
                    last = dve.bn_aggr(mv[u][:, t, :], st[u][:, t, :])
                last.then_inc(s_mv[u], 1)
                dve.wait_ge(s_rs[u], b + 1)
                dve.wait_ge(s_xt[u ^ 1], b + u % 2)
                for t in range(NT):
                    last = dve.tensor_scalar(xn[u // 2][:, t, :], xs[u][:, t, :], mv[u][:, t, 0:1], rstd[u][:, t:t + 1],
                                             ALU.subtract, ALU.mult)
                last.then_inc(s_xn[u], 1)

            def norm_heads(s, b, half_, po):
                dve.wait_ge(s_pv[s], b * H + (half_ + 1) * HPO)
                ps = bank[po][:, 0:HPO * NT * (HD + 1)].rearrange("p (h t e) -> p h t e", h=HPO, t=NT)
                dve.reciprocal(rzo[s][:, :, :], ps[:, :, :, HD]).then_inc(s_rzo[s], 1)
                dve.wait_ge(s_rzo[s], b * 2 + half_ + 1)
                dve.wait_ge(s_ot[s], b)
                for t in range(NT):
                    last = dve.tensor_tensor(
                        o[s][:, t, half_ * HPO * HD:(half_ + 1) * HPO * HD].rearrange("p (h d) -> p h d", d=HD),
                        ps[:, :, t, 0:HD], rzo[s][:, :, t:t + 1].broadcast_to([P, HPO, HD]), ALU.mult)
                last.then_inc(s_o[s], 1)

            def ffn(s, b, misc, up):
                for c in range(FC):
                    dve.wait_ge(s_g[s], b * 2 * FC + 2 * c + 2)
                    dve.wait_ge(s_sil[s], b * FC + c + 1)
                    if c == 0:
                        dve.wait_ge(s_dn[1 - s], b + (1 if s else 0))
                    dve.tensor_tensor(hid[:, c, :], bank[up][:, :], sil[:, c, :], ALU.mult).then_inc(s_hid[s], 1)
                u = 2 * s + 1
                dve.wait_ge(s_dn[s], b + 1)
                if s:
                    dve.wait_ge(s_out, b * DMA)
                dve.tensor_tensor(xs[u + 1][:, :, :].rearrange("p t d -> p (t d)"), bank[misc][:, :],
                                  xs[u][:, :, :].rearrange("p t d -> p (t d)"), ALU.add).then_inc(s_xr[u + 1], 1)

            with dve.Fori(0, B) as b:
                dve.wait_ge(s_xin, b * DMA + DMA)
                ln(0, b)
                dve.wait_ge(s_proj[0], b * 3 + 3)
                dve.wait_ge(s_pv[0], b * H)
                for t in range(NT):
                    last = dve.tensor_tensor(vA[:, t, :, 0:HD],
                                             bank[7][:, t * P:(t + 1) * P].rearrange("p (h d) -> p h d", d=HD),
                                             bv[:, :].rearrange("p (h d) -> p h d", d=HD), ALU.add)
                last.then_inc(s_vt[0], 1)
                dve.wait_ge(s_mt[0], b)
                for h in range(H):
                    for i, parts in enumerate((((3, 0),), ((0, 0), (2, P)), ((1, 0),))):
                        n = 3 * h + i
                        dve.wait_ge(s_s1[0], b * 3 * H + n + 1)
                        for t, c in parts:
                            last = dve.tensor_reduce(nm[0][:, t, h:h + 1], bank[3 + n % 2][:, c:c + (t + 1) * P],
                                                     AX_X, ALU.max, negate=True)
                        last.then_inc(s_m1[0], 1)
                norm_heads(0, b, 0, 5)
                norm_heads(0, b, 1, 5)
                dve.wait_ge(s_op[0], b + 1)
                dve.wait_ge(s_xbo, b + 1)
                dve.tensor_tensor(xs[1][:, :, :].rearrange("p t d -> p (t d)"), bank[7][:, :],
                                  xbo[:, :, :].rearrange("p t d -> p (t d)"), ALU.add).then_inc(s_xr[1], 1)
                dve.wait_ge(s_xr[1], b + 1)
                ln(1, b)
                ffn(0, b, 7, 5)
                dve.wait_ge(s_xr[2], b + 1)
                ln(2, b)
                for i in range(2):
                    dve.wait_ge(s_sq, b * 2 + i + 1)
                    dve.wait_ge(s_nrm, b * 2)
                    dve.tensor_reduce(n2[:, i, :, :].rearrange("p t h -> p (t h)"),
                                      sq[:, :].rearrange("p (g d) -> p g d", d=HD), AX_X, ALU.add).then_inc(s_n2, 1)
                for i in range(2):
                    dve.wait_ge(s_nt, b * 2 + i + 1)
                    dve.tensor_reduce(nnm[:, i:i + 1], bank[6][0:H, :], AX_X, ALU.max, negate=True
                                      ).then_inc(s_nnm, 1)
                    dve.wait_ge(s_ew, b * 2 + i + 1)
                    dve.reciprocal(rzw[:, i:i + 1], zw[:, i:i + 1]).then_inc(s_rzw, 1)
                for i in range(2):
                    dve.wait_ge(s_wte, b * 2 + i + 1)
                    dve.wait_ge(s_cmp, b * 2 + i)
                    for t in range(NT):
                        last = dve.tensor_tensor(
                            kw[:, i, t, :].rearrange("p (h d) -> p h d", d=HD),
                            ktok[:, i, t, :].rearrange("p (h d) -> p h d", d=HD),
                            wt[:, i, t, :].rearrange("p (h a) -> p h a", a=1).broadcast_to([P, H, HD]), ALU.mult)
                        if i == 0:
                            last = dve.tensor_copy(
                                wrep[:, t, :].rearrange("p (h d) -> p h d", d=HD),
                                wt[:, 0, t, :].rearrange("p (h a) -> p h a", a=1).broadcast_to([P, H, HD]))
                    last.then_inc(s_kw, 1)
                dve.wait_ge(s_cmp, b * 2 + 1)
                dve.tensor_scalar(den[:, :], bank[6][:, L:2 * L], 1e-8, None, ALU.add).then_inc(s_den, 1)
                dve.wait_ge(s_den, b * 2 + 1)
                dve.reciprocal(rden[:, :], den[:, :]).then_inc(s_rden, 1)
                dve.wait_ge(s_rden, b * 2 + 1)
                dve.wait_ge(s_kp, b * 2)
                dve.tensor_tensor(kcat[:, 0:L], bank[6][:, 0:L], rden[:, :], ALU.mult).then_inc(s_cat, 1)
                dve.wait_ge(s_cmp, b * 2 + 2)
                dve.tensor_scalar(vden[:, :], bank[6][0:L, P:P + H], 1e-8, None, ALU.add).then_inc(s_den, 1)
                dve.wait_ge(s_den, b * 2 + 2)
                dve.reciprocal(vrden[:, :], vden[:, :]).then_inc(s_rden, 1)
                dve.wait_ge(s_rden, b * 2 + 2)
                dve.wait_ge(s_pv[1], b * H)
                dve.tensor_tensor(vcat[0:L, :, 0:HD], bank[6][0:L, 0:P].rearrange("p (h d) -> p h d", d=HD),
                                  vrden[:, :].rearrange("p (h a) -> p h a", a=1).broadcast_to([L, H, HD]),
                                  ALU.mult).then_inc(s_cat, 1)

                def entropy(n):
                    h, t = n // NT, n % NT
                    dve.wait_ge(s_bn, b * NT * H + n)
                    dve.wait_ge(s_bt, b * NT * H + n + 1)
                    dve.scalar_tensor_tensor(out=junk[:, :], in0=bank[n % 3][:, :], scalar=thr[:, h, t:t + 1],
                                             in1=E[:, n % NE, :], op0=ALU.max, op1=ALU.mult,
                                             accum_out=acc[:, h, t:t + 1]).then_inc(s_bn, 1)
                    if t == NT - 1:
                        dve.reciprocal(rz[:, h, :], Z[:, h, :]).then_inc(s_brz, 1)

                for n in range(NT * H):
                    h, t = n // NT, n % NT
                    dve.wait_ge(s_bs, b * NT * H + n + 1)
                    dve.tensor_reduce(nmB[:, h, t:t + 1], bank[n % 3][:, :], AX_X, ALU.max, negate=True
                                      ).then_inc(s_bm, 1)
                    if n >= 2:
                        entropy(n - 2)
                entropy(NT * H - 2)
                entropy(NT * H - 1)

                dve.wait_ge(s_bn, b * NT * H + NT * H)
                dve.wait_ge(s_brz, b * H + H)
                dve.tensor_tensor(t1[:, :, :], acc[:, :, :], rz[:, :, :], ALU.mult).then_inc(s_imp, 1)
                dve.wait_ge(s_imp, b * 6 + 1)
                dve.scalar_tensor_tensor(out=t2[:, :, :], in0=t1[:, :, :], scalar=LOG_CLIP, in1=thr[:, :, :],
                                         op0=ALU.add, op1=ALU.subtract).then_inc(s_imp, 1)
                dve.wait_ge(s_imp, b * 6 + 2)
                dve.scalar_tensor_tensor(out=t3[:, :, :], in0=t2[:, :, :], scalar=0.4 / 0.3, in1=rz[:, :, :],
                                         op0=ALU.mult, op1=ALU.add).then_inc(s_imp, 1)
                dve.wait_ge(s_imp, b * 6 + 3)
                dve.tensor_reduce(own[:, :], t3[:, :, :].rearrange("p h t -> p t h"), AX_X, ALU.add
                                  ).then_inc(s_imp, 1)
                dve.wait_ge(s_bi, b * H + H)
                dve.tensor_reduce(infl[:, :], bank[6][:, 0:NT * H].rearrange("p (h t) -> p t h", t=NT), AX_X,
                                  ALU.add).then_inc(s_imp, 1)
                dve.wait_ge(s_imp, b * 6 + 5)
                dve.tensor_tensor(imp[:, :], own[:, :], infl[:, :], ALU.add).then_inc(s_imp, 1)
                dve.wait_ge(s_imp, b * 6 + 6)
                for t in range(NT):
                    last = dve.tensor_scalar(diag[:, t, :], identf[:, :], imp[:, t:t + 1], None, ALU.mult)
                last.then_inc(s_dg, 1)
                dve.wait_ge(s_rb, b + 1)
                for t in range(NT):
                    dve.tensor_scalar(E[:, t, 0:T - t * P], bank[6][:, t * P:T], imp[:, t:t + 1], None,
                                      ALU.is_gt, ALU.add, accum_out=cnt[:, 0, t:t + 1])
                    dve.scalar_tensor_tensor(out=E[:, 4, t * P:(t + 1) * P], in0=bank[6][:, t * P:(t + 1) * P],
                                             scalar=imp[:, t:t + 1], in1=tri[:, :], op0=ALU.is_equal, op1=ALU.mult,
                                             accum_out=cnt[:, 1, t:t + 1])
                    if t:
                        last = dve.tensor_scalar(E[:, 4 + t, 0:t * P], bank[6][:, 0:t * P], imp[:, t:t + 1], None,
                                                 ALU.is_ge, ALU.add, accum_out=cnt[:, 2, t:t + 1])
                    else:
                        dve.memset(cnt[:, 2, 0:1], 0.0)
                last.then_inc(s_cnt, 1)
                dve.wait_ge(s_cnt, b * 3 + 1)
                dve.tensor_tensor(rank2[:, :], cnt[:, 0, :], cnt[:, 1, :], ALU.add).then_inc(s_cnt, 1)
                dve.wait_ge(s_cnt, b * 3 + 2)
                dve.tensor_tensor(rank[:, :], rank2[:, :], cnt[:, 2, :], ALU.add).then_inc(s_cnt, 1)
                dve.wait_ge(s_cnt, b * 3 + 3)
                for t in range(NT):
                    last = dve.tensor_scalar(sel[:, t, :], iota_f[:, :], rank[:, t:t + 1], None, ALU.is_equal)
                last.then_inc(s_sel, 1)
                dve.wait_ge(s_gat, b + 1)
                dve.tensor_copy(kcat[:, L:NK], bank[6][:, 0:HH]).then_inc(s_hhe, 1)
                dve.tensor_copy(vcat[L:NK, :, 0:HD], bank[6][L:NK, P:2 * P].rearrange("p (h d) -> p h d", d=HD)
                                ).then_inc(s_hhe, 1)
                dve.wait_ge(s_mt[1], b)
                for h in range(H):
                    dve.wait_ge(s_s1[1], b * H + h + 1)
                    dve.tensor_reduce(nm[1][:, :, h],
                                      bank[h % 2][:, 0:NT * NK].rearrange("p (t k) -> p t k", t=NT), AX_X, ALU.max,
                                      negate=True).then_inc(s_m1[1], 1)
                norm_heads(1, b, 0, 2)
                norm_heads(1, b, 1, 2)
                dve.wait_ge(s_op[1], b + 1)
                dve.tensor_tensor(xs[3][:, :, :].rearrange("p t d -> p (t d)"), bank[6][:, :],
                                  xs[2][:, :, :].rearrange("p t d -> p (t d)"), ALU.add).then_inc(s_xr[3], 1)
                dve.wait_ge(s_xr[3], b + 1)
                ln(3, b)
                ffn(1, b, 6, 2)

        @block.tensor
        def _(pe):
            pe.wait_ge(s_const, 3)
            pe.wait_ge(s_w, 14 * DMA)
            for n in range(4):
                pe.transpose(bank[n][:, 0:P], wload[:, n, :], identf[:, :]).then_inc(s_wtr, 1)
            pe.wait_ge(s_wfp, 1)
            for i in range(3):
                for c in range(FC):
                    n = 4 + i * FC + c
                    if n >= 8:
                        pe.wait_ge(s_wev, n - 7)
                    pe.transpose(bank[n % 8][:, 0:P], wfp[:, i, c * P:(c + 1) * P], identf[:, :]).then_inc(s_wtr, 1)
            pe.wait_ge(s_wev, 4 + 3 * FC)
            pe.wait_ge(s_rows, (2 * AL + 6) * DMA)

            def ln(u, b, misc):
                pe.wait_ge(s_xn[u], b + 1)
                for t in range(NT):
                    last = pe.transpose(bank[misc][:, t * P:(t + 1) * P], xn[u // 2][:, t, :], identf[:, :])
                last.then_inc(s_xt[u], 1)
                pe.wait_ge(s_xe[u], b + 1)

            def tokens_by(w, u, misc):
                for t in range(NT):
                    last = pe.matmul(bank[misc][:, t * P:(t + 1) * P], xnT[u // 2][:, t * P:(t + 1) * P], w,
                                     start=True, stop=True)
                return last

            def transpose_max(s, b, misc):
                for t in range(NT):
                    last = pe.transpose(bank[misc][0:H, t * P:(t + 1) * P], nm[s][:, t, :], identf[:, :])
                last.then_inc(s_mt[s], 1)

            def project(s, b, misc, w):
                pe.wait_ge(s_o[s], b * 2 + 2)
                for t in range(NT):
                    last = pe.transpose(bank[misc][:, t * P:(t + 1) * P], o[s][:, t, :], identf[:, :])
                last.then_inc(s_ot[s], 1)
                pe.wait_ge(s_oe[s], b + 1)
                for t in range(NT):
                    last = pe.matmul(bank[misc][:, t * P:(t + 1) * P], oT[s][:, t * P:(t + 1) * P], w,
                                     start=True, stop=True)
                last.then_inc(s_op[s], 1)

            def ffn(s, b, misc, up):
                u = 2 * s + 1
                for c in range(FC):
                    if c:
                        pe.wait_ge(s_sil[s], b * FC + c)
                    pe.matmul(bank[misc][:, :], wgT[:, c, :], xnT[u // 2][:, :], start=True, stop=True
                              ).then_inc(s_g[s], 1)
                    if c:
                        pe.wait_ge(s_hid[s], b * FC + c)
                    pe.matmul(bank[up][:, :], wuT[:, c, :], xnT[u // 2][:, :], start=True, stop=True
                              ).then_inc(s_g[s], 1)
                pe.wait_ge(s_hid[s], b * FC + FC)
                for t in range(NT):
                    for c in range(FC):
                        last = pe.matmul(bank[misc][:, t * P:(t + 1) * P], hid[:, c, t * P:(t + 1) * P],
                                         wdT[:, c, :], start=(c == 0), stop=(c == FC - 1))
                last.then_inc(s_dn[s], 1)

            with pe.Fori(0, B) as b:
                pe.wait_ge(s_xr[2], b)
                ln(0, b, 7)
                pe.matmul(bank[7][:, :], wqkvT[:, 0:P], xnT[0][:, :], start=True, stop=True).then_inc(s_proj[0], 1)
                pe.wait_ge(s_qf[0], b * 2 + 1)
                pe.matmul(bank[7][:, :], wqkvT[:, P:2 * P], xnT[0][:, :], start=True, stop=True
                          ).then_inc(s_proj[0], 1)
                pe.wait_ge(s_qf[0], b * 2 + 2)
                tokens_by(wqkvT[:, 2 * P:3 * P], 0, 7).then_inc(s_proj[0], 1)
                pe.wait_ge(s_stack[0], b * 2 * NPAIR * DMA + 2 * NPAIR * DMA)
                for h in range(H):
                    for i, parts in enumerate((((3, 0),), ((0, 0), (2, P)), ((1, 0),))):
                        n = 3 * h + i
                        if n >= 2:
                            pe.wait_ge(s_m1[0], b * 3 * H + n - 1)
                        for t, c in parts:
                            q = qst[0][0:A_SC, h, t * P:(t + 1) * P]
                            pe.matmul(bank[3 + n % 2][:, c:c + (t + 1) * P], q, kst[0][0:A_SC, h, 0:(t + 1) * P],
                                      start=True, stop=True)
                            last = pe.matmul(bank[3 + n % 2][:, c + t * P:c + (t + 1) * P], identb[:, :],
                                             maskqk[:, :], start=False, stop=True, skip_group_check=True)
                        last.then_inc(s_s1[0], 1)
                pe.wait_ge(s_m1[0], b * 3 * H + 3 * H)
                pe.wait_ge(s_vt[0], b + 1)
                transpose_max(0, b, 7)
                pe.wait_ge(s_mrow[0], b * DMA + DMA)

                def weigh(h):
                    pe.wait_ge(s_p[0], b * 3 * H + 3 * h + 3)
                    if h == 0:
                        pe.wait_ge(s_hid[0], b * FC)
                    if h == HPO:
                        pe.wait_ge(s_o[0], b * 2 + 1)
                    for t in range(NT):
                        c = ((h % HPO) * NT + t) * (HD + 1)
                        for k in range(t + 1):
                            at = PT_AT[k] + (t - k) * P
                            last = pe.matmul(bank[5][:, c:c + HD + 1], pT[h % 2][:, at:at + P], vA[:, k, h, :],
                                             start=(k == 0), stop=(k == t))
                    last.then_inc(s_pv[0], 1)

                for h in range(H):
                    for i, parts in enumerate(TILES):
                        n = 3 * h + i
                        if n >= 2:
                            pe.wait_ge(s_p[0], b * 3 * H + n - 1)
                        for k, c in parts:
                            w = T - k * P
                            pe.matmul(bank[3 + n % 2][:, c:c + w], kst[0][0:A_MX, h, k * P:(k + 1) * P],
                                      qst[0][0:A_MX, h, k * P:T], start=True, stop=True)
                            last = pe.matmul(bank[3 + n % 2][:, c:c + P], identb[:, :], maskkq[:, :],
                                             start=False, stop=True, skip_group_check=True)
                        last.then_inc(s_s2[0], 1)
                    if h:
                        weigh(h - 1)
                weigh(H - 1)
                pe.wait_ge(s_ma[0], b * 3 + 1)
                project(0, b, 7, woutT[:, :])
                pe.wait_ge(s_xr[1], b + 1)
                ln(1, b, 7)
                ffn(0, b, 7, 5)
                pe.wait_ge(s_xr[4], b)
                ln(2, b, 6)
                pe.matmul(bank[6][:, :], wqb[:, 0, :], xnT[1][:, :], start=True, stop=True).then_inc(s_proj[1], 1)
                pe.wait_ge(s_qf[1], b * 2 + 1)
                pe.matmul(bank[6][:, :], wqb[:, 1, :], xnT[1][:, :], start=True, stop=True).then_inc(s_proj[1], 1)
                pe.wait_ge(s_qf[1], b * 2 + 2)
                tokens_by(wqb[:, 1, :], 2, 6).then_inc(s_proj[1], 1)
                pe.wait_ge(s_vt[1], b * 2 + 1)
                tokens_by(wqb[:, 2, :], 2, 6).then_inc(s_proj[1], 1)
                pe.wait_ge(s_vt[1], b * 2 + 2)
                for i in range(2):
                    pe.wait_ge(s_nrm, b * 2 + i + 1)
                    if i:
                        pe.wait_ge(s_ew, b * 2 + 1)
                    for t in range(NT):
                        last = pe.transpose(bank[6][0:H, t * P:(t + 1) * P], nrm[:, i, t, :], identf[:, :])
                    last.then_inc(s_nt, 1)
                for i in range(2):
                    pe.wait_ge(s_wn, b * 2 + i + 1)
                    pe.wait_ge(s_ew, b * 2 + 2)
                    if i:
                        pe.wait_ge(s_wte, b * 2 + 1)
                    for t in range(NT):
                        last = pe.matmul(bank[6][:, t * H:(t + 1) * H], ew[:, i, t * P:(t + 1) * P],
                                         identf[0:H, 0:H], start=True, stop=True)
                    last.then_inc(s_wt, 1)
                pe.wait_ge(s_wte, b * 2 + 2)
                pe.wait_ge(s_kw, b * 2 + 1)
                for t in range(NT):
                    own_g = group[:, t, t * GPT:(t + 1) * GPT]
                    pe.matmul(bank[6][:, t * GPT:(t + 1) * GPT], kw[:, 0, t, :], own_g, start=True, stop=True)
                    last = pe.matmul(bank[6][:, L + t * GPT:L + (t + 1) * GPT], wrep[:, t, :], own_g,
                                     start=True, stop=True)
                last.then_inc(s_cmp, 1)
                pe.wait_ge(s_kw, b * 2 + 2)
                pe.wait_ge(s_cat, b * 2 + 1)
                for t in range(NT):
                    pe.matmul(bank[6][0:L, 0:P], group[:, t, :], kw[:, 1, t, :], start=(t == 0), stop=(t == NT - 1))
                for t in range(NT):
                    last = pe.matmul(bank[6][0:L, P:P + H], group[:, t, :], wt[:, 1, t, :], start=(t == 0),
                                     stop=(t == NT - 1))
                last.then_inc(s_cmp, 1)

                def influence(h):
                    pe.wait_ge(s_brz, b * H + h + 1)
                    for k in range(NT):
                        for t in range(NT):
                            last = pe.matmul(bank[6][:, h * NT + k:h * NT + k + 1],
                                             E[:, (h * NT + t) % NE, k * P:(k + 1) * P], rz[:, h, t:t + 1],
                                             start=(t == 0), stop=(t == NT - 1))
                    last.then_inc(s_bi, 1)

                pe.wait_ge(s_stack[1], b * 2 * NPAIR * DMA + 2 * NPAIR * DMA)
                pe.wait_ge(s_cat, b * 2 + 2)
                for n in range(NT * H):
                    h, t = n // NT, n % NT
                    if n >= 3:
                        pe.wait_ge(s_bn, b * NT * H + n - 2)
                    pe.matmul(bank[n % 3][:, :], qst[1][0:B_SC, h, t * P:(t + 1) * P], kst[1][0:B_SC, h, :],
                              start=True, stop=True).then_inc(s_bs, 1)
                    if t == NT - 1 and h:
                        influence(h - 1)
                influence(H - 1)
                pe.wait_ge(s_dg, b + 1)
                for t in range(NT):
                    last = pe.matmul(bank[6][:, t * P:(t + 1) * P], onesf[:, :], diag[:, t, :], start=True,
                                     stop=True)
                last.then_inc(s_rb, 1)
                pe.wait_ge(s_sel, b + 1)
                for t in range(NT):
                    pe.matmul(bank[6][:, 0:HH], ktok[:, 0, t, :], sel[:, t, :], start=(t == 0), stop=(t == NT - 1))
                for t in range(NT):
                    last = pe.matmul(bank[6][L:NK, P:2 * P], sel[:, t, :], ktok[:, 1, t, :], start=(t == 0),
                                     stop=(t == NT - 1))
                last.then_inc(s_gat, 1)
                pe.wait_ge(s_kc, b * NPAIR * DMA + NPAIR * DMA)
                for h in range(H):
                    if h >= 2:
                        pe.wait_ge(s_m1[1], b * H + h - 1)
                    else:
                        pe.wait_ge(s_bn, b * NT * H + NT * H)
                    for t in range(NT):
                        last = pe.matmul(bank[h % 2][:, t * NK:(t + 1) * NK], qst[1][0:B_SC, h, t * P:(t + 1) * P],
                                         kcst[0:B_SC, h, :], start=True, stop=True)
                    last.then_inc(s_s1[1], 1)
                pe.wait_ge(s_m1[1], b * H + H)
                pe.wait_ge(s_hhe, b * 2 + 2)
                transpose_max(1, b, 6)
                pe.wait_ge(s_mrow[1], b * DMA + DMA)

                def weigh_hh(h):
                    pe.wait_ge(s_p[1], b * H + h + 1)
                    if h == HPO:
                        pe.wait_ge(s_o[1], b * 2 + 1)
                    for t in range(NT):
                        c = ((h % HPO) * NT + t) * (HD + 1)
                        last = pe.matmul(bank[2][:, c:c + HD + 1], p2[h % 2][0:NK, t * P:(t + 1) * P],
                                         vcat[0:NK, h, :], start=True, stop=True)
                    last.then_inc(s_pv[1], 1)

                for h in range(H):
                    if h >= 2:
                        pe.wait_ge(s_p[1], b * H + h - 1)
                    pe.matmul(bank[h % 2][0:NK, :], kcst[0:B_MX, h, :], qst[1][0:B_MX, h, :], start=True, stop=True
                              ).then_inc(s_s2[1], 1)
                    if h:
                        weigh_hh(h - 1)
                weigh_hh(H - 1)
                pe.wait_ge(s_ma[1], b * 3 + 1)
                project(1, b, 6, wqb[:, 3, :])
                pe.wait_ge(s_xr[3], b + 1)
                ln(3, b, 6)
                ffn(1, b, 6, 2)


_INS = ['L0_attn_a_x', 'L0_attn_a_w_qkv', 'L0_attn_a_b_qkv', 'L0_attn_a_w_out', 'L0_attn_a_b_out',
        'L0_attn_b_Wq', 'L0_attn_b_Wk', 'L0_attn_b_Wv', 'L0_attn_b_Wo',
        'L0_ffn_w_gate', 'L0_ffn_w_up', 'L0_ffn_w_down']
_OUTS = [((8, 512, 128), 'float32')]


def kernel(**inputs):
    import numpy as _np
    import concourse.bacc as _bacc
    from concourse import mybir as _mybir
    from concourse.bass_utils import run_bass_kernel_spmd as _run

    nc = _bacc.Bacc("TRN2", target_bir_lowering=False, num_devices=1)
    arrays, args = {}, []
    for name in _INS:
        a = _np.ascontiguousarray(inputs[name])
        arrays[f"in_{name}_dram"] = a
        args.append(nc.dram_tensor(f"in_{name}_dram", a.shape, _mybir.dt.from_np(a.dtype), kind="ExternalInput").ap())
    for i, (shape, dtype) in enumerate(_OUTS):
        dt = _mybir.dt.from_np(_np.dtype(dtype))
        args.append(nc.dram_tensor(f"out_{i}_dram", shape, dt, kind="ExternalOutput").ap())
    hybrid_block(nc, *args)
    r = _run(nc, [arrays], core_ids=[0])
    got = tuple(r.results[0][f"out_{i}_dram"] for i in range(len(_OUTS)))
    return got[0]
```

```python
import math
from contextlib import ExitStack

import concourse.bass as bass
from concourse import mybir

ALU = mybir.AluOpType
ACT = mybir.ActivationFunctionType
F32 = mybir.dt.float32
BF16 = mybir.dt.bfloat16
I32 = mybir.dt.int32
AX_X = mybir.AxisListType.X

P = 128
EPS = 1e-5
NEG = -1e30
QSCALE = 8.0 ** -0.5
CLIP = 1e-8
LOG_CLIP = math.log(CLIP)
DMA = 16


def hybrid_block(nc, x, w_qkv, b_qkv, w_out, b_out, wq_b, wk_b, wv_b, wo_b, w_gate, w_up, w_down, out):
    B, T, D = x.shape
    H, HD = 16, D // 16
    NT = T // P
    FC = w_gate.shape[0] // P
    RATIO = min(8, max(1, T // 64))
    L = T // RATIO
    GPT = P // RATIO
    HH = min(128, int(T * 0.1))
    NK = L + HH
    HPO = H // 2
    assert D == P and T == 512 and NK <= P

    Q_PART = (0, 0, 1, 1, 0, 2)
    K_PART = (0, 1, 0, 1, 2, 0)
    NPAIR = len(Q_PART)
    AL = 4
    A_SC = AL + NPAIR * HD
    A_MX = A_SC + 3
    B_SC = NPAIR * HD
    B_MX = B_SC + 3
    TILES = (((0, 0),), ((1, 0), (3, T - P)), ((2, 0),))
    WIDTH = (T, T, T - 2 * P)

    with ExitStack() as ctx:
        def sb(name, shape, dt=F32):
            return ctx.enter_context(nc.sbuf_tensor(name, shape, dt))

        def sem(name):
            return ctx.enter_context(nc.semaphore(name))

        bank = [ctx.enter_context(nc.psum_tensor(f"bank{i}", [P, 512], F32)) for i in range(8)]

        identf = sb("identf", [P, P])
        identb = sb("identb", [P, P], BF16)
        onesf = sb("onesf", [P, P])
        maskqk = sb("maskqk", [P, P], BF16)
        maskkq = sb("maskkq", [P, P], BF16)
        tri = sb("tri", [P, P])
        iota_i = sb("iota_i", [P, HH], I32)
        iota_f = sb("iota_f", [P, HH])
        group = sb("group", [P, NT, L])
        neghalf = sb("neghalf", [P, NT])
        eps = sb("eps", [P, NT])
        setup = sb("setup", [P, 8 * T])
        wload = setup[:, 0:4 * P].rearrange("p (i d) -> p i d", i=4)
        wfp = setup[:, 4 * P:4 * P + 9 * P].rearrange("p (i d) -> p i d", i=3)
        wint = setup[:, 13 * P:22 * P].bitcast(I32).rearrange("p (i d) -> p i d", i=3)
        wqkvT = sb("wqkvT", [P, 3 * P])
        woutT = sb("woutT", [P, P])
        wqb = sb("wqb", [P, 4, P])
        wgT = sb("wgT", [P, FC, P])
        wuT = sb("wuT", [P, FC, P])
        wdT = sb("wdT", [P, FC, P])
        bqk = sb("bqk", [P, 2])
        bqs = sb("bqs", [P, 1])
        bv = sb("bv", [P, P])
        bo = sb("bo", [P, P])

        xs = [sb(f"x{u}", [P, NT, P]) for u in range(5)]
        xbo = sb("xbo", [P, NT, P])
        x2s = sb("x2s", [P, NT, P])
        st = [sb(f"st{u}", [P, NT, 6]) for u in range(4)]
        mv = [sb(f"mv{u}", [P, NT, 2]) for u in range(4)]
        ve = [sb(f"ve{u}", [P, NT]) for u in range(4)]
        rstd = [sb(f"rstd{u}", [P, NT]) for u in range(4)]
        xn = [sb(f"xn{s}", [P, NT, P]) for s in range(2)]
        xnT = [sb(f"xnT{s}", [P, T]) for s in range(2)]
        qf = [sb("qf", [P, 2, T])] * 2
        rest = [sb("rest", [P, 2, T])] * 2
        part = [sb("part", [P, 2, 3, T], BF16)] * 2
        q_stacks = sb("q_stacks", [P, H, T], BF16)
        k_stacks = sb("k_stacks", [P, H, T], BF16)
        qst = [q_stacks[64 * s:64 * s + 64, :, :] for s in range(2)]
        kst = [k_stacks[64 * s:64 * s + 64, :, :] for s in range(2)]
        nm = [sb(f"nm{s}", [P, NT, H]) for s in range(2)]
        qsm = sb("qsm", [64, H, T], BF16)
        nmf = [sb(f"nmf{s}", [H, T]) for s in range(2)]
        nmr = [sb(f"nmr{s}", [H, T]) for s in range(2)]
        nmp = [sb(f"nmp{s}", [H, 3, T], BF16) for s in range(2)]
        vA = sb("vA", [P, NT, H, HD + 1])
        pT = [sb(f"pT{i}", [P, sum(WIDTH)]) for i in range(2)]
        ov = sb("ov", [P, T])
        rzo4 = sb("rzo4", [P, NT, 4])
        rzo = [sb(f"rzo{s}", [P, HPO, NT]) for s in range(2)]
        o = [sb(f"o{s}", [P, NT, P]) for s in range(2)]
        oT = [sb(f"oT{s}", [P, T]) for s in range(2)]
        gated = sb("gated", [P, 2, FC, T])
        alibi_i = gated[0:1, :, :, :].rearrange("p a c t -> p (a c t)")[:, 0:AL * T].bitcast(I32).rearrange(
            "p (a t) -> p a t", a=AL)
        ktok = sb("ktok", [P, 2, NT, P])
        n2 = sb("n2", [P, 2, NT, H])
        nroot = sb("nroot", [P, 2, NT, H])
        nrec = sb("nrec", [P, 2, NT, H])
        nquot = sb("nquot", [P, 2, NT, H])
        nrm = sb("nrm", [P, 2, NT, H])
        nnm = sb("nnm", [H, 2])
        ew = sb("ew", [H, 2, T])
        zw = sb("zw", [H, 2])
        rzw = sb("rzw", [H, 2])
        wt = sb("wt", [P, 2, NT, H])
        kw = sb("kw", [P, 2, NT, P])
        ncl = sb("ncl", [P, 2, NT, H])
        nln = sb("nln", [P, 2, NT, H])
        wrep = sb("wrep", [P, NT, P])
        den = sb("den", [P, L])
        rden = sb("rden", [P, L])
        vden = sb("vden", [L, H])
        vrden = sb("vrden", [L, H])
        NE = 8
        E = setup[:, :].rearrange("p (n t) -> p n t", n=NE)
        alibi = sb("alibi", [1, AL + 1, T], BF16)
        junk = sb("junk", [P, T])
        spare = sb("spare", [P, 1])
        nmB = sb("nmB", [P, H, NT])
        Z = sb("Z", [P, H, NT])
        lnZ = sb("lnZ", [P, H, NT])
        thr = sb("thr", [P, H, NT])
        acc = sb("acc", [P, H, NT])
        rz = sb("rz", [P, H, NT])
        t1 = sb("t1", [P, H, NT])
        t2 = sb("t2", [P, H, NT])
        t3 = sb("t3", [P, H, NT])
        own = sb("own", [P, NT])
        psum = sb("psum", [P, T])
        imp = sb("imp", [P, NT])
        diag = sb("diag", [P, NT, P])
        cnt = sb("cnt", [P, 3, NT])
        rank = sb("rank", [P, NT])
        rank2 = sb("rank2", [P, NT])
        sel = sb("sel", [P, NT, HH])
        kcat = sb("kcat", [P, NK])
        krest = sb("krest", [P, NK])
        kcp = sb("kcp", [P, 3, NK], BF16)
        kcst = sb("kcst", [64, H, NK], BF16)
        vcat = sb("vcat", [P, H, HD])
        vsm = sb("vsm", [P, H, HD + 1])
        p2 = [sb(f"p2_{i}", [P, T]) for i in range(2)]

        part_dram = [nc.dram_tensor(f"part_dram{s}", [B, P, 2, 3, T], BF16, kind="Internal").ap() for s in range(2)]
        x2_dram = nc.dram_tensor("x2_dram", [B, T, D], F32, kind="Internal").ap()
        nm_dram = [nc.dram_tensor(f"nm_dram{s}", [H, 3, T], BF16, kind="Internal").ap() for s in range(2)]
        kcp_dram = nc.dram_tensor("kcp_dram", [P, 3, NK], BF16, kind="Internal").ap()

        s_w = sem("weights_loaded")
        s_const = sem("pool_constants_made")
        s_wfp = sem("weights_scaled")
        s_wtr = sem("weights_transposed")
        s_wev = sem("weights_in_sbuf")
        s_cdve = sem("dve_constants_made")
        s_rows = sem("constant_rows_in_stacks")
        s_xin = sem("x_loaded")
        s_out = sem("out_stored")
        s_x2st = sem("x2_stored")
        s_x2ld = sem("x2_loaded")
        s_qsm = sem("small_query_stack_loaded")
        s_vs = sem("small_values_in_place")
        s_gc = [sem(f"gates_in_sbuf{s}") for s in range(2)]
        s_xr = [None] + [sem(f"x{u}_ready") for u in range(1, 5)]
        s_xbo = sem("x_plus_bias_ready")
        s_st = [sem(f"ln_stats{u}") for u in range(4)]
        s_mv = [sem(f"ln_moments{u}") for u in range(4)]
        s_ve = [sem(f"ln_var_eps{u}") for u in range(4)]
        s_rs = [sem(f"ln_rstd{u}") for u in range(4)]
        s_xn = [sem(f"ln_normed{u}") for u in range(4)]
        s_xt = [sem(f"ln_transposed{u}") for u in range(4)]
        s_xe = [sem(f"ln_evacuated{u}") for u in range(4)]
        s_proj = [sem(f"projected{s}") for s in range(2)]
        s_qf = [sem(f"qk_evacuated{s}") for s in range(2)]
        s_vt = [sem(f"v_evacuated{s}") for s in range(2)]
        s_hi = [sem(f"high_and_mid_parts{s}") for s in range(2)]
        s_rest = [sem(f"rests_and_low_parts{s}") for s in range(2)]
        s_stack = [sem(f"stacks_loaded{s}") for s in range(2)]
        s_s1 = [sem(f"scores_for_max{s}") for s in range(2)]
        s_pd = [sem(f"parts_in_dram{s}") for s in range(2)]
        s_nd = [sem(f"maxima_in_dram{s}") for s in range(2)]
        s_kd = sem("key_parts_in_dram")
        s_m1 = [sem(f"maxima{s}") for s in range(2)]
        s_mt = [sem(f"maxima_transposed{s}") for s in range(2)]
        s_ma = [sem(f"maxima_act_steps{s}") for s in range(2)]
        s_mp = [sem(f"maxima_pool_steps{s}") for s in range(2)]
        s_mrow = [sem(f"maxima_rows_loaded{s}") for s in range(2)]
        s_s2 = [sem(f"scores_minus_max{s}") for s in range(2)]
        s_p = [sem(f"probabilities{s}") for s in range(2)]
        s_pv = [sem(f"heads_weighted{s}") for s in range(2)]
        s_rzo = [sem(f"sums_inverted{s}") for s in range(2)]
        s_o = [sem(f"heads_normalised{s}") for s in range(2)]
        s_ot = [sem(f"o_transposed{s}") for s in range(2)]
        s_oe = [sem(f"oT_evacuated{s}") for s in range(2)]
        s_op = [sem(f"o_projected{s}") for s in range(2)]
        s_g = [sem(f"gate_up_products{s}") for s in range(2)]
        s_sil = [sem(f"silu_done{s}") for s in range(2)]
        s_hid = [sem(f"hidden_done{s}") for s in range(2)]
        s_dn = [sem(f"down_product{s}") for s in range(2)]
        s_sq = sem("squares")
        s_n2 = sem("squared_norms")
        s_nrm = sem("norms")
        s_root = sem("norm_roots_begun")
        s_newton = sem("norm_newton_steps")
        s_nt = sem("norms_transposed")
        s_nnm = sem("norm_maxima")
        s_ew = sem("norm_exponentials")
        s_rzw = sem("norm_sums_inverted")
        s_wn = sem("token_weights")
        s_wt = sem("token_weights_transposed")
        s_wte = sem("token_weights_in_sbuf")
        s_kw = sem("weighted_tokens")
        s_wrep = sem("weights_repeated")
        s_sc = sem("probabilities_in_place")
        s_ov = sem("four_heads_out_of_psum")
        s_tv = sem("four_heads_transposed")
        s_ic = sem("influence_columns_summed")
        s_cmp = sem("compressed_sums")
        s_den = sem("compressed_denominators")
        s_rden = sem("compressed_denominators_inverted")
        s_cat = sem("compressed_in_place")
        s_bs = sem("full_scores")
        s_bm = sem("full_maxima")
        s_be = sem("full_exponentials")
        s_bz = sem("full_log_sums")
        s_bt = sem("clip_thresholds")
        s_bn = sem("entropy_sums")
        s_brz = sem("full_sums_inverted")
        s_bi = sem("influences")
        s_imp = sem("importance_steps")
        s_dg = sem("importance_diagonals")
        s_rb = sem("importance_rows")
        s_cnt = sem("ranks_counted")
        s_sel = sem("selection_made")
        s_gat = sem("heavy_hitters_gathered")
        s_hhe = sem("heavy_hitters_in_place")
        s_ka = sem("key_parts_act")
        s_kp = sem("key_parts_pool")
        s_kc = sem("key_stack_loaded")


        PT_AT = {0: 0, 1: T, 3: T + T - P, 2: 2 * T}

        def stack_rows(st_, j, base):
            return st_[base + j * HD:base + (j + 1) * HD, :, :]

        with nc.Block() as block:
            @block.sync
            def _(sp):
                for c in range(3):
                    sp.dma_start(wload[:, c, :], w_qkv[c * P:(c + 1) * P, :]).then_inc(s_w, DMA)
                sp.dma_start(wload[:, 3, :], w_out).then_inc(s_w, DMA)
                for i, w in enumerate((wq_b, wk_b, wv_b, wo_b)):
                    sp.dma_start(wqb[:, i, :], w).then_inc(s_w, DMA)
                sp.dma_start(wint[:, 0, :].rearrange("p (c d) -> p c d", c=FC),
                             w_gate.rearrange("(c p) d -> p c d", p=P)).then_inc(s_w, DMA)
                sp.dma_start(wint[:, 1, :].rearrange("p (c d) -> p c d", c=FC),
                             w_up.rearrange("(c p) d -> p c d", p=P)).then_inc(s_w, DMA)
                sp.dma_start(wint[:, 2, :], w_down).then_inc(s_w, DMA)
                sp.dma_start(bqk[:, :], b_qkv[0:2 * P].rearrange("(c p) -> p c", p=P),
                             allow_slow_non_contiguous=True).then_inc(s_w, DMA)
                sp.dma_start(bv[:, :], b_qkv[2 * P:3 * P].rearrange("(a n) -> a n", a=1).broadcast_to([P, P])
                             ).then_inc(s_w, DMA)
                sp.dma_start(bo[:, :], b_out.rearrange("(a n) -> a n", a=1).broadcast_to([P, P])).then_inc(s_w, DMA)
                sp.wait_ge(s_cdve, 2)
                ones_row = alibi[:, AL:AL + 1, :].broadcast_to([1, H, T])
                q_rows = (alibi[:, 0:1, :], alibi[:, AL:AL + 1, :], alibi[:, 1:2, :], alibi[:, AL:AL + 1, :])
                k_rows = (alibi[:, AL:AL + 1, :], alibi[:, 2:3, :], alibi[:, AL:AL + 1, :], alibi[:, 3:4, :])
                for r in range(AL):
                    sp.dma_start(qst[0][r:r + 1, :, :], q_rows[r].broadcast_to([1, H, T])).then_inc(s_rows, DMA)
                    sp.dma_start(kst[0][r:r + 1, :, :], k_rows[r].broadcast_to([1, H, T])).then_inc(s_rows, DMA)
                for r in range(3):
                    sp.dma_start(kst[0][A_SC + r:A_SC + r + 1, :, :], ones_row).then_inc(s_rows, DMA)
                    sp.dma_start(kcst[B_SC + r:B_SC + r + 1, :, :],
                                 alibi[:, AL:AL + 1, 0:NK].broadcast_to([1, H, NK])).then_inc(s_rows, DMA)
                sp.wait_ge(s_rows, (2 * AL + 6) * DMA)


            @block.gpsimd
            def _(pool):
                pool.memset(identf[:, :], 0.0)
                pool.memset(identb[:, :], 0.0)
                pool.memset(onesf[:, :], 1.0)
                pool.memset(maskqk[:, :], 0.0)
                pool.memset(maskkq[:, :], 0.0)
                pool.memset(tri[:, :], 1.0)
                pool.memset(neghalf[:, :], -0.5)
                pool.memset(eps[:, :], EPS)
                pool.memset(vA[:, :, :, :], 1.0)
                pool.memset(vsm[:, :, :], 1.0)
                pool.memset(alibi[:, AL:AL + 1, :], 1.0)
                pool.memset(group[:, :, :], 1.0).then_inc(s_const, 1)
                pool.wait_ge(s_const, 1)
                pool.affine_select(out=identf[:, :], in_=identf[:, :], compare_op=ALU.not_equal, fill=1.0, base=0,
                                   pattern=[[-1, P]], channel_multiplier=1)
                pool.affine_select(out=identb[:, :], in_=identb[:, :], compare_op=ALU.not_equal, fill=1.0, base=0,
                                   pattern=[[-1, P]], channel_multiplier=1)
                pool.affine_select(out=maskqk[:, :], in_=maskqk[:, :], compare_op=ALU.is_ge, fill=NEG, base=0,
                                   pattern=[[-1, P]], channel_multiplier=1)
                pool.affine_select(out=maskkq[:, :], in_=maskkq[:, :], compare_op=ALU.is_ge, fill=NEG, base=0,
                                   pattern=[[1, P]], channel_multiplier=-1)
                pool.affine_select(out=tri[:, :], in_=tri[:, :], compare_op=ALU.is_gt, fill=0.0, base=0,
                                   pattern=[[-1, P]], channel_multiplier=1)
                pool.affine_select(out=group[:, :, :], in_=group[:, :, :], compare_op=ALU.is_ge, fill=0.0, base=0,
                                   pattern=[[P, NT], [-RATIO, L]], channel_multiplier=1).then_inc(s_const, 1)
                pool.wait_ge(s_const, 2)
                pool.affine_select(out=group[:, :, :], in_=group[:, :, :], compare_op=ALU.is_ge, fill=0.0,
                                   base=RATIO - 1, pattern=[[-P, NT], [RATIO, L]], channel_multiplier=-1)
                pool.iota(iota_i[:, :], pattern=[[1, HH]], base=0, channel_multiplier=0)
                pool.iota(alibi_i[:, 0, :], pattern=[[-256, T // 256], [0, 256]], base=0, channel_multiplier=0)
                pool.iota(alibi_i[:, 1, :], pattern=[[0, T // 256], [-1, 256]], base=0, channel_multiplier=0)
                pool.iota(alibi_i[:, 2, :], pattern=[[256, T // 256], [0, 256]], base=0, channel_multiplier=0)
                pool.iota(alibi_i[:, 3, :], pattern=[[0, T // 256], [1, 256]], base=0, channel_multiplier=0
                          ).then_inc(s_const, 1)


            @block.scalar
            def _(act):
                act.preload_act_table_set("natural_log_exp_and_others")
                for n, dst in enumerate((wqkvT[:, 0:P], wqkvT[:, P:2 * P], wqkvT[:, 2 * P:3 * P], woutT[:, :])):
                    act.wait_ge(s_wtr, n + 1)
                    act.activation(dst, bank[n][:, 0:P], ACT.Copy).then_inc(s_wev, 1)
                for i, w in enumerate((wgT, wuT, wdT)):
                    for c in range(FC):
                        n = 4 + i * FC + c
                        act.wait_ge(s_wtr, n + 1)
                        act.activation(w[:, c, :], bank[n % 8][:, 0:P], ACT.Copy).then_inc(s_wev, 1)


            @block.vector
            def _(dve):
                dve.wait_ge(s_const, 3)
                dve.tensor_copy(iota_f[:, :], iota_i[:, :]).then_inc(s_cdve, 1)
                dve.tensor_copy(alibi[:, 0:AL, :], alibi_i[:, :, :]).then_inc(s_cdve, 1)
                dve.wait_ge(s_w, 14 * DMA)
                dve.memset(bank[5][:, :], 0.0)
                dve.tensor_scalar(bqs[:, :], bqk[:, 0:1], QSCALE, None, ALU.mult).then_inc(s_cdve, 1)
                dve.tensor_scalar(wfp[:, :, :], wint[:, :, :], 1.0 / 127.0, None, ALU.mult).then_inc(s_wfp, 1)


            @block.tensor
            def _(pe):
                pe.wait_ge(s_const, 3)
                pe.wait_ge(s_w, 14 * DMA)
                for n in range(4):
                    pe.transpose(bank[n][:, 0:P], wload[:, n, :], identf[:, :]).then_inc(s_wtr, 1)
                pe.wait_ge(s_wfp, 1)
                for i in range(3):
                    for c in range(FC):
                        n = 4 + i * FC + c
                        if n >= 8:
                            pe.wait_ge(s_wev, n - 7)
                        pe.transpose(bank[n % 8][:, 0:P], wfp[:, i, c * P:(c + 1) * P], identf[:, :]).then_inc(s_wtr, 1)
                pe.wait_ge(s_wev, 4 + 3 * FC)



        RING = (bank[0], bank[1], bank[2], bank[6])
        RN = len(RING)
        A2_AT = 8
        OUT_W = HPO * NT * (HD + 1)
        QROWS = 32
        HPQ = P // QROWS
        A2_END = A2_AT + 2 * H
        TURN_AT = tuple(min(A2_AT + 2 * (3 * HPQ * (g + 1) + 2) // 3, A2_END) + 1 for g in range(H // HPQ))
        NMAIN = NT * H
        LEAD = 1
        INFL_LAG = 6
        S2_AT = 42

        def a2_tiles(n):
            return [u for u in range(3 * H) if A2_AT + (2 * u) // 3 == n]

        def s1_heads(n):
            return range(2 * n, 2 * n + 2) if n < H // 2 else ()

        def s2_heads(n):
            return range(2 * (n - S2_AT), 2 * (n - S2_AT) + 2) if S2_AT <= n < S2_AT + H // 2 else ()

        CAUSAL = (((3, 0),), ((0, 0), (2, P)), ((1, 0),))

        def one_pass(i, a, p, m, s):
            with nc.Block() as block:
                @block.sync
                def _(sp):
                    if p:
                        sp.dma_start(xs[0][:, :, :],
                                     x[bass.ds(i + 1, 1), :, :].rearrange("a (t p) d -> p (a t) d", p=P)
                                     ).then_inc(s_xin, DMA)
                    if s:
                        for j, pt in enumerate(Q_PART):
                            sp.dma_start(qsm[j * HD:(j + 1) * HD, :, :],
                                         part_dram[1][bass.ds(i - 2, 1), :, 0, pt, :].rearrange(
                                             "a (h d) t -> (a d) h t", d=HD)).then_inc(s_qsm, DMA)
                        sp.dma_start(x2s[:, :, :],
                                     x2_dram[bass.ds(i - 2, 1), :, :].rearrange("a (t p) d -> p (a t) d", p=P)
                                     ).then_inc(s_x2ld, DMA)
                        sp.wait_ge(s_ka, 2)
                        sp.wait_ge(s_kp, 2)
                        sp.dma_start(kcp_dram, kcp[:, :, :]).then_inc(s_kd, DMA)
                        sp.wait_ge(s_kd, DMA)
                        for j, pt in enumerate(K_PART):
                            sp.dma_start(stack_rows(kcst, j, 0),
                                         kcp_dram[:, pt, :].rearrange("(h d) t -> d h t", d=HD)).then_inc(s_kc, DMA)
                    if m:
                        sp.wait_ge(s_hi[1], 4)
                        sp.wait_ge(s_rest[1], 4)
                        pd = part_dram[1][bass.ds(i - 1, 1), :, :, :, :]
                        sp.dma_start(pd.rearrange("a p i c t -> p (a i) c t"), part[1][:, :, :, :]
                                     ).then_inc(s_pd[1], DMA)
                        sp.wait_ge(s_pd[1], DMA)
                        for k, (stk, parts) in enumerate(((qst[1], Q_PART), (kst[1], K_PART))):
                            for j, pt in enumerate(parts):
                                sp.dma_start(stack_rows(stk, j, 0),
                                             part_dram[1][bass.ds(i - 1, 1), :, k, pt, :].rearrange(
                                                 "a (h d) t -> (a d) h t", d=HD)).then_inc(s_stack[1], DMA)

                    def max_rows(s_, stk, base):
                        sp.wait_ge(s_mp[s_], 2)
                        sp.dma_start(nm_dram[s_], nmp[s_][:, :, :]).then_inc(s_nd[s_], DMA)
                        sp.wait_ge(s_nd[s_], DMA)
                        sp.dma_start(stk[base:base + 3, :, :], nm_dram[s_].rearrange("h r t -> r h t")
                                     ).then_inc(s_mrow[s_], DMA)

                    if a:
                        max_rows(0, qst[0], A_SC)
                    if s:
                        max_rows(1, qsm, B_SC)
                    if a:
                        sp.wait_ge(s_xr[2], 1)
                        sp.dma_start(x2_dram[bass.ds(i, 1), :, :].rearrange("a (t p) d -> p (a t) d", p=P),
                                     xs[2][:, :, :]).then_inc(s_x2st, DMA)
                    if p:
                        sp.wait_ge(s_hi[0], 4)
                        sp.wait_ge(s_rest[0], 4)
                        sp.dma_start(part_dram[0][0], part[0][:, :, :, :]).then_inc(s_pd[0], DMA)
                        sp.wait_ge(s_pd[0], DMA)
                        if a:
                            sp.wait_ge(s_s2[0], 3 * H)
                        for k, (stk, parts) in enumerate(((qst[0], Q_PART), (kst[0], K_PART))):
                            for j, pt in enumerate(parts):
                                sp.dma_start(stack_rows(stk, j, AL),
                                             part_dram[0][0][:, k, pt, :].rearrange("(h d) t -> d h t", d=HD)
                                             ).then_inc(s_stack[0], DMA)
                    if s:
                        sp.wait_ge(s_xr[4], 1)
                        sp.dma_start(out[bass.ds(i - 2, 1), :, :].rearrange("a (t p) d -> p (a t) d", p=P),
                                     xs[4][:, :, :]).then_inc(s_out, DMA)
                        sp.wait_ge(s_out, DMA)
                    if a:
                        sp.wait_ge(s_x2st, DMA)
                    if p:
                        sp.wait_ge(s_stack[0], 2 * NPAIR * DMA)

                @block.gpsimd
                def _(pool):
                    def ln(u):
                        pool.wait_ge(s_mv[u], 1)
                        pool.tensor_tensor(ve[u][:, :], mv[u][:, :, 1], eps[:, :], ALU.add).then_inc(s_ve[u], 1)
                        pool.wait_ge(s_ve[u], 1)
                        pool.tensor_tensor(rstd[u][:, :], ve[u][:, :], neghalf[:, :], ALU.pow).then_inc(s_rs[u], 1)

                    def rests(k):
                        pool.wait_ge(s_hi[k], 1)
                        for c in range(2):
                            if c:
                                pool.wait_ge(s_hi[k], 2)
                            pool.tensor_tensor(rest[k][:, c, :], qf[k][:, c, :], part[k][:, c, 0, :], ALU.subtract
                                               ).then_inc(s_rest[k], 1)

                    def lows(k):
                        for c in range(2):
                            pool.wait_ge(s_hi[k], 3 + c)
                            pool.tensor_tensor(part[k][:, c, 2, :], rest[k][:, c, :], part[k][:, c, 1, :],
                                               ALU.subtract).then_inc(s_rest[k], 1)

                    def max_rest(k):
                        pool.wait_ge(s_ma[k], 2)
                        pool.tensor_tensor(nmr[k][:, :], nmf[k][:, :], nmp[k][:, 0, :], ALU.subtract
                                           ).then_inc(s_mp[k], 1)

                    def max_low(k):
                        pool.wait_ge(s_ma[k], 3)
                        pool.tensor_tensor(nmp[k][:, 2, :], nmr[k][:, :], nmp[k][:, 1, :], ALU.subtract
                                           ).then_inc(s_mp[k], 1)

                    def influence(n):
                        pool.wait_ge(s_sc, n + 1)
                        pool.wait_ge(s_bi, n + 1)
                        pool.tensor_tensor(psum[:, :], psum[:, :], E[:, n % NE, :], ALU.add).then_inc(s_bi, 1)

                    if m:
                        pool.memset(psum[:, :], 0.0).then_inc(s_bi, 1)
                    if s:
                        pool.wait_ge(s_ka, 1)
                        pool.tensor_tensor(krest[:, :], kcat[:, :], kcp[:, 0, :], ALU.subtract).then_inc(s_kp, 1)
                        pool.wait_ge(s_ka, 2)
                        pool.tensor_tensor(kcp[:, 2, :], krest[:, :], kcp[:, 1, :], ALU.subtract).then_inc(s_kp, 1)
                    if m:
                        ln(2)
                        rests(1)
                        lows(1)
                        for c in range(2):
                            pool.wait_ge(s_vt[1], c + 1)
                            pool.tensor_tensor(kw[:, c, :, :], ktok[:, c, :, :], ktok[:, c, :, :], ALU.mult
                                               ).then_inc(s_sq, 1)
                    for n in range(NMAIN):
                        if m:
                            h, t = n // NT, n % NT
                            pool.wait_ge(s_bz, n + 1)
                            pool.tensor_tensor(thr[:, h, t:t + 1], lnZ[:, h, t:t + 1], nmB[:, h, t:t + 1],
                                               ALU.subtract).then_inc(s_bt, 1)
                            if n >= INFL_LAG:
                                influence(n - INFL_LAG)
                        if a and n == 1:
                            max_rest(0)
                        if a and n == 2:
                            max_low(0)
                        if s and n == 10:
                            max_rest(1)
                        if s and n == 11:
                            max_low(1)
                        if a and n == 44:
                            ln(1)
                        if p and n == 46:
                            pool.wait_ge(s_xin, DMA)
                            if a:
                                pool.wait_ge(s_xr[1], 1)
                            for t in range(NT):
                                last = pool.tensor_tensor(xbo[:, t, :], xs[0][:, t, :], bo[:, :], ALU.add)
                            last.then_inc(s_xbo, 1)
                        if p and n == 50:
                            ln(0)
                        if s and n == 54:
                            ln(3)
                        if p and n == 60:
                            rests(0)
                        if p and n == 62:
                            lows(0)
                    if m:
                        for n in range(NMAIN - INFL_LAG, NMAIN):
                            influence(n)

                @block.scalar
                def _(act):
                    def ln(u, ps):
                        act.wait_ge(s_xt[u], 1)
                        act.activation(xnT[u // 2][:, :], ps[:, :], ACT.Copy).then_inc(s_xe[u], 1)

                    def qk(k, c, ps):
                        act.wait_ge(s_proj[k], c + 1)
                        if k == 0 and c == 0 and m:
                            act.wait_ge(s_rest[1], 4)
                        if k == 0:
                            act.activation(qf[k][:, c, :], ps[:, :], ACT.Identity,
                                           bias=bqk[:, 1:2] if c else bqs[:, 0:1],
                                           scale=1.0 if c else QSCALE).then_inc(s_qf[k], 1)
                        else:
                            act.activation(qf[k][:, c, :], ps[:, :], ACT.Copy, scale=1.0 if c else QSCALE
                                           ).then_inc(s_qf[k], 1)

                    def high(k, c):
                        act.wait_ge(s_qf[k], c + 1)
                        if k == 0 and c == 0 and m:
                            act.wait_ge(s_pd[1], DMA)
                        act.activation(part[k][:, c, 0, :], qf[k][:, c, :], ACT.Copy).then_inc(s_hi[k], 1)

                    def mid(k, c):
                        act.wait_ge(s_rest[k], c + 1)
                        act.activation(part[k][:, c, 1, :], rest[k][:, c, :], ACT.Copy).then_inc(s_hi[k], 1)

                    def max_high(k):
                        act.wait_ge(s_mt[k], 1)
                        act.activation(nmf[k][:, :], bank[7][0:H, :], ACT.Copy).then_inc(s_ma[k], 1)
                        act.wait_ge(s_ma[k], 1)
                        act.activation(nmp[k][:, 0, :], nmf[k][:, :], ACT.Copy).then_inc(s_ma[k], 1)

                    def max_mid(k):
                        act.wait_ge(s_mp[k], 1)
                        act.activation(nmp[k][:, 1, :], nmr[k][:, :], ACT.Copy).then_inc(s_ma[k], 1)

                    def probabilities(n):
                        h, t = n // NT, n % NT
                        act.wait_ge(s_bn, n + 1)
                        act.wait_ge(s_brz, h + 1)
                        act.activation(E[:, n % NE, :], E[:, n % NE, :], ACT.Copy, scale=rz[:, h, t:t + 1]
                                       ).then_inc(s_sc, 1)

                    def out_t(k, ps):
                        act.wait_ge(s_ot[k], 1)
                        act.activation(oT[k][:, :], ps[:, :], ACT.Copy).then_inc(s_oe[k], 1)

                    def gate(k, c, ps):
                        act.wait_ge(s_g[k], c + 1)
                        act.activation(gated[:, k, c, :], ps[:, :], ACT.Copy).then_inc(s_gc[k], 1)

                    def silu(k):
                        act.wait_ge(s_gc[k], FC)
                        act.activation(gated[:, k, :, :], gated[:, k, :, :], ACT.Silu).then_inc(s_sil[k], 1)
                        act.preload_act_table_set("natural_log_exp_and_others")

                    if s:
                        act.activation(kcp[:, 0, :], kcat[:, :], ACT.Copy).then_inc(s_ka, 1)
                        act.activation(vsm[0:NK, :, 0:HD], vcat[0:NK, :, :], ACT.Copy).then_inc(s_vs, 1)
                        act.wait_ge(s_kp, 1)
                        act.activation(kcp[:, 1, :], krest[:, :], ACT.Copy).then_inc(s_ka, 1)
                    if m:
                        ln(2, bank[6])
                        qk(1, 0, bank[6])
                        qk(1, 1, bank[6])
                        high(1, 0)
                        high(1, 1)
                        act.wait_ge(s_proj[1], 3)
                        act.activation(ktok[:, 0, :, :].rearrange("p t d -> p (t d)"), bank[6][:, :], ACT.Copy
                                       ).then_inc(s_vt[1], 1)
                        mid(1, 0)
                        act.wait_ge(s_proj[1], 4)
                        act.activation(ktok[:, 1, :, :].rearrange("p t d -> p (t d)"), bank[6][:, :], ACT.Copy
                                       ).then_inc(s_vt[1], 1)
                        mid(1, 1)
                        act.wait_ge(s_n2, 2)
                        act.activation(nln[:, :, :, :], ncl[:, :, :, :], ACT.Ln).then_inc(s_root, 1)
                        act.wait_ge(s_root, 1)
                        act.activation(nroot[:, :, :, :], nln[:, :, :, :], ACT.Exp, scale=0.5).then_inc(s_root, 1)
                        for c in range(2):
                            act.wait_ge(s_nnm, c + 1)
                            act.activation(ew[:, c, :], bank[6][0:H, :], ACT.Exp, bias=nnm[:, c:c + 1],
                                           accum_out=zw[:, c:c + 1]).then_inc(s_ew, 1)
                        for c in range(2):
                            act.wait_ge(s_ew, c + 1)
                            act.wait_ge(s_rzw, c + 1)
                            act.activation(ew[:, c, :], ew[:, c, :], ACT.Copy, scale=rzw[:, c:c + 1]
                                           ).then_inc(s_wn, 1)
                        act.wait_ge(s_wt, 1)
                        act.activation(wt[:, :, :, :].rearrange("p i t h -> p (i t h)"), bank[6][:, 0:2 * NT * H],
                                       ACT.Copy).then_inc(s_wte, 1)
                        act.wait_ge(s_wte, 1)
                        act.activation(wrep[:, :, :].rearrange("p t (h d) -> p (t h) d", d=HD),
                                       wt[:, 0, :, :].rearrange("p t (h a) -> p (t h) a", a=1).broadcast_to(
                                           [P, NT * H, HD]), ACT.Copy).then_inc(s_wrep, 1)
                    for n in range(NMAIN):
                        if a:
                            if n == 0:
                                max_high(0)
                            if n == 2:
                                max_mid(0)
                            for u in a2_tiles(n):
                                h, c = u // 3, u % 3
                                if h >= 2:
                                    act.wait_ge(s_pv[0], h - 1)
                                act.wait_ge(s_s2[0], u + 1)
                                act.activation(pT[h % 2][:, c * T:c * T + WIDTH[c]], bank[3 + u % 2][:, 0:WIDTH[c]],
                                               ACT.Exp).then_inc(s_p[0], 1)
                        if s:
                            if n == 9:
                                max_high(1)
                            if n == 11:
                                max_mid(1)
                            for h in s2_heads(n):
                                if h >= 2:
                                    act.wait_ge(s_pv[1], h - 1)
                                act.wait_ge(s_s2[1], h + 1)
                                act.activation(p2[h % 2][0:NK, :], bank[3 + h % 2][0:NK, :], ACT.Exp
                                               ).then_inc(s_p[1], 1)
                        if m:
                            h, t = n // NT, n % NT
                            act.wait_ge(s_bm, n + 1)
                            if n >= NE:
                                act.wait_ge(s_bn, n - NE + 1)
                                act.wait_ge(s_bi, n - NE + 2)
                            act.activation(E[:, n % NE, :], RING[n % RN][:, :], ACT.Exp, bias=nmB[:, h, t:t + 1],
                                           accum_out=Z[:, h, t:t + 1]).then_inc(s_be, 1)
                            act.wait_ge(s_be, n + 1)
                            act.activation(lnZ[:, h, t:t + 1], Z[:, h, t:t + 1], ACT.Ln, scale=CLIP
                                           ).then_inc(s_bz, 1)
                            if n >= INFL_LAG:
                                probabilities(n - INFL_LAG)
                        if a:
                            if n in TURN_AT:
                                g = TURN_AT.index(n)
                                act.wait_ge(s_pv[0], HPQ * (g + 1))
                                if g:
                                    act.wait_ge(s_tv, g)
                                act.activation(ov[:, :], bank[5][:, :], ACT.Copy).then_inc(s_ov, 1)
                            if n == 42:
                                out_t(0, bank[7])
                            if n == 47:
                                ln(1, bank[7])
                            if 48 <= n < 48 + FC:
                                gate(0, n - 48, bank[7])
                            if n == 48 + FC:
                                silu(0)
                        if s:
                            if n == 52:
                                out_t(1, bank[3])
                            if n == 56:
                                ln(3, bank[3])
                            if 57 <= n < 57 + FC:
                                gate(1, n - 57, bank[3])
                            if n == 57 + FC:
                                silu(1)
                        if p:
                            if n == 57:
                                ln(0, bank[7])
                            if n == 58:
                                qk(0, 0, bank[7])
                            if n == 59:
                                qk(0, 1, bank[7])
                                high(0, 0)
                            if n == 60:
                                high(0, 1)
                            if n == 61:
                                mid(0, 0)
                            if n == 62:
                                mid(0, 1)
                    if m:
                        for n in range(NMAIN - INFL_LAG, NMAIN):
                            probabilities(n)

                @block.vector
                def _(dve):
                    def stats(u):
                        for t in range(NT):
                            last = dve.bn_stats(st[u][:, t, :], (xs[0], xs[1], xs[2], xs[3])[u][:, t, :])
                        last.then_inc(s_st[u], 1)
                        dve.wait_ge(s_st[u], 1)
                        for t in range(NT):
                            last = dve.bn_aggr(mv[u][:, t, :], st[u][:, t, :])
                        last.then_inc(s_mv[u], 1)

                    def normalise(u):
                        dve.wait_ge(s_rs[u], 1)
                        if u == 0 and a:
                            dve.wait_ge(s_xt[1], 1)
                        if u == 3 and m:
                            dve.wait_ge(s_xt[2], 1)
                        for t in range(NT):
                            last = dve.tensor_scalar(xn[u // 2][:, t, :], xs[u][:, t, :], mv[u][:, t, 0:1],
                                                     rstd[u][:, t:t + 1], ALU.subtract, ALU.mult)
                        last.then_inc(s_xn[u], 1)

                    def causal_maxima(h):
                        for c, parts in enumerate(CAUSAL):
                            u = 3 * h + c
                            dve.wait_ge(s_s1[0], u + 1)
                            for t, at in parts:
                                last = dve.tensor_reduce(nm[0][:, t, h:h + 1],
                                                         bank[3 + u % 2][:, at:at + (t + 1) * P], AX_X, ALU.max,
                                                         negate=True)
                            last.then_inc(s_m1[0], 1)

                    def norm_heads(k, half):
                        dve.wait_ge(s_pv[k], (half + 1) * HPO)
                        ps = bank[5][:, 0:OUT_W].rearrange("p (h t e) -> p h t e", h=HPO, t=NT)
                        dve.reciprocal(rzo[k][:, :, :], ps[:, :, :, HD]).then_inc(s_rzo[k], 1)
                        dve.wait_ge(s_rzo[k], half + 1)
                        for t in range(NT):
                            last = dve.tensor_tensor(
                                o[k][:, t, half * HPO * HD:(half + 1) * HPO * HD].rearrange("p (h d) -> p h d", d=HD),
                                ps[:, :, t, 0:HD], rzo[k][:, :, t:t + 1].broadcast_to([P, HPO, HD]), ALU.mult)
                        last.then_inc(s_o[k], 1)

                    def norm_four(g):
                        dve.wait_ge(s_tv, g + 1)
                        ps = bank[7][:, :].rearrange("p (t j e) -> p t j e", t=NT, j=HPQ)
                        dve.reciprocal(rzo4[:, :, :], ps[:, :, :, HD]).then_inc(s_rzo[0], 1)
                        dve.wait_ge(s_rzo[0], g + 1)
                        dve.tensor_tensor(
                            o[0][:, :, g * HPQ * HD:(g + 1) * HPQ * HD].rearrange("p t (j d) -> p t j d", d=HD),
                            ps[:, :, :, 0:HD],
                            rzo4[:, :, :].rearrange("p t (j a) -> p t j a", a=1).broadcast_to([P, NT, HPQ, HD]),
                            ALU.mult).then_inc(s_o[0], 1)

                    def residual(u, ps, written, before):
                        dve.wait_ge(written, 1)
                        dve.tensor_tensor(xs[u][:, :, :].rearrange("p t d -> p (t d)"), ps[:, :],
                                          before[:, :, :].rearrange("p t d -> p (t d)"), ALU.add
                                          ).then_inc(s_xr[u], 1)

                    def hidden(k, c, ps):
                        dve.wait_ge(s_g[k], FC + c + 1)
                        dve.wait_ge(s_sil[k], 1)
                        dve.tensor_tensor(gated[:, k, c, :], ps[:, :], gated[:, k, c, :], ALU.mult
                                          ).then_inc(s_hid[k], 1)

                    def entropy(n):
                        h, t = n // NT, n % NT
                        if n:
                            dve.wait_ge(s_bn, n)
                        dve.wait_ge(s_bt, n + 1)
                        dve.scalar_tensor_tensor(out=junk[:, :], in0=RING[n % RN][:, :], scalar=thr[:, h, t:t + 1],
                                                 in1=E[:, n % NE, :], op0=ALU.max, op1=ALU.mult,
                                                 accum_out=acc[:, h, t:t + 1]).then_inc(s_bn, 1)
                        if t == NT - 1:
                            dve.reciprocal(rz[:, h, :], Z[:, h, :]).then_inc(s_brz, 1)

                    if m:
                        stats(2)
                    for h in range(H):
                        if a:
                            causal_maxima(h)
                        if not m:
                            continue
                        if h == 0:
                            normalise(2)
                        if h == 7:
                            dve.wait_ge(s_sq, 2)
                            dve.tensor_reduce(n2[:, :, :, :].rearrange("p i t h -> p (i t h)"),
                                              kw[:, :, :, :].rearrange("p i t (h d) -> p (i t h) d", d=HD), AX_X,
                                              ALU.add).then_inc(s_n2, 1)
                            dve.wait_ge(s_n2, 1)
                            dve.tensor_scalar(ncl[:, :, :, :], n2[:, :, :, :], 1e-18, None, ALU.max
                                              ).then_inc(s_n2, 1)
                        if h == 8:
                            dve.wait_ge(s_root, 2)
                            dve.reciprocal(nrec[:, :, :, :], nroot[:, :, :, :]).then_inc(s_newton, 1)
                            dve.wait_ge(s_newton, 1)
                            dve.scalar_tensor_tensor(out=nquot[:, :, :, :], in0=n2[:, :, :, :], scalar=0.5,
                                                     in1=nrec[:, :, :, :], op0=ALU.mult, op1=ALU.mult
                                                     ).then_inc(s_newton, 1)
                            dve.wait_ge(s_newton, 2)
                            dve.scalar_tensor_tensor(out=nrm[:, :, :, :], in0=nroot[:, :, :, :], scalar=0.5,
                                                     in1=nquot[:, :, :, :], op0=ALU.mult, op1=ALU.add
                                                     ).then_inc(s_nrm, 1)
                        if h in (10, 12):
                            c = (h - 10) // 2
                            dve.wait_ge(s_nt, c + 1)
                            dve.tensor_reduce(nnm[:, c:c + 1], bank[6][0:H, :], AX_X, ALU.max, negate=True
                                              ).then_inc(s_nnm, 1)
                        if h in (11, 13):
                            c = (h - 11) // 2
                            dve.wait_ge(s_ew, c + 1)
                            dve.reciprocal(rzw[:, c:c + 1], zw[:, c:c + 1]).then_inc(s_rzw, 1)
                        if h == 14:
                            dve.wait_ge(s_wte, 1)
                            dve.tensor_tensor(kw[:, :, :, :].rearrange("p i t (h d) -> p (i t h) d", d=HD),
                                              ktok[:, :, :, :].rearrange("p i t (h d) -> p (i t h) d", d=HD),
                                              wt[:, :, :, :].rearrange("p i t (h a) -> p (i t h) a", a=1
                                                                       ).broadcast_to([P, 2 * NT * H, HD]),
                                              ALU.mult).then_inc(s_kw, 1)
                    if m:
                        dve.wait_ge(s_cmp, 1)
                        dve.tensor_scalar(den[:, :], bank[6][:, L:2 * L], 1e-8, None, ALU.add)
                        dve.tensor_scalar(vden[:, :], bank[6][0:L, 3 * P:3 * P + H], 1e-8, None, ALU.add
                                          ).then_inc(s_den, 1)
                        dve.wait_ge(s_den, 1)
                        dve.reciprocal(rden[:, :], den[:, :])
                        dve.reciprocal(vrden[:, :], vden[:, :]).then_inc(s_rden, 1)
                        dve.wait_ge(s_rden, 1)
                        if s:
                            dve.wait_ge(s_kp, 1)
                            dve.wait_ge(s_vs, 1)
                        dve.tensor_tensor(kcat[:, 0:L], bank[6][:, 0:L], rden[:, :], ALU.mult).then_inc(s_cat, 1)
                        dve.tensor_tensor(vcat[0:L, :, :],
                                          bank[6][0:L, 2 * P:3 * P].rearrange("p (h d) -> p h d", d=HD),
                                          vrden[:, :].rearrange("p (h a) -> p h a", a=1).broadcast_to([L, H, HD]),
                                          ALU.mult).then_inc(s_cat, 1)
                    for n in range(NMAIN):
                        if m:
                            h, t = n // NT, n % NT
                            dve.wait_ge(s_bs, n + 1)
                            dve.tensor_reduce(nmB[:, h, t:t + 1], RING[n % RN][:, :], AX_X, ALU.max, negate=True
                                              ).then_inc(s_bm, 1)
                            if n >= 2:
                                entropy(n - 2)
                        if s:
                            for h in s1_heads(n):
                                dve.wait_ge(s_s1[1], h + 1)
                                dve.tensor_reduce(nm[1][:, :, h], bank[3 + h % 2][:, 0:NT * NK].rearrange(
                                    "p (t k) -> p t k", t=NT), AX_X, ALU.max, negate=True).then_inc(s_m1[1], 1)
                        if a:
                            if n in TURN_AT:
                                norm_four(TURN_AT.index(n))
                            if n == 43:
                                residual(1, bank[7], s_op[0], xbo)
                            if n == 44:
                                dve.wait_ge(s_xr[1], 1)
                                stats(1)
                            if n == 46:
                                normalise(1)
                            if 52 <= n < 52 + FC:
                                hidden(0, n - 52, bank[7])
                            if n == 55:
                                if m:
                                    dve.wait_ge(s_xn[2], 1)
                                residual(2, bank[7], s_dn[0], xs[1])
                        if s:
                            if n == 46:
                                norm_heads(1, 0)
                            if n == 50:
                                norm_heads(1, 1)
                            if n == 53:
                                dve.wait_ge(s_x2ld, DMA)
                                residual(3, bank[3], s_op[1], x2s)
                                dve.wait_ge(s_xr[3], 1)
                                stats(3)
                            if n == 55:
                                normalise(3)
                            if 61 <= n < 61 + FC:
                                hidden(1, n - 61, bank[3])
                        if p:
                            if n == 49:
                                dve.wait_ge(s_xin, DMA)
                                stats(0)
                            if n == 51:
                                normalise(0)
                            if n == 60:
                                dve.wait_ge(s_proj[0], 3)
                                if a:
                                    dve.wait_ge(s_pv[0], H)
                                for t in range(NT):
                                    last = dve.tensor_tensor(
                                        vA[:, t, :, 0:HD],
                                        bank[7][:, t * P:(t + 1) * P].rearrange("p (h d) -> p h d", d=HD),
                                        bv[:, :].rearrange("p (h d) -> p h d", d=HD), ALU.add)
                                last.then_inc(s_vt[0], 1)
                    if m:
                        entropy(NMAIN - 2)
                        entropy(NMAIN - 1)
                        dve.wait_ge(s_bn, NMAIN)
                        dve.wait_ge(s_brz, H)
                        dve.tensor_tensor(t1[:, :, :], acc[:, :, :], rz[:, :, :], ALU.mult).then_inc(s_imp, 1)
                        dve.wait_ge(s_imp, 1)
                        dve.scalar_tensor_tensor(out=t2[:, :, :], in0=t1[:, :, :], scalar=LOG_CLIP, in1=thr[:, :, :],
                                                 op0=ALU.add, op1=ALU.subtract).then_inc(s_imp, 1)
                        dve.wait_ge(s_imp, 2)
                        dve.scalar_tensor_tensor(out=t3[:, :, :], in0=t2[:, :, :], scalar=0.4 / 0.3, in1=rz[:, :, :],
                                                 op0=ALU.mult, op1=ALU.add).then_inc(s_imp, 1)
                        dve.wait_ge(s_imp, 3)
                        dve.tensor_reduce(own[:, :], t3[:, :, :].rearrange("p h t -> p t h"), AX_X, ALU.add
                                          ).then_inc(s_imp, 1)
                        dve.wait_ge(s_ic, 1)
                        dve.wait_ge(s_imp, 4)
                        dve.tensor_tensor(imp[:, :], own[:, :], bank[0][:, 0:NT], ALU.add).then_inc(s_imp, 1)
                        dve.wait_ge(s_imp, 5)
                        for t in range(NT):
                            last = dve.tensor_scalar(diag[:, t, :], identf[:, :], imp[:, t:t + 1], None, ALU.mult)
                        last.then_inc(s_dg, 1)
                    if s:
                        residual(4, bank[3], s_dn[1], xs[3])
                    if m:
                        dve.wait_ge(s_rb, 1)
                        for t in range(NT):
                            dve.tensor_scalar(E[:, t, 0:T - t * P], bank[6][:, t * P:T], imp[:, t:t + 1], None,
                                              ALU.is_gt, ALU.add, accum_out=cnt[:, 0, t:t + 1])
                            dve.scalar_tensor_tensor(out=E[:, 4, t * P:(t + 1) * P],
                                                     in0=bank[6][:, t * P:(t + 1) * P], scalar=imp[:, t:t + 1],
                                                     in1=tri[:, :], op0=ALU.is_equal, op1=ALU.mult,
                                                     accum_out=cnt[:, 1, t:t + 1])
                            if t:
                                last = dve.tensor_scalar(E[:, 4 + t, 0:t * P], bank[6][:, 0:t * P],
                                                         imp[:, t:t + 1], None, ALU.is_ge, ALU.add,
                                                         accum_out=cnt[:, 2, t:t + 1])
                            else:
                                dve.memset(cnt[:, 2, 0:1], 0.0)
                        last.then_inc(s_cnt, 1)
                        dve.wait_ge(s_cnt, 1)
                        dve.tensor_tensor(rank2[:, :], cnt[:, 0, :], cnt[:, 1, :], ALU.add).then_inc(s_cnt, 1)
                        dve.wait_ge(s_cnt, 2)
                        dve.tensor_tensor(rank[:, :], rank2[:, :], cnt[:, 2, :], ALU.add).then_inc(s_cnt, 1)
                        dve.wait_ge(s_cnt, 3)
                        for t in range(NT):
                            last = dve.tensor_scalar(sel[:, t, :], iota_f[:, :], rank[:, t:t + 1], None,
                                                     ALU.is_equal)
                        last.then_inc(s_sel, 1)
                        dve.wait_ge(s_gat, 1)
                        dve.tensor_copy(kcat[:, L:NK], bank[6][:, 0:HH])
                        dve.tensor_copy(vcat[L:NK, :, :], bank[6][L:NK, P:2 * P].rearrange("p (h d) -> p h d", d=HD))

                @block.tensor
                def _(pe):
                    def ln(u, ps):
                        pe.wait_ge(s_xn[u], 1)
                        for t in range(NT):
                            last = pe.transpose(ps[:, t * P:(t + 1) * P], xn[u // 2][:, t, :], identf[:, :])
                        last.then_inc(s_xt[u], 1)

                    def channels_by(w, k, u, ps):
                        pe.matmul(ps[:, :], w, xnT[u // 2][:, :], start=True, stop=True).then_inc(s_proj[k], 1)

                    def tokens_by(w, k, u, ps):
                        for t in range(NT):
                            last = pe.matmul(ps[:, t * P:(t + 1) * P], xnT[u // 2][:, t * P:(t + 1) * P], w,
                                             start=True, stop=True)
                        last.then_inc(s_proj[k], 1)

                    def causal_scores(h):
                        for c, parts in enumerate(CAUSAL):
                            u = 3 * h + c
                            if u >= 2:
                                pe.wait_ge(s_m1[0], u - 1)
                            for t, at in parts:
                                pe.matmul(bank[3 + u % 2][:, at:at + (t + 1) * P],
                                          qst[0][0:A_SC, h, t * P:(t + 1) * P], kst[0][0:A_SC, h, 0:(t + 1) * P],
                                          start=True, stop=True)
                                last = pe.matmul(bank[3 + u % 2][:, at + t * P:at + (t + 1) * P], identb[:, :],
                                                 maskqk[:, :], start=False, stop=True, skip_group_check=True)
                            last.then_inc(s_s1[0], 1)

                    def transpose_max(k):
                        for t in range(NT):
                            last = pe.transpose(bank[7][0:H, t * P:(t + 1) * P], nm[k][:, t, :], identf[:, :])
                        last.then_inc(s_mt[k], 1)

                    def causal_minus_max(u):
                        h, parts = u // 3, TILES[u % 3]
                        if u >= 2:
                            pe.wait_ge(s_p[0], u - 1)
                        elif s:
                            pe.wait_ge(s_m1[1], H)
                        for k, at in parts:
                            w = T - k * P
                            pe.matmul(bank[3 + u % 2][:, at:at + w], kst[0][0:A_MX, h, k * P:(k + 1) * P],
                                      qst[0][0:A_MX, h, k * P:T], start=True, stop=True)
                            last = pe.matmul(bank[3 + u % 2][:, at:at + P], identb[:, :], maskkq[:, :],
                                             start=False, stop=True, skip_group_check=True)
                        last.then_inc(s_s2[0], 1)

                    def weigh(h):
                        pe.wait_ge(s_p[0], 3 * h + 3)
                        if h >= HPQ and h % HPQ == 0:
                            pe.wait_ge(s_ov, h // HPQ)
                        q = QROWS * (h % HPQ)
                        for k in range(NT):
                            last = pe.matmul(bank[5][q:q + HD + 1, k * P:T], vA[:, k, h, :],
                                             pT[h % 2][:, PT_AT[k]:PT_AT[k] + T - k * P], start=(k == 0), stop=True,
                                             skip_group_check=(k > 0))
                        last.then_inc(s_pv[0], 1)

                    def turn(g):
                        pe.wait_ge(s_ov, g + 1)
                        if g:
                            pe.wait_ge(s_o[0], g)
                        elif s:
                            pe.wait_ge(s_ma[1], 1)
                        else:
                            pe.wait_ge(s_ma[0], 1)
                        for t in range(NT):
                            last = pe.transpose(bank[7][:, t * P:(t + 1) * P], ov[:, t * P:(t + 1) * P], identf[:, :])
                        last.then_inc(s_tv, 1)

                    def weigh_hh(h):
                        pe.wait_ge(s_p[1], h + 1)
                        if h == 0 and a:
                            pe.wait_ge(s_ov, H // HPQ)
                        if h == HPO:
                            pe.wait_ge(s_o[1], 1)
                        for t in range(NT):
                            c = ((h % HPO) * NT + t) * (HD + 1)
                            last = pe.matmul(bank[5][:, c:c + HD + 1], p2[h % 2][0:NK, t * P:(t + 1) * P],
                                             vsm[0:NK, h, :], start=True, stop=True)
                        last.then_inc(s_pv[1], 1)

                    def full_scores(n):
                        h, t = n // NT, n % NT
                        if n >= RN:
                            pe.wait_ge(s_bn, n - RN + 1)
                        elif RING[n] is bank[6]:
                            pe.wait_ge(s_cat, 2)
                        pe.matmul(RING[n % RN][:, :], qst[1][0:B_SC, h, t * P:(t + 1) * P],
                                  kst[1][0:B_SC, h, :], start=True, stop=True).then_inc(s_bs, 1)

                    def transpose_out(k, ps):
                        pe.wait_ge(s_o[k], 2 if k else H // HPQ)
                        for t in range(NT):
                            last = pe.transpose(ps[:, t * P:(t + 1) * P], o[k][:, t, :], identf[:, :])
                        last.then_inc(s_ot[k], 1)

                    def project_out(k, w, ps):
                        pe.wait_ge(s_oe[k], 1)
                        for t in range(NT):
                            last = pe.matmul(ps[:, t * P:(t + 1) * P], oT[k][:, t * P:(t + 1) * P], w,
                                             start=True, stop=True)
                        last.then_inc(s_op[k], 1)

                    def gate(k, c, ps):
                        if c:
                            pe.wait_ge(s_gc[k], c)
                        else:
                            pe.wait_ge(s_xe[2 * k + 1], 1)
                        pe.matmul(ps[:, :], wgT[:, c, :], xnT[k][:, :], start=True, stop=True).then_inc(s_g[k], 1)

                    def up(k, c, ps):
                        if c:
                            pe.wait_ge(s_hid[k], c)
                        else:
                            pe.wait_ge(s_gc[k], FC)
                        pe.matmul(ps[:, :], wuT[:, c, :], xnT[k][:, :], start=True, stop=True).then_inc(s_g[k], 1)

                    def down(k, ps):
                        pe.wait_ge(s_hid[k], FC)
                        for t in range(NT):
                            for c in range(FC):
                                last = pe.matmul(ps[:, t * P:(t + 1) * P], gated[:, k, c, t * P:(t + 1) * P],
                                                 wdT[:, c, :], start=(c == 0), stop=(c == FC - 1))
                        last.then_inc(s_dn[k], 1)

                    for h in range(H):
                        if a:
                            causal_scores(h)
                        if not m:
                            continue
                        if h == 0:
                            ln(2, bank[6])
                        if h == 1:
                            pe.wait_ge(s_xe[2], 1)
                            channels_by(wqb[:, 0, :], 1, 2, bank[6])
                            pe.wait_ge(s_qf[1], 1)
                            channels_by(wqb[:, 1, :], 1, 2, bank[6])
                        if h == 2:
                            pe.wait_ge(s_qf[1], 2)
                            tokens_by(wqb[:, 1, :], 1, 2, bank[6])
                            pe.wait_ge(s_vt[1], 1)
                            tokens_by(wqb[:, 2, :], 1, 2, bank[6])
                        if h in (9, 11):
                            c = (h - 9) // 2
                            if c:
                                pe.wait_ge(s_ew, 1)
                            else:
                                pe.wait_ge(s_vt[1], 2)
                                pe.wait_ge(s_nrm, 1)
                            for t in range(NT):
                                last = pe.transpose(bank[6][0:H, t * P:(t + 1) * P], nrm[:, c, t, :], identf[:, :])
                            last.then_inc(s_nt, 1)
                        if h == 13:
                            pe.wait_ge(s_ew, 2)
                            pe.wait_ge(s_wn, 2)
                            for c in range(2):
                                for t in range(NT):
                                    at = (c * NT + t) * H
                                    last = pe.matmul(bank[6][:, at:at + H], ew[:, c, t * P:(t + 1) * P],
                                                     identf[0:H, 0:H], start=True, stop=True)
                            last.then_inc(s_wt, 1)
                        if h == 15:
                            pe.wait_ge(s_wte, 1)
                            pe.wait_ge(s_kw, 1)
                            pe.wait_ge(s_wrep, 1)
                            for t in range(NT):
                                own_g = group[:, t, t * GPT:(t + 1) * GPT]
                                pe.matmul(bank[6][:, t * GPT:(t + 1) * GPT], kw[:, 0, t, :], own_g, start=True,
                                          stop=True)
                                pe.matmul(bank[6][:, L + t * GPT:L + (t + 1) * GPT], wrep[:, t, :], own_g,
                                          start=True, stop=True)
                            for t in range(NT):
                                pe.matmul(bank[6][0:L, 2 * P:3 * P], group[:, t, :], kw[:, 1, t, :], start=(t == 0),
                                          stop=(t == NT - 1))
                            for t in range(NT):
                                last = pe.matmul(bank[6][0:L, 3 * P:3 * P + H], group[:, t, :], wt[:, 1, t, :],
                                                 start=(t == 0), stop=(t == NT - 1))
                            last.then_inc(s_cmp, 1)
                    if m:
                        pe.wait_ge(s_stack[1], 2 * NPAIR * DMA)
                        for n in range(LEAD):
                            full_scores(n)
                    for n in range(NMAIN):
                        if m and n + LEAD < NMAIN:
                            full_scores(n + LEAD)
                        if a and n == 0:
                            pe.wait_ge(s_m1[0], 3 * H)
                            transpose_max(0)
                        if s:
                            for h in s1_heads(n):
                                if h >= 2:
                                    pe.wait_ge(s_m1[1], h - 1)
                                else:
                                    pe.wait_ge(s_kc, NPAIR * DMA)
                                    pe.wait_ge(s_qsm, NPAIR * DMA)
                                    if a:
                                        pe.wait_ge(s_m1[0], 3 * H)
                                for t in range(NT):
                                    last = pe.matmul(bank[3 + h % 2][:, t * NK:(t + 1) * NK],
                                                     qsm[0:B_SC, h, t * P:(t + 1) * P], kcst[0:B_SC, h, :],
                                                     start=True, stop=True)
                                last.then_inc(s_s1[1], 1)
                            if n == 9:
                                pe.wait_ge(s_m1[1], H)
                                if a:
                                    pe.wait_ge(s_ma[0], 1)
                                transpose_max(1)
                        if a:
                            if n == A2_AT:
                                pe.wait_ge(s_mrow[0], DMA)
                            for u in a2_tiles(n):
                                causal_minus_max(u)
                                if u % 3 == 2 and u > 2:
                                    weigh(u // 3 - 1)
                            if n == A2_END:
                                weigh(H - 1)
                            if n in TURN_AT:
                                turn(TURN_AT.index(n))
                        if s:
                            if n == S2_AT:
                                pe.wait_ge(s_mrow[1], DMA)
                                if a:
                                    pe.wait_ge(s_p[0], 3 * H)
                            for h in s2_heads(n):
                                if h >= 2:
                                    pe.wait_ge(s_p[1], h - 1)
                                pe.matmul(bank[3 + h % 2][0:NK, :], kcst[0:B_MX, h, :], qsm[0:B_MX, h, :],
                                          start=True, stop=True).then_inc(s_s2[1], 1)
                                if h:
                                    weigh_hh(h - 1)
                            if n == S2_AT + H // 2 - 1:
                                weigh_hh(H - 1)
                        if a:
                            if n == 42:
                                if s:
                                    pe.wait_ge(s_ma[1], 1)
                                else:
                                    pe.wait_ge(s_ma[0], 1)
                                transpose_out(0, bank[7])
                            if n == 43:
                                project_out(0, woutT[:, :], bank[7])
                            if n == 47:
                                pe.wait_ge(s_xr[1], 1)
                                ln(1, bank[7])
                            if 48 <= n < 48 + FC:
                                gate(0, n - 48, bank[7])
                            if 51 <= n < 51 + FC:
                                up(0, n - 51, bank[7])
                            if n == 54:
                                down(0, bank[7])
                        if s:
                            if n == 51:
                                transpose_out(1, bank[3])
                            if n == 52:
                                project_out(1, wqb[:, 3, :], bank[3])
                            if n == 56:
                                pe.wait_ge(s_xr[3], 1)
                                ln(3, bank[3])
                            if 57 <= n < 57 + FC:
                                gate(1, n - 57, bank[3])
                            if 60 <= n < 60 + FC:
                                up(1, n - 60, bank[3])
                        if p:
                            if n == 57:
                                if a:
                                    pe.wait_ge(s_xr[2], 1)
                                ln(0, bank[7])
                            if n == 58:
                                pe.wait_ge(s_xe[0], 1)
                                channels_by(wqkvT[:, 0:P], 0, 0, bank[7])
                            if n == 59:
                                pe.wait_ge(s_qf[0], 1)
                                channels_by(wqkvT[:, P:2 * P], 0, 0, bank[7])
                            if n == 60:
                                pe.wait_ge(s_qf[0], 2)
                                tokens_by(wqkvT[:, 2 * P:3 * P], 0, 0, bank[7])
                    if s:
                        down(1, bank[3])
                    if m:
                        pe.wait_ge(s_bn, NMAIN)
                        pe.wait_ge(s_bi, NMAIN + 1)
                        for t in range(NT):
                            last = pe.matmul(bank[0][:, t:t + 1], psum[:, t * P:(t + 1) * P], onesf[:, 0:1],
                                             start=True, stop=True)
                        last.then_inc(s_ic, 1)
                        pe.wait_ge(s_dg, 1)
                        for t in range(NT):
                            last = pe.matmul(bank[6][:, t * P:(t + 1) * P], onesf[:, :], diag[:, t, :], start=True,
                                             stop=True)
                        last.then_inc(s_rb, 1)
                        pe.wait_ge(s_sel, 1)
                        for t in range(NT):
                            pe.matmul(bank[6][:, 0:HH], ktok[:, 0, t, :], sel[:, t, :], start=(t == 0),
                                      stop=(t == NT - 1))
                        for t in range(NT):
                            last = pe.matmul(bank[6][L:NK, P:2 * P], sel[:, t, :], ktok[:, 1, t, :], start=(t == 0),
                                             stop=(t == NT - 1))
                        last.then_inc(s_gat, 1)
            nc.sync.sem_clear(range(s_xin.num, s_kc.num + 1))
            nc.all_engine_barrier()

        one_pass(-1, False, True, False, False)
        one_pass(0, True, True, False, False)
        one_pass(1, True, True, True, False)
        with nc.Fori(2, B - 1) as batch:
            one_pass(batch, True, True, True, True)
        one_pass(B - 1, True, False, True, True)
        one_pass(B, False, False, True, True)
        one_pass(B + 1, False, False, False, True)


_INS = ['L0_attn_a_x', 'L0_attn_a_w_qkv', 'L0_attn_a_b_qkv', 'L0_attn_a_w_out', 'L0_attn_a_b_out',
        'L0_attn_b_Wq', 'L0_attn_b_Wk', 'L0_attn_b_Wv', 'L0_attn_b_Wo',
        'L0_ffn_w_gate', 'L0_ffn_w_up', 'L0_ffn_w_down']
_OUTS = [((8, 512, 128), 'float32')]


def kernel(**inputs):
    import numpy as _np
    import concourse.bacc as _bacc
    from concourse import mybir as _mybir
    from concourse.bass_utils import run_bass_kernel_spmd as _run

    nc = _bacc.Bacc("TRN2", target_bir_lowering=False, num_devices=1)
    arrays, args = {}, []
    for name in _INS:
        a = _np.ascontiguousarray(inputs[name])
        arrays[f"in_{name}_dram"] = a
        args.append(nc.dram_tensor(f"in_{name}_dram", a.shape, _mybir.dt.from_np(a.dtype), kind="ExternalInput").ap())
    for i, (shape, dtype) in enumerate(_OUTS):
        dt = _mybir.dt.from_np(_np.dtype(dtype))
        args.append(nc.dram_tensor(f"out_{i}_dram", shape, dt, kind="ExternalOutput").ap())
    hybrid_block(nc, *args)
    r = _run(nc, [arrays], core_ids=[0])
    got = tuple(r.results[0][f"out_{i}_dram"] for i in range(len(_OUTS)))
    return got[0]
```

```python
import math
from contextlib import ExitStack

import concourse.bass as bass
from concourse import mybir

ALU = mybir.AluOpType
ACT = mybir.ActivationFunctionType
F32 = mybir.dt.float32
BF16 = mybir.dt.bfloat16
I32 = mybir.dt.int32
AX_X = mybir.AxisListType.X

P = 128
EPS = 1e-5
NEG = -1e30
QSCALE = 8.0 ** -0.5
CLIP = 1e-8
LOG_CLIP = math.log(CLIP)
DMA = 16


def hybrid_block(nc, x, w_qkv, b_qkv, w_out, b_out, wq_b, wk_b, wv_b, wo_b, w_gate, w_up, w_down, out):
    B, T, D = x.shape
    H, HD = 16, D // 16
    NT = T // P
    FC = w_gate.shape[0] // P
    RATIO = min(8, max(1, T // 64))
    L = T // RATIO
    GPT = P // RATIO
    HH = min(128, int(T * 0.1))
    NK = L + HH
    assert D == P and T == 512 and NK <= P

    Q_PART = (0, 0, 1, 1, 0, 2)
    K_PART = (0, 1, 0, 1, 2, 0)
    NPAIR = len(Q_PART)
    AL = 4
    A_SC = AL + NPAIR * HD
    A_MX = A_SC + 3
    B_SC = NPAIR * HD
    B_MX = B_SC + 3
    TILES = (((0, 0),), ((1, 0), (3, T - P)), ((2, 0),))
    WIDTH = (T, T, T - 2 * P)

    with ExitStack() as ctx:
        def sb(name, shape, dt=F32):
            return ctx.enter_context(nc.sbuf_tensor(name, shape, dt))

        def sem(name):
            return ctx.enter_context(nc.semaphore(name))

        bank = [ctx.enter_context(nc.psum_tensor(f"bank{i}", [P, 512], F32)) for i in range(8)]

        identf = sb("identf", [P, P])
        identb = sb("identb", [P, P], BF16)
        onesf = sb("onesf", [P, P])
        maskqk = sb("maskqk", [P, P], BF16)
        maskkq = sb("maskkq", [P, P], BF16)
        tri = sb("tri", [P, P])
        iota_i = sb("iota_i", [P, HH], I32)
        iota_f = sb("iota_f", [P, HH])
        group = sb("group", [P, NT, L])
        neghalf = sb("neghalf", [P, NT])
        eps = sb("eps", [P, NT])
        setup = sb("setup", [P, 8 * T])
        wload = setup[:, 0:4 * P].rearrange("p (i d) -> p i d", i=4)
        wfp = setup[:, 4 * P:4 * P + 9 * P].rearrange("p (i d) -> p i d", i=3)
        wint = setup[:, 13 * P:22 * P].bitcast(I32).rearrange("p (i d) -> p i d", i=3)
        wqkvT = sb("wqkvT", [P, 3 * P])
        woutT = sb("woutT", [P, P])
        wqb = sb("wqb", [P, 4, P])
        wgT = sb("wgT", [P, FC, P])
        wuT = sb("wuT", [P, FC, P])
        wdT = sb("wdT", [P, FC, P])
        bqk = sb("bqk", [P, 2])
        bqs = sb("bqs", [P, 1])
        bv = sb("bv", [P, P])
        bo = sb("bo", [P, P])

        xs = [sb(f"x{u}", [P, NT, P]) for u in range(5)]
        xbo = sb("xbo", [P, NT, P])
        x2s = sb("x2s", [P, NT, P])
        st = [sb(f"st{u}", [P, NT, 6]) for u in range(4)]
        mv = [sb(f"mv{u}", [P, NT, 2]) for u in range(4)]
        ve = [sb(f"ve{u}", [P, NT]) for u in range(4)]
        rstd = [sb(f"rstd{u}", [P, NT]) for u in range(4)]
        xn = [sb(f"xn{s}", [P, NT, P]) for s in range(2)]
        xnT = [sb(f"xnT{s}", [P, T]) for s in range(3)]
        XN = (2, 0, 1, 1)
        qf = [sb("qf", [P, 2, T])] * 2
        rest = [sb("rest", [P, 2, T])] * 2
        part = [sb("part", [P, 2, 3, T], BF16)] * 2
        q_stacks = sb("q_stacks", [P, H, T], BF16)
        k_stacks = sb("k_stacks", [P, H, T], BF16)
        qst = [q_stacks[64 * s:64 * s + 64, :, :] for s in range(2)]
        kst = [k_stacks[64 * s:64 * s + 64, :, :] for s in range(2)]
        nm = [sb(f"nm{s}", [P, NT, H]) for s in range(2)]
        qsm = sb("qsm", [64, H, T], BF16)
        nmf = [sb(f"nmf{s}", [H, T]) for s in range(2)]
        nmr = [sb(f"nmr{s}", [H, T]) for s in range(2)]
        nmp = [sb(f"nmp{s}", [H, 3, T], BF16) for s in range(2)]
        vA = sb("vA", [P, NT, H, HD + 1])
        pT = [sb(f"pT{i}", [P, sum(WIDTH)]) for i in range(2)]
        ov = sb("ov", [P, T])
        rzo = [sb(f"rzo{s}", [P, NT, 4]) for s in range(2)]
        o = [sb(f"o{s}", [P, NT, P]) for s in range(2)]
        oT = [sb(f"oT{s}", [P, T]) for s in range(2)]
        gated = sb("gated", [P, 2, FC, T])
        alibi_i = gated[0:1, :, :, :].rearrange("p a c t -> p (a c t)")[:, 0:AL * T].bitcast(I32).rearrange(
            "p (a t) -> p a t", a=AL)
        ktok = sb("ktok", [P, 2, NT, P])
        n2 = sb("n2", [P, 2, NT, H])
        nroot = sb("nroot", [P, 2, NT, H])
        nrec = sb("nrec", [P, 2, NT, H])
        nquot = sb("nquot", [P, 2, NT, H])
        nrm = sb("nrm", [P, 2, NT, H])
        nnm = sb("nnm", [H, 2])
        ew = sb("ew", [H, 2, T])
        zw = sb("zw", [H, 2])
        rzw = sb("rzw", [H, 2])
        wt = sb("wt", [P, 2, NT, H])
        kw = sb("kw", [P, 2, NT, P])
        ncl = sb("ncl", [P, 2, NT, H])
        nln = sb("nln", [P, 2, NT, H])
        wrep = sb("wrep", [P, NT, P])
        den = sb("den", [P, L])
        rden = sb("rden", [P, L])
        vden = sb("vden", [L, H])
        vrden = sb("vrden", [L, H])
        NE = 8
        E = setup[:, :].rearrange("p (n t) -> p n t", n=NE)
        alibi = sb("alibi", [1, AL + 1, T], BF16)
        junk = sb("junk", [P, T])
        nmB = sb("nmB", [P, H, NT])
        Z = sb("Z", [P, H, NT])
        lnZ = sb("lnZ", [P, H, NT])
        thr = sb("thr", [P, H, NT])
        acc = sb("acc", [P, H, NT])
        rz = sb("rz", [P, H, NT])
        t1 = sb("t1", [P, H, NT])
        t2 = sb("t2", [P, H, NT])
        t3 = sb("t3", [P, H, NT])
        own = sb("own", [P, NT])
        psum = sb("psum", [P, T])
        imp = sb("imp", [P, NT])
        cnt = sb("cnt", [P, 3, NT])
        rank = sb("rank", [P, NT])
        rank2 = sb("rank2", [P, NT])
        sel = sb("sel", [P, NT, HH])
        kcat = sb("kcat", [P, NK])
        krest = sb("krest", [P, NK])
        kcp = sb("kcp", [P, 3, NK], BF16)
        kcst = sb("kcst", [64, H, NK], BF16)
        vcat = sb("vcat", [P, H, HD])
        vsm = sb("vsm", [P, H, HD + 1])
        p2 = [sb(f"p2_{i}", [P, T]) for i in range(2)]

        part_dram = [nc.dram_tensor(f"part_dram{s}", [B, P, 2, 3, T], BF16, kind="Internal").ap() for s in range(2)]
        x2_dram = nc.dram_tensor("x2_dram", [B, T, D], F32, kind="Internal").ap()
        nm_dram = [nc.dram_tensor(f"nm_dram{s}", [H, 3, T], BF16, kind="Internal").ap() for s in range(2)]
        kcp_dram = nc.dram_tensor("kcp_dram", [P, 3, NK], BF16, kind="Internal").ap()

        s_w = sem("weights_loaded")
        s_const = sem("pool_constants_made")
        s_wfp = sem("weights_scaled")
        s_wtr = sem("weights_transposed")
        s_wev = sem("weights_in_sbuf")
        s_cdve = sem("dve_constants_made")
        s_rows = sem("constant_rows_in_stacks")
        s_xin = sem("x_loaded")
        s_out = sem("out_stored")
        s_x2st = sem("x2_stored")
        s_x2ld = sem("x2_loaded")
        s_qsm = sem("small_query_stack_loaded")
        s_vs = sem("small_values_in_place")
        s_gc = [sem(f"gates_in_sbuf{s}") for s in range(2)]
        s_xr = [None] + [sem(f"x{u}_ready") for u in range(1, 5)]
        s_xbo = sem("x_plus_bias_ready")
        s_st = [sem(f"ln_stats{u}") for u in range(4)]
        s_mv = [sem(f"ln_moments{u}") for u in range(4)]
        s_ve = [sem(f"ln_var_eps{u}") for u in range(4)]
        s_rs = [sem(f"ln_rstd{u}") for u in range(4)]
        s_xn = [sem(f"ln_normed{u}") for u in range(4)]
        s_xt = [sem(f"ln_transposed{u}") for u in range(4)]
        s_xe = [sem(f"ln_evacuated{u}") for u in range(4)]
        s_proj = [sem(f"projected{s}") for s in range(2)]
        s_qf = [sem(f"qk_evacuated{s}") for s in range(2)]
        s_vt = [sem(f"v_evacuated{s}") for s in range(2)]
        s_hi = [sem(f"high_and_mid_parts{s}") for s in range(2)]
        s_rest = [sem(f"rests_and_low_parts{s}") for s in range(2)]
        s_stack = [sem(f"stacks_loaded{s}") for s in range(2)]
        s_s1 = [sem(f"scores_for_max{s}") for s in range(2)]
        s_pd = [sem(f"parts_in_dram{s}") for s in range(2)]
        s_nd = [sem(f"maxima_in_dram{s}") for s in range(2)]
        s_kd = sem("key_parts_in_dram")
        s_m1 = [sem(f"maxima{s}") for s in range(2)]
        s_mt = [sem(f"maxima_transposed{s}") for s in range(2)]
        s_ma = [sem(f"maxima_act_steps{s}") for s in range(2)]
        s_mp = [sem(f"maxima_pool_steps{s}") for s in range(2)]
        s_mrow = [sem(f"maxima_rows_loaded{s}") for s in range(2)]
        s_s2 = [sem(f"scores_minus_max{s}") for s in range(2)]
        s_p = [sem(f"probabilities{s}") for s in range(2)]
        s_pv = [sem(f"heads_weighted{s}") for s in range(2)]
        s_rzo = [sem(f"sums_inverted{s}") for s in range(2)]
        s_o = [sem(f"heads_normalised{s}") for s in range(2)]
        s_ot = [sem(f"o_transposed{s}") for s in range(2)]
        s_oe = [sem(f"oT_evacuated{s}") for s in range(2)]
        s_op = [sem(f"o_projected{s}") for s in range(2)]
        s_g = [sem(f"gate_up_products{s}") for s in range(2)]
        s_sil = [sem(f"silu_done{s}") for s in range(2)]
        s_hid = [sem(f"hidden_done{s}") for s in range(2)]
        s_dn = [sem(f"down_product{s}") for s in range(2)]
        s_sq = sem("squares")
        s_n2 = sem("squared_norms")
        s_nrm = sem("norms")
        s_root = sem("norm_roots_begun")
        s_newton = sem("norm_newton_steps")
        s_nt = sem("norms_transposed")
        s_nnm = sem("norm_maxima")
        s_ew = sem("norm_exponentials")
        s_rzw = sem("norm_sums_inverted")
        s_wn = sem("token_weights")
        s_wt = sem("token_weights_transposed")
        s_wte = sem("token_weights_in_sbuf")
        s_kw = sem("weighted_tokens")
        s_wrep = sem("weights_repeated")
        s_sc = sem("probabilities_in_place")
        s_scv = sem("probabilities_in_place_by_vector_engine")
        s_ov = [sem(f"four_heads_out_of_psum{s}") for s in range(2)]
        s_tv = [sem(f"four_heads_transposed{s}") for s in range(2)]
        s_last = sem("last_head_summed")
        s_ic = sem("influence_columns_summed")
        s_cmp = sem("compressed_sums")
        s_den = sem("compressed_denominators")
        s_rden = sem("compressed_denominators_inverted")
        s_cat = sem("compressed_in_place")
        s_bs = sem("full_scores")
        s_bm = sem("full_maxima")
        s_be = sem("full_exponentials")
        s_bz = sem("full_log_sums")
        s_bt = sem("clip_thresholds")
        s_bn = sem("entropy_sums")
        s_brz = sem("full_sums_inverted")
        s_bi = sem("influences")
        s_imp = sem("importance_steps")
        s_dg = sem("importance_diagonals")
        s_rb = sem("importance_rows")
        s_cnt = sem("ranks_counted")
        s_sel = sem("selection_made")
        s_gat = sem("heavy_hitters_gathered")
        s_hhe = sem("heavy_hitters_in_place")
        s_ka = sem("key_parts_act")
        s_kp = sem("key_parts_pool")
        s_kc = sem("key_stack_loaded")


        PT_AT = {0: 0, 1: T, 3: T + T - P, 2: 2 * T}

        def stack_rows(st_, j, base):
            return st_[base + j * HD:base + (j + 1) * HD, :, :]

        with nc.Block() as block:
            @block.sync
            def _(sp):
                for c in range(3):
                    sp.dma_start(wload[:, c, :], w_qkv[c * P:(c + 1) * P, :]).then_inc(s_w, DMA)
                sp.dma_start(wload[:, 3, :], w_out).then_inc(s_w, DMA)
                for i, w in enumerate((wq_b, wk_b, wv_b, wo_b)):
                    sp.dma_start(wqb[:, i, :], w).then_inc(s_w, DMA)
                sp.dma_start(wint[:, 0, :].rearrange("p (c d) -> p c d", c=FC),
                             w_gate.rearrange("(c p) d -> p c d", p=P)).then_inc(s_w, DMA)
                sp.dma_start(wint[:, 1, :].rearrange("p (c d) -> p c d", c=FC),
                             w_up.rearrange("(c p) d -> p c d", p=P)).then_inc(s_w, DMA)
                sp.dma_start(wint[:, 2, :], w_down).then_inc(s_w, DMA)
                sp.dma_start(bqk[:, :], b_qkv[0:2 * P].rearrange("(c p) -> p c", p=P),
                             allow_slow_non_contiguous=True).then_inc(s_w, DMA)
                sp.dma_start(bv[:, :], b_qkv[2 * P:3 * P].rearrange("(a n) -> a n", a=1).broadcast_to([P, P])
                             ).then_inc(s_w, DMA)
                sp.dma_start(bo[:, :], b_out.rearrange("(a n) -> a n", a=1).broadcast_to([P, P])).then_inc(s_w, DMA)
                sp.wait_ge(s_cdve, 2)
                ones_row = alibi[:, AL:AL + 1, :].broadcast_to([1, H, T])
                q_rows = (alibi[:, 0:1, :], alibi[:, AL:AL + 1, :], alibi[:, 1:2, :], alibi[:, AL:AL + 1, :])
                k_rows = (alibi[:, AL:AL + 1, :], alibi[:, 2:3, :], alibi[:, AL:AL + 1, :], alibi[:, 3:4, :])
                for r in range(AL):
                    sp.dma_start(qst[0][r:r + 1, :, :], q_rows[r].broadcast_to([1, H, T])).then_inc(s_rows, DMA)
                    sp.dma_start(kst[0][r:r + 1, :, :], k_rows[r].broadcast_to([1, H, T])).then_inc(s_rows, DMA)
                for r in range(3):
                    sp.dma_start(kst[0][A_SC + r:A_SC + r + 1, :, :], ones_row).then_inc(s_rows, DMA)
                    sp.dma_start(kcst[B_SC + r:B_SC + r + 1, :, :],
                                 alibi[:, AL:AL + 1, 0:NK].broadcast_to([1, H, NK])).then_inc(s_rows, DMA)
                sp.wait_ge(s_rows, (2 * AL + 6) * DMA)


            @block.gpsimd
            def _(pool):
                pool.memset(identf[:, :], 0.0)
                pool.memset(identb[:, :], 0.0)
                pool.memset(onesf[:, :], 1.0)
                pool.memset(maskqk[:, :], 0.0)
                pool.memset(maskkq[:, :], 0.0)
                pool.memset(tri[:, :], 1.0)
                pool.memset(neghalf[:, :], -0.5)
                pool.memset(eps[:, :], EPS)
                pool.memset(vA[:, :, :, :], 1.0)
                pool.memset(vsm[:, :, :], 1.0)
                pool.memset(alibi[:, AL:AL + 1, :], 1.0)
                pool.memset(group[:, :, :], 1.0).then_inc(s_const, 1)
                pool.wait_ge(s_const, 1)
                pool.affine_select(out=identf[:, :], in_=identf[:, :], compare_op=ALU.not_equal, fill=1.0, base=0,
                                   pattern=[[-1, P]], channel_multiplier=1)
                pool.affine_select(out=identb[:, :], in_=identb[:, :], compare_op=ALU.not_equal, fill=1.0, base=0,
                                   pattern=[[-1, P]], channel_multiplier=1)
                pool.affine_select(out=maskqk[:, :], in_=maskqk[:, :], compare_op=ALU.is_ge, fill=NEG, base=0,
                                   pattern=[[-1, P]], channel_multiplier=1)
                pool.affine_select(out=maskkq[:, :], in_=maskkq[:, :], compare_op=ALU.is_ge, fill=NEG, base=0,
                                   pattern=[[1, P]], channel_multiplier=-1)
                pool.affine_select(out=tri[:, :], in_=tri[:, :], compare_op=ALU.is_gt, fill=0.0, base=0,
                                   pattern=[[-1, P]], channel_multiplier=1)
                pool.affine_select(out=group[:, :, :], in_=group[:, :, :], compare_op=ALU.is_ge, fill=0.0, base=0,
                                   pattern=[[P, NT], [-RATIO, L]], channel_multiplier=1).then_inc(s_const, 1)
                pool.wait_ge(s_const, 2)
                pool.affine_select(out=group[:, :, :], in_=group[:, :, :], compare_op=ALU.is_ge, fill=0.0,
                                   base=RATIO - 1, pattern=[[-P, NT], [RATIO, L]], channel_multiplier=-1)
                pool.iota(iota_i[:, :], pattern=[[1, HH]], base=0, channel_multiplier=0)
                pool.iota(alibi_i[:, 0, :], pattern=[[-256, T // 256], [0, 256]], base=0, channel_multiplier=0)
                pool.iota(alibi_i[:, 1, :], pattern=[[0, T // 256], [-1, 256]], base=0, channel_multiplier=0)
                pool.iota(alibi_i[:, 2, :], pattern=[[256, T // 256], [0, 256]], base=0, channel_multiplier=0)
                pool.iota(alibi_i[:, 3, :], pattern=[[0, T // 256], [1, 256]], base=0, channel_multiplier=0
                          ).then_inc(s_const, 1)


            @block.scalar
            def _(act):
                act.preload_act_table_set("natural_log_exp_and_others")
                for n, dst in enumerate((wqkvT[:, 0:P], wqkvT[:, P:2 * P], wqkvT[:, 2 * P:3 * P], woutT[:, :])):
                    act.wait_ge(s_wtr, n + 1)
                    act.activation(dst, bank[n][:, 0:P], ACT.Copy).then_inc(s_wev, 1)
                for i, w in enumerate((wgT, wuT, wdT)):
                    for c in range(FC):
                        n = 4 + i * FC + c
                        act.wait_ge(s_wtr, n + 1)
                        act.activation(w[:, c, :], bank[n % 8][:, 0:P], ACT.Copy).then_inc(s_wev, 1)


            @block.vector
            def _(dve):
                dve.wait_ge(s_const, 3)
                dve.tensor_copy(iota_f[:, :], iota_i[:, :]).then_inc(s_cdve, 1)
                dve.tensor_copy(alibi[:, 0:AL, :], alibi_i[:, :, :]).then_inc(s_cdve, 1)
                dve.wait_ge(s_w, 14 * DMA)
                dve.memset(bank[5][:, :], 0.0)
                dve.tensor_scalar(bqs[:, :], bqk[:, 0:1], QSCALE, None, ALU.mult).then_inc(s_cdve, 1)
                dve.tensor_scalar(wfp[:, :, :], wint[:, :, :], 1.0 / 127.0, None, ALU.mult).then_inc(s_wfp, 1)


            @block.tensor
            def _(pe):
                pe.wait_ge(s_const, 3)
                pe.wait_ge(s_w, 14 * DMA)
                for n in range(4):
                    pe.transpose(bank[n][:, 0:P], wload[:, n, :], identf[:, :]).then_inc(s_wtr, 1)
                pe.wait_ge(s_wfp, 1)
                for i in range(3):
                    for c in range(FC):
                        n = 4 + i * FC + c
                        if n >= 8:
                            pe.wait_ge(s_wev, n - 7)
                        pe.transpose(bank[n % 8][:, 0:P], wfp[:, i, c * P:(c + 1) * P], identf[:, :]).then_inc(s_wtr, 1)
                pe.wait_ge(s_wev, 4 + 3 * FC)



        RING = (bank[0], bank[1], bank[2], bank[6])
        RN = len(RING)
        QROWS = 32
        HPQ = P // QROWS
        NMAIN = NT * H
        INFL_LAG = 6
        LEAD = 1
        A1_PRE = H // 2
        S2_AT = A1_PRE
        A2_AT = S2_AT + 12
        A2_END = A2_AT + 29
        LEAVE_AT = (tuple(min(A2_AT + 3 * (3 * HPQ * (g + 1) + 2) // 5, A2_END) for g in range(H // HPQ)),
                    tuple(S2_AT + 3 * g + 3 for g in range(H // HPQ)))
        TURN_AT = ((32, 39, 47, 51), tuple(n + 2 for n in LEAVE_AT[1]))
        DIVIDE_AT = (tuple(n + 1 for n in TURN_AT[0]), tuple(n + 1 for n in TURN_AT[1]))
        S_TAIL = DIVIDE_AT[1][-1] + 1
        S_GATE_AT = (34, 37, 41)
        S_UP_AT = (44, 50, 50)
        S_UP_BANK = (bank[7], bank[3], bank[4])
        S_DOWN_AT = 53
        A_TAIL = DIVIDE_AT[0][-1] + 1
        P_TAIL = A_TAIL - 1
        LAST = NMAIN - NT
        ON_ACT = [n for n in range(LAST) if n < 14 or 46 <= n < 56]
        ON_DVE = [n for n in range(LAST) if n not in ON_ACT]
        M_TAIL = NMAIN + 2
        STEPS = NMAIN + 11

        def a1_bank(u):
            return (3, 4, 0, 1, 2)[u % 5] if u < 3 * (A1_PRE - 4) else 3 + u % 2

        def a1_before(u):
            return max([v + 1 for v in range(u) if a1_bank(v) == a1_bank(u)], default=0)

        def a2_tiles(n):
            return [u for u in range(3 * H) if A2_AT + (3 * u) // 5 == n]

        def s1_heads(h):
            return range(4 * (h - 4), 4 * (h - 4) + 4) if 4 <= h < 8 else ()

        def s2_heads(n):
            g, j = (n - S2_AT) // 3, (n - S2_AT) % 3
            return range(4 * g + (0, 1, 3)[j], 4 * g + (1, 3, 4)[j]) if 0 <= g < H // HPQ else ()

        CAUSAL = (((3, 0),), ((0, 0), (2, P)), ((1, 0),))

        def one_pass(i, a, p, m, s):
            with nc.Block() as block:
                @block.sync
                def _(sp):
                    if p:
                        sp.dma_start(xs[0][:, :, :],
                                     x[bass.ds(i + 1, 1), :, :].rearrange("a (t p) d -> p (a t) d", p=P)
                                     ).then_inc(s_xin, DMA)
                    if s:
                        for j, pt in enumerate(Q_PART):
                            sp.dma_start(qsm[j * HD:(j + 1) * HD, :, :],
                                         part_dram[1][bass.ds(i - 2, 1), :, 0, pt, :].rearrange(
                                             "a (h d) t -> (a d) h t", d=HD)).then_inc(s_qsm, DMA)
                        sp.dma_start(x2s[:, :, :],
                                     x2_dram[bass.ds(i - 2, 1), :, :].rearrange("a (t p) d -> p (a t) d", p=P)
                                     ).then_inc(s_x2ld, DMA)
                        sp.wait_ge(s_ka, 2)
                        sp.wait_ge(s_kp, 2)
                        sp.dma_start(kcp_dram, kcp[:, :, :]).then_inc(s_kd, DMA)
                        sp.wait_ge(s_kd, DMA)
                        for j, pt in enumerate(K_PART):
                            sp.dma_start(stack_rows(kcst, j, 0),
                                         kcp_dram[:, pt, :].rearrange("(h d) t -> d h t", d=HD)).then_inc(s_kc, DMA)
                    if m:
                        sp.wait_ge(s_hi[1], 4)
                        sp.wait_ge(s_rest[1], 4)
                        pd = part_dram[1][bass.ds(i - 1, 1), :, :, :, :]
                        sp.dma_start(pd.rearrange("a p i c t -> p (a i) c t"), part[1][:, :, :, :]
                                     ).then_inc(s_pd[1], DMA)
                        sp.wait_ge(s_pd[1], DMA)
                        for k, (stk, parts) in enumerate(((qst[1], Q_PART), (kst[1], K_PART))):
                            for j, pt in enumerate(parts):
                                sp.dma_start(stack_rows(stk, j, 0),
                                             part_dram[1][bass.ds(i - 1, 1), :, k, pt, :].rearrange(
                                                 "a (h d) t -> (a d) h t", d=HD)).then_inc(s_stack[1], DMA)

                    def max_rows(s_, stk, base):
                        sp.wait_ge(s_mp[s_], 2)
                        sp.dma_start(nm_dram[s_], nmp[s_][:, :, :]).then_inc(s_nd[s_], DMA)
                        sp.wait_ge(s_nd[s_], DMA)
                        sp.dma_start(stk[base:base + 3, :, :], nm_dram[s_].rearrange("h r t -> r h t")
                                     ).then_inc(s_mrow[s_], DMA)

                    if s:
                        max_rows(1, qsm, B_SC)
                    if a:
                        max_rows(0, qst[0], A_SC)
                    if s:
                        sp.wait_ge(s_xr[4], 1)
                        sp.dma_start(out[bass.ds(i - 2, 1), :, :].rearrange("a (t p) d -> p (a t) d", p=P),
                                     xs[4][:, :, :]).then_inc(s_out, DMA)
                    if p:
                        sp.wait_ge(s_hi[0], 4)
                        sp.wait_ge(s_rest[0], 4)
                        sp.dma_start(part_dram[0][0], part[0][:, :, :, :]).then_inc(s_pd[0], DMA)
                        sp.wait_ge(s_pd[0], DMA)
                        if a:
                            sp.wait_ge(s_s2[0], 3 * H)
                        for k, (stk, parts) in enumerate(((qst[0], Q_PART), (kst[0], K_PART))):
                            for j, pt in enumerate(parts):
                                sp.dma_start(stack_rows(stk, j, AL),
                                             part_dram[0][0][:, k, pt, :].rearrange("(h d) t -> d h t", d=HD)
                                             ).then_inc(s_stack[0], DMA)
                    if a:
                        sp.wait_ge(s_xr[2], 1)
                        sp.dma_start(x2_dram[bass.ds(i, 1), :, :].rearrange("a (t p) d -> p (a t) d", p=P),
                                     xs[2][:, :, :]).then_inc(s_x2st, DMA)
                    if s:
                        sp.wait_ge(s_out, DMA)
                    if a:
                        sp.wait_ge(s_x2st, DMA)
                    if p:
                        sp.wait_ge(s_stack[0], 2 * NPAIR * DMA)

                @block.gpsimd
                def _(pool):
                    def ln(u):
                        pool.wait_ge(s_mv[u], 1)
                        pool.tensor_tensor(ve[u][:, :], mv[u][:, :, 1], eps[:, :], ALU.add).then_inc(s_ve[u], 1)
                        pool.wait_ge(s_ve[u], 1)
                        pool.tensor_tensor(rstd[u][:, :], ve[u][:, :], neghalf[:, :], ALU.pow).then_inc(s_rs[u], 1)

                    def rest_of(k, c):
                        pool.wait_ge(s_hi[k], c + 1)
                        pool.tensor_tensor(rest[k][:, c, :], qf[k][:, c, :], part[k][:, c, 0, :], ALU.subtract
                                           ).then_inc(s_rest[k], 1)

                    def lows(k):
                        for c in range(2):
                            pool.wait_ge(s_hi[k], 3 + c)
                            pool.tensor_tensor(part[k][:, c, 2, :], rest[k][:, c, :], part[k][:, c, 1, :],
                                               ALU.subtract).then_inc(s_rest[k], 1)

                    def max_rest(k):
                        pool.wait_ge(s_ma[k], 2)
                        pool.tensor_tensor(nmr[k][:, :], nmf[k][:, :], nmp[k][:, 0, :], ALU.subtract
                                           ).then_inc(s_mp[k], 1)

                    def max_low(k):
                        pool.wait_ge(s_ma[k], 3)
                        pool.tensor_tensor(nmp[k][:, 2, :], nmr[k][:, :], nmp[k][:, 1, :], ALU.subtract
                                           ).then_inc(s_mp[k], 1)

                    def influence(n):
                        if n in ON_ACT:
                            pool.wait_ge(s_sc, ON_ACT.index(n) + 1)
                        else:
                            pool.wait_ge(s_scv, ON_DVE.index(n) + 1)
                        pool.wait_ge(s_bi, n + 1)
                        pool.tensor_tensor(psum[:, :], psum[:, :], E[:, n % NE, :], ALU.add).then_inc(s_bi, 1)

                    if m:
                        pool.memset(psum[:, :], 0.0).then_inc(s_bi, 1)
                    if s:
                        pool.wait_ge(s_ka, 1)
                        pool.tensor_tensor(krest[:, :], kcat[:, :], kcp[:, 0, :], ALU.subtract).then_inc(s_kp, 1)
                        pool.wait_ge(s_ka, 2)
                        pool.tensor_tensor(kcp[:, 2, :], krest[:, :], kcp[:, 1, :], ALU.subtract).then_inc(s_kp, 1)
                    if m:
                        ln(2)
                        rest_of(1, 0)
                        rest_of(1, 1)
                        lows(1)
                        for c in range(2):
                            pool.wait_ge(s_vt[1], c + 1)
                            pool.tensor_tensor(kw[:, c, :, :], ktok[:, c, :, :], ktok[:, c, :, :], ALU.mult
                                               ).then_inc(s_sq, 1)
                    for n in range(STEPS):
                        if m and n < NMAIN:
                            h, t = n // NT, n % NT
                            pool.wait_ge(s_bz, n + 1)
                            pool.tensor_tensor(thr[:, h, t:t + 1], lnZ[:, h, t:t + 1], nmB[:, h, t:t + 1],
                                               ALU.subtract).then_inc(s_bt, 1)
                        if s and n == 1:
                            max_rest(1)
                        if s and n == 2:
                            max_low(1)
                        if a and n == S2_AT + 1:
                            max_rest(0)
                        if a and n == S2_AT + 2:
                            max_low(0)
                        if s and n == S_TAIL + 4:
                            ln(3)
                        if a and n == A_TAIL + 4:
                            ln(1)
                        if p and n == A_TAIL + 6:
                            pool.wait_ge(s_xin, DMA)
                            if a:
                                pool.wait_ge(s_xr[1], 1)
                            for t in range(NT):
                                last = pool.tensor_tensor(xbo[:, t, :], xs[0][:, t, :], bo[:, :], ALU.add)
                            last.then_inc(s_xbo, 1)
                        if p and n == P_TAIL - 3:
                            ln(0)
                        if p and n == P_TAIL + 5:
                            rest_of(0, 0)
                        if p and n == P_TAIL + 7:
                            rest_of(0, 1)
                        if p and n == P_TAIL + 8:
                            lows(0)
                        if m and INFL_LAG <= n < INFL_LAG + LAST:
                            influence(n - INFL_LAG)

                @block.scalar
                def _(act):
                    def ln(u, ps):
                        act.wait_ge(s_xt[u], 1)
                        act.activation(xnT[XN[u]][:, :], ps[:, :], ACT.Copy).then_inc(s_xe[u], 1)

                    def qk(k, c, ps):
                        act.wait_ge(s_proj[k], c + 1)
                        if k == 0 and c == 0 and m:
                            act.wait_ge(s_rest[1], 4)
                        if k == 0:
                            act.activation(qf[k][:, c, :], ps[:, :], ACT.Identity,
                                           bias=bqk[:, 1:2] if c else bqs[:, 0:1],
                                           scale=1.0 if c else QSCALE).then_inc(s_qf[k], 1)
                        else:
                            act.activation(qf[k][:, c, :], ps[:, :], ACT.Copy, scale=1.0 if c else QSCALE
                                           ).then_inc(s_qf[k], 1)

                    def high(k, c):
                        act.wait_ge(s_qf[k], c + 1)
                        if k == 0 and c == 0 and m:
                            act.wait_ge(s_pd[1], DMA)
                        act.activation(part[k][:, c, 0, :], qf[k][:, c, :], ACT.Copy).then_inc(s_hi[k], 1)

                    def mid(k, c):
                        act.wait_ge(s_rest[k], c + 1)
                        act.activation(part[k][:, c, 1, :], rest[k][:, c, :], ACT.Copy).then_inc(s_hi[k], 1)

                    def max_high(k):
                        act.wait_ge(s_mt[k], 1)
                        act.activation(nmf[k][:, :], bank[5][0:H, :], ACT.Copy).then_inc(s_ma[k], 1)
                        act.wait_ge(s_ma[k], 1)
                        act.activation(nmp[k][:, 0, :], nmf[k][:, :], ACT.Copy).then_inc(s_ma[k], 1)

                    def max_mid(k):
                        act.wait_ge(s_mp[k], 1)
                        act.activation(nmp[k][:, 1, :], nmr[k][:, :], ACT.Copy).then_inc(s_ma[k], 1)

                    def leave(k, g):
                        act.wait_ge(s_pv[k], HPQ * (g + 1) * (1 if k else 3))
                        if g:
                            act.wait_ge(s_tv[k], g)
                        elif k == 0 and s:
                            act.wait_ge(s_tv[1], H // HPQ)
                        act.activation(ov[:, :], bank[5][:, :], ACT.Copy).then_inc(s_ov[k], 1)

                    def probabilities(n):
                        h, t = n // NT, n % NT
                        act.wait_ge(s_bn, n + 1)
                        act.wait_ge(s_brz, h + 1)
                        act.activation(E[:, n % NE, :], E[:, n % NE, :], ACT.Copy, scale=rz[:, h, t:t + 1]
                                       ).then_inc(s_sc, 1)

                    def out_t(k, ps):
                        act.wait_ge(s_ot[k], 1)
                        act.activation(oT[k][:, :], ps[:, :], ACT.Copy).then_inc(s_oe[k], 1)

                    def gate(k, c, ps):
                        act.wait_ge(s_g[k], c + 1)
                        act.activation(gated[:, k, c, :], ps[:, :], ACT.Copy).then_inc(s_gc[k], 1)

                    def silu(k):
                        act.wait_ge(s_gc[k], FC)
                        act.activation(gated[:, k, :, :], gated[:, k, :, :], ACT.Silu).then_inc(s_sil[k], 1)
                        act.preload_act_table_set("natural_log_exp_and_others")

                    if s:
                        act.activation(kcp[:, 0, :], kcat[:, :], ACT.Copy).then_inc(s_ka, 1)
                        act.activation(vsm[0:NK, :, 0:HD], vcat[0:NK, :, :], ACT.Copy).then_inc(s_vs, 1)
                        act.wait_ge(s_kp, 1)
                        act.activation(kcp[:, 1, :], krest[:, :], ACT.Copy).then_inc(s_ka, 1)
                    if m:
                        ln(2, bank[6])
                        qk(1, 0, bank[6])
                        qk(1, 1, bank[7])
                        high(1, 0)
                        high(1, 1)
                        act.wait_ge(s_proj[1], 3)
                        act.activation(ktok[:, 0, :, :].rearrange("p t d -> p (t d)"), bank[5][:, :], ACT.Copy
                                       ).then_inc(s_vt[1], 1)
                        mid(1, 0)
                        act.wait_ge(s_proj[1], 4)
                        act.activation(ktok[:, 1, :, :].rearrange("p t d -> p (t d)"), bank[6][:, :], ACT.Copy
                                       ).then_inc(s_vt[1], 1)
                        mid(1, 1)
                        act.wait_ge(s_n2, 2)
                        act.activation(nln[:, :, :, :], ncl[:, :, :, :], ACT.Ln).then_inc(s_root, 1)
                        act.wait_ge(s_root, 1)
                        act.activation(nroot[:, :, :, :], nln[:, :, :, :], ACT.Exp, scale=0.5).then_inc(s_root, 1)
                    for n in range(STEPS):
                        if m and n < NMAIN:
                            h, t = n // NT, n % NT
                            act.wait_ge(s_bm, n + 1)
                            if n >= NE:
                                act.wait_ge(s_bn, n - NE + 1)
                                act.wait_ge(s_bi, n - NE + 2)
                            act.activation(E[:, n % NE, :], RING[n % RN][:, :], ACT.Exp, bias=nmB[:, h, t:t + 1],
                                           accum_out=Z[:, h, t:t + 1]).then_inc(s_be, 1)
                            act.wait_ge(s_be, n + 1)
                            act.activation(lnZ[:, h, t:t + 1], Z[:, h, t:t + 1], ACT.Ln, scale=CLIP
                                           ).then_inc(s_bz, 1)
                            if n - INFL_LAG in ON_ACT:
                                probabilities(n - INFL_LAG)
                        if s:
                            if n == 0:
                                max_high(1)
                            if n == 2:
                                max_mid(1)
                            for h in s2_heads(n):
                                if h >= 2:
                                    act.wait_ge(s_pv[1], h - 1)
                                act.wait_ge(s_s2[1], h + 1)
                                act.activation(p2[h % 2][0:NK, :], bank[3 + h % 2][0:NK, :], ACT.Exp
                                               ).then_inc(s_p[1], 1)
                        if a:
                            if n == S2_AT:
                                max_high(0)
                            if n == S2_AT + 2:
                                max_mid(0)
                            for u in a2_tiles(n):
                                h, c = u // 3, u % 3
                                if h >= 2:
                                    act.wait_ge(s_pv[0], u - 5)
                                act.wait_ge(s_s2[0], u + 1)
                                act.activation(pT[h % 2][:, c * T:c * T + WIDTH[c]], bank[3 + u % 2][:, 0:WIDTH[c]],
                                               ACT.Exp).then_inc(s_p[0], 1)
                        if m:
                            if n in (2, 4):
                                c = (n - 2) // 2
                                act.wait_ge(s_nnm, c + 1)
                                act.activation(ew[:, c, :], bank[7][0:H, :], ACT.Exp, bias=nnm[:, c:c + 1],
                                               accum_out=zw[:, c:c + 1]).then_inc(s_ew, 1)
                            if n in (4, 6):
                                c = (n - 4) // 2
                                act.wait_ge(s_ew, c + 1)
                                act.wait_ge(s_rzw, c + 1)
                                act.activation(ew[:, c, :], ew[:, c, :], ACT.Copy, scale=rzw[:, c:c + 1]
                                               ).then_inc(s_wn, 1)
                            if n == 8:
                                act.wait_ge(s_wt, 1)
                                act.activation(wt[:, :, :, :].rearrange("p i t h -> p (i t h)"),
                                               bank[7][:, 0:2 * NT * H], ACT.Copy).then_inc(s_wte, 1)
                                act.wait_ge(s_wte, 1)
                                act.activation(wrep[:, :, :].rearrange("p t (h d) -> p (t h) d", d=HD),
                                               wt[:, 0, :, :].rearrange("p t (h a) -> p (t h) a", a=1).broadcast_to(
                                                   [P, NT * H, HD]), ACT.Copy).then_inc(s_wrep, 1)
                        if s:
                            if n in LEAVE_AT[1]:
                                leave(1, LEAVE_AT[1].index(n))
                            if n == S_TAIL + 1:
                                out_t(1, bank[7])
                            if n == S_TAIL + 7:
                                ln(3, bank[7])
                            if n - 1 in S_GATE_AT:
                                gate(1, S_GATE_AT.index(n - 1), bank[7])
                            if n == S_GATE_AT[-1] + 2:
                                silu(1)
                        if a:
                            if n in LEAVE_AT[0]:
                                leave(0, LEAVE_AT[0].index(n))
                            if n == A_TAIL + 1:
                                out_t(0, bank[7])
                            if n == A_TAIL + 8:
                                ln(1, bank[7])
                            if n == A_TAIL + 10:
                                for c in range(FC):
                                    gate(0, c, bank[3 + c])
                                silu(0)
                        if p:
                            if n == P_TAIL + 1:
                                ln(0, bank[5])
                            if n == P_TAIL + 3:
                                qk(0, 0, bank[5])
                            if n == P_TAIL + 4:
                                high(0, 0)
                            if n == P_TAIL + 5:
                                qk(0, 1, bank[5])
                                high(0, 1)
                            if n == P_TAIL + 6:
                                mid(0, 0)
                            if n == P_TAIL + 8:
                                mid(0, 1)

                @block.vector
                def _(dve):
                    def stats(u):
                        for t in range(NT):
                            last = dve.bn_stats(st[u][:, t, :], (xs[0], xs[1], xs[2], xs[3])[u][:, t, :])
                        last.then_inc(s_st[u], 1)
                        dve.wait_ge(s_st[u], 1)
                        for t in range(NT):
                            last = dve.bn_aggr(mv[u][:, t, :], st[u][:, t, :])
                        last.then_inc(s_mv[u], 1)

                    def normalise(u):
                        dve.wait_ge(s_rs[u], 1)
                        if u == 1 and p:
                            dve.wait_ge(s_xt[0], 1)
                        if u == 3 and m:
                            dve.wait_ge(s_xt[2], 1)
                        for t in range(NT):
                            last = dve.tensor_scalar(xn[u // 2][:, t, :], xs[u][:, t, :], mv[u][:, t, 0:1],
                                                     rstd[u][:, t:t + 1], ALU.subtract, ALU.mult)
                        last.then_inc(s_xn[u], 1)

                    def causal_maxima(h):
                        for c, parts in enumerate(CAUSAL):
                            u = 3 * h + c
                            dve.wait_ge(s_s1[0], u + 1)
                            for t, at in parts:
                                last = dve.tensor_reduce(nm[0][:, t, h:h + 1],
                                                         bank[a1_bank(u)][:, at:at + (t + 1) * P], AX_X, ALU.max,
                                                         negate=True)
                            last.then_inc(s_m1[0], 1)

                    def norm_four(k, g):
                        dve.wait_ge(s_tv[k], g + 1)
                        ps = bank[7][:, :].rearrange("p (t j e) -> p t j e", t=NT, j=HPQ)
                        dve.reciprocal(rzo[k][:, :, :], ps[:, :, :, HD]).then_inc(s_rzo[k], 1)
                        dve.wait_ge(s_rzo[k], g + 1)
                        dve.tensor_tensor(
                            o[k][:, :, g * HPQ * HD:(g + 1) * HPQ * HD].rearrange("p t (j d) -> p t j d", d=HD),
                            ps[:, :, :, 0:HD],
                            rzo[k][:, :, :].rearrange("p t (j a) -> p t j a", a=1).broadcast_to([P, NT, HPQ, HD]),
                            ALU.mult).then_inc(s_o[k], 1)

                    def residual(u, ps, written, before):
                        dve.wait_ge(written, 1)
                        dve.tensor_tensor(xs[u][:, :, :].rearrange("p t d -> p (t d)"), ps[:, :],
                                          before[:, :, :].rearrange("p t d -> p (t d)"), ALU.add
                                          ).then_inc(s_xr[u], 1)

                    def hidden(k, c, ps):
                        dve.wait_ge(s_g[k], FC + c + 1)
                        dve.wait_ge(s_sil[k], 1)
                        dve.tensor_tensor(gated[:, k, c, :], ps[:, :], gated[:, k, c, :], ALU.mult
                                          ).then_inc(s_hid[k], 1)

                    def entropy(n):
                        h, t = n // NT, n % NT
                        if n:
                            dve.wait_ge(s_bn, n)
                        dve.wait_ge(s_bt, n + 1)
                        dve.scalar_tensor_tensor(out=junk[:, :], in0=RING[n % RN][:, :], scalar=thr[:, h, t:t + 1],
                                                 in1=E[:, n % NE, :], op0=ALU.max, op1=ALU.mult,
                                                 accum_out=acc[:, h, t:t + 1]).then_inc(s_bn, 1)
                        if t == NT - 1:
                            dve.reciprocal(rz[:, h, :], Z[:, h, :]).then_inc(s_brz, 1)

                    def small_maxima(h):
                        dve.wait_ge(s_s1[1], h + 1)
                        dve.tensor_reduce(nm[1][:, :, h], bank[h % 3][:, 0:NT * NK].rearrange(
                            "p (t k) -> p t k", t=NT), AX_X, ALU.max, negate=True).then_inc(s_m1[1], 1)

                    def probabilities(n):
                        h, t = n // NT, n % NT
                        dve.wait_ge(s_bn, n + 1)
                        dve.wait_ge(s_brz, h + 1)
                        dve.tensor_scalar(E[:, n % NE, :], E[:, n % NE, :], rz[:, h, t:t + 1], None, ALU.mult
                                          ).then_inc(s_scv, 1)

                    if m:
                        stats(2)
                    for h in range(A1_PRE):
                        if a:
                            causal_maxima(h)
                        if s:
                            for hs in s1_heads(h):
                                small_maxima(hs)
                        if m and h == 0:
                            normalise(2)
                    if m:
                        dve.wait_ge(s_sq, 2)
                        dve.tensor_reduce(n2[:, :, :, :].rearrange("p i t h -> p (i t h)"),
                                          kw[:, :, :, :].rearrange("p i t (h d) -> p (i t h) d", d=HD), AX_X,
                                          ALU.add).then_inc(s_n2, 1)
                        dve.wait_ge(s_n2, 1)
                        dve.tensor_scalar(ncl[:, :, :, :], n2[:, :, :, :], 1e-18, None, ALU.max).then_inc(s_n2, 1)
                    for n in range(STEPS):
                        if m and n < NMAIN:
                            h, t = n // NT, n % NT
                            dve.wait_ge(s_bs, n + 1)
                            dve.tensor_reduce(nmB[:, h, t:t + 1], RING[n % RN][:, :], AX_X, ALU.max, negate=True
                                              ).then_inc(s_bm, 1)
                        if m and 2 <= n < NMAIN + 2:
                            entropy(n - 2)
                        if m and n - INFL_LAG in ON_DVE:
                            probabilities(n - INFL_LAG)
                        if m:
                            if n == M_TAIL:
                                dve.wait_ge(s_bn, NMAIN)
                                dve.wait_ge(s_brz, H)
                                dve.tensor_scalar(E[:, LAST % NE, :], E[:, LAST % NE, :], rz[:, H - 1, 0:1], None,
                                                  ALU.mult).then_inc(s_last, 1)
                                for t in range(1, NT):
                                    dve.wait_ge(s_last, t)
                                    dve.scalar_tensor_tensor(out=E[:, LAST % NE, :], in0=E[:, LAST % NE + t, :],
                                                             scalar=rz[:, H - 1, t:t + 1], in1=E[:, LAST % NE, :],
                                                             op0=ALU.mult, op1=ALU.add).then_inc(s_last, 1)
                                dve.wait_ge(s_bn, NMAIN)
                                dve.wait_ge(s_brz, H)
                                dve.tensor_tensor(t1[:, :, :], acc[:, :, :], rz[:, :, :], ALU.mult).then_inc(s_imp, 1)
                                dve.wait_ge(s_imp, 1)
                                dve.scalar_tensor_tensor(out=t2[:, :, :], in0=t1[:, :, :], scalar=LOG_CLIP, in1=thr[:, :, :],
                                                         op0=ALU.add, op1=ALU.subtract).then_inc(s_imp, 1)
                                dve.wait_ge(s_imp, 2)
                                dve.scalar_tensor_tensor(out=t3[:, :, :], in0=t2[:, :, :], scalar=0.4 / 0.3, in1=rz[:, :, :],
                                                         op0=ALU.mult, op1=ALU.add).then_inc(s_imp, 1)
                                dve.wait_ge(s_imp, 3)
                                dve.tensor_reduce(own[:, :], t3[:, :, :].rearrange("p h t -> p t h"), AX_X, ALU.add
                                                  ).then_inc(s_imp, 1)
                            if n == M_TAIL + 2:
                                dve.wait_ge(s_ic, 1)
                                dve.wait_ge(s_imp, 4)
                                dve.tensor_tensor(imp[:, :], own[:, :], bank[0][:, 0:NT], ALU.add).then_inc(s_imp, 1)
                                dve.wait_ge(s_imp, 5)
                                for t in range(NT):
                                    last = dve.tensor_scalar(wrep[:, t, :], identf[:, :], imp[:, t:t + 1], None, ALU.mult)
                                last.then_inc(s_dg, 1)
                            if n == M_TAIL + 4:
                                dve.wait_ge(s_rb, 1)
                                for t in range(NT):
                                    dve.tensor_scalar(E[:, t, 0:T - t * P], bank[6][:, t * P:T], imp[:, t:t + 1], None,
                                                      ALU.is_gt, ALU.add, accum_out=cnt[:, 0, t:t + 1])
                                    dve.scalar_tensor_tensor(out=E[:, 4, t * P:(t + 1) * P],
                                                             in0=bank[6][:, t * P:(t + 1) * P], scalar=imp[:, t:t + 1],
                                                             in1=tri[:, :], op0=ALU.is_equal, op1=ALU.mult,
                                                             accum_out=cnt[:, 1, t:t + 1])
                                    if t:
                                        last = dve.tensor_scalar(E[:, 4 + t, 0:t * P], bank[6][:, 0:t * P],
                                                                 imp[:, t:t + 1], None, ALU.is_ge, ALU.add,
                                                                 accum_out=cnt[:, 2, t:t + 1])
                                    else:
                                        dve.memset(cnt[:, 2, 0:1], 0.0)
                                last.then_inc(s_cnt, 1)
                                dve.wait_ge(s_cnt, 1)
                                dve.tensor_tensor(rank2[:, :], cnt[:, 0, :], cnt[:, 1, :], ALU.add).then_inc(s_cnt, 1)
                                dve.wait_ge(s_cnt, 2)
                                dve.tensor_tensor(rank[:, :], rank2[:, :], cnt[:, 2, :], ALU.add).then_inc(s_cnt, 1)
                                dve.wait_ge(s_cnt, 3)
                                for t in range(NT):
                                    last = dve.tensor_scalar(sel[:, t, :], iota_f[:, :], rank[:, t:t + 1], None,
                                                             ALU.is_equal)
                                last.then_inc(s_sel, 1)
                            if n == M_TAIL + 6:
                                dve.wait_ge(s_gat, 1)
                                dve.tensor_copy(kcat[:, L:NK], bank[6][:, 0:HH])
                                dve.tensor_copy(vcat[L:NK, :, :], bank[6][L:NK, P:2 * P].rearrange("p (h d) -> p h d", d=HD))
                        if a and n < H - A1_PRE:
                            causal_maxima(A1_PRE + n)
                        if m:
                            if n == 0:
                                dve.wait_ge(s_root, 2)
                                dve.reciprocal(nrec[:, :, :, :], nroot[:, :, :, :]).then_inc(s_newton, 1)
                                dve.wait_ge(s_newton, 1)
                                dve.scalar_tensor_tensor(out=nquot[:, :, :, :], in0=n2[:, :, :, :], scalar=0.5,
                                                         in1=nrec[:, :, :, :], op0=ALU.mult, op1=ALU.mult
                                                         ).then_inc(s_newton, 1)
                                dve.wait_ge(s_newton, 2)
                                dve.scalar_tensor_tensor(out=nrm[:, :, :, :], in0=nroot[:, :, :, :], scalar=0.5,
                                                         in1=nquot[:, :, :, :], op0=ALU.mult, op1=ALU.add
                                                         ).then_inc(s_nrm, 1)
                            if n in (2, 4):
                                c = (n - 2) // 2
                                dve.wait_ge(s_nt, c + 1)
                                dve.tensor_reduce(nnm[:, c:c + 1], bank[7][0:H, :], AX_X, ALU.max, negate=True
                                                  ).then_inc(s_nnm, 1)
                            if n in (3, 5):
                                c = (n - 3) // 2
                                dve.wait_ge(s_ew, c + 1)
                                dve.reciprocal(rzw[:, c:c + 1], zw[:, c:c + 1]).then_inc(s_rzw, 1)
                            if n == 9:
                                dve.wait_ge(s_wte, 1)
                                dve.tensor_tensor(kw[:, :, :, :].rearrange("p i t (h d) -> p (i t h) d", d=HD),
                                                  ktok[:, :, :, :].rearrange("p i t (h d) -> p (i t h) d", d=HD),
                                                  wt[:, :, :, :].rearrange("p i t (h a) -> p (i t h) a", a=1
                                                                           ).broadcast_to([P, 2 * NT * H, HD]),
                                                  ALU.mult).then_inc(s_kw, 1)
                            if n == 12:
                                dve.wait_ge(s_cmp, 1)
                                dve.tensor_scalar(den[:, :], bank[7][:, L:2 * L], 1e-8, None, ALU.add)
                                dve.tensor_scalar(vden[:, :], bank[7][0:L, 3 * P:3 * P + H], 1e-8, None, ALU.add
                                                  ).then_inc(s_den, 1)
                                dve.wait_ge(s_den, 1)
                                dve.reciprocal(rden[:, :], den[:, :])
                                dve.reciprocal(vrden[:, :], vden[:, :]).then_inc(s_rden, 1)
                                dve.wait_ge(s_rden, 1)
                                if s:
                                    dve.wait_ge(s_kp, 1)
                                    dve.wait_ge(s_vs, 1)
                                dve.tensor_tensor(kcat[:, 0:L], bank[7][:, 0:L], rden[:, :], ALU.mult).then_inc(s_cat, 1)
                                dve.tensor_tensor(vcat[0:L, :, :],
                                                  bank[7][0:L, 2 * P:3 * P].rearrange("p (h d) -> p h d", d=HD),
                                                  vrden[:, :].rearrange("p (h a) -> p h a", a=1).broadcast_to([L, H, HD]),
                                                  ALU.mult).then_inc(s_cat, 1)
                        if s:
                            if n in DIVIDE_AT[1]:
                                norm_four(1, DIVIDE_AT[1].index(n))
                            if n == S_TAIL + 3:
                                dve.wait_ge(s_x2ld, DMA)
                                residual(3, bank[7], s_op[1], x2s)
                                dve.wait_ge(s_xr[3], 1)
                                stats(3)
                            if n == S_TAIL + 5:
                                normalise(3)
                            for c in range(FC):
                                if n - 1 == S_UP_AT[c]:
                                    hidden(1, c, S_UP_BANK[c])
                            if n == S_DOWN_AT + 2:
                                residual(4, bank[4], s_dn[1], xs[3])
                        if a:
                            if n in DIVIDE_AT[0]:
                                norm_four(0, DIVIDE_AT[0].index(n))
                            if n == A_TAIL + 3:
                                residual(1, bank[7], s_op[0], xbo)
                                dve.wait_ge(s_xr[1], 1)
                                stats(1)
                            if n == A_TAIL + 6:
                                normalise(1)
                            if n == A_TAIL + 13:
                                for c in range(FC):
                                    hidden(0, c, bank[3 + c])
                            if n == A_TAIL + 15:
                                if m:
                                    dve.wait_ge(s_xn[2], 1)
                                residual(2, bank[3], s_dn[0], xs[1])
                        if p:
                            if n == P_TAIL - 4:
                                dve.wait_ge(s_xin, DMA)
                                stats(0)
                            if n == P_TAIL - 1:
                                normalise(0)
                            if n == P_TAIL + 7:
                                dve.wait_ge(s_proj[0], 3)
                                if a:
                                    dve.wait_ge(s_pv[0], 3 * H)
                                for t in range(NT):
                                    last = dve.tensor_tensor(
                                        vA[:, t, :, 0:HD],
                                        bank[5][:, t * P:(t + 1) * P].rearrange("p (h d) -> p h d", d=HD),
                                        bv[:, :].rearrange("p (h d) -> p h d", d=HD), ALU.add)
                                last.then_inc(s_vt[0], 1)

                @block.tensor
                def _(pe):
                    def ln(u, ps):
                        pe.wait_ge(s_xn[u], 1)
                        for t in range(NT):
                            last = pe.transpose(ps[:, t * P:(t + 1) * P], xn[u // 2][:, t, :], identf[:, :])
                        last.then_inc(s_xt[u], 1)

                    def channels_by(w, k, u, ps):
                        pe.matmul(ps[:, :], w, xnT[XN[u]][:, :], start=True, stop=True).then_inc(s_proj[k], 1)

                    def tokens_by(w, k, u, ps):
                        for t in range(NT):
                            last = pe.matmul(ps[:, t * P:(t + 1) * P], xnT[XN[u]][:, t * P:(t + 1) * P], w,
                                             start=True, stop=True)
                        last.then_inc(s_proj[k], 1)

                    def causal_scores(h):
                        for c, parts in enumerate(CAUSAL):
                            u = 3 * h + c
                            if a1_before(u):
                                pe.wait_ge(s_m1[0], a1_before(u))
                            for t, at in parts:
                                pe.matmul(bank[a1_bank(u)][:, at:at + (t + 1) * P],
                                          qst[0][0:A_SC, h, t * P:(t + 1) * P], kst[0][0:A_SC, h, 0:(t + 1) * P],
                                          start=True, stop=True)
                                last = pe.matmul(bank[a1_bank(u)][:, at + t * P:at + (t + 1) * P], identb[:, :],
                                                 maskqk[:, :], start=False, stop=True, skip_group_check=True)
                            last.then_inc(s_s1[0], 1)

                    def transpose_max(k):
                        for t in range(NT):
                            last = pe.transpose(bank[5][0:H, t * P:(t + 1) * P], nm[k][:, t, :], identf[:, :])
                        last.then_inc(s_mt[k], 1)

                    def causal_minus_max(u):
                        h, parts = u // 3, TILES[u % 3]
                        if u >= 2:
                            pe.wait_ge(s_p[0], u - 1)
                        elif s:
                            pe.wait_ge(s_p[1], H)
                        for k, at in parts:
                            w = T - k * P
                            pe.matmul(bank[3 + u % 2][:, at:at + w], kst[0][0:A_MX, h, k * P:(k + 1) * P],
                                      qst[0][0:A_MX, h, k * P:T], start=True, stop=True)
                            last = pe.matmul(bank[3 + u % 2][:, at:at + P], identb[:, :], maskkq[:, :],
                                             start=False, stop=True, skip_group_check=True)
                        last.then_inc(s_s2[0], 1)

                    def weigh(u):
                        h, c = u // 3, u % 3
                        pe.wait_ge(s_p[0], u + 1)
                        if h >= HPQ and h % HPQ == 0:
                            pe.wait_ge(s_ov[0], h // HPQ)
                        if h == 0 and s:
                            pe.wait_ge(s_ov[1], H // HPQ)
                        elif h == 0:
                            pe.wait_ge(s_ma[0], 1)
                        q = QROWS * (h % HPQ)
                        for k, at in TILES[c]:
                            last = pe.matmul(bank[5][q:q + HD + 1, k * P:T], vA[:, k, h, :],
                                             pT[h % 2][:, c * T + at:c * T + at + T - k * P], start=(k == 0),
                                             stop=True, skip_group_check=(k > 0))
                        last.then_inc(s_pv[0], 1)

                    def weigh_hh(h):
                        pe.wait_ge(s_p[1], h + 1)
                        if h >= HPQ and h % HPQ == 0:
                            pe.wait_ge(s_ov[1], h // HPQ)
                        if h == 0 and a:
                            pe.wait_ge(s_ma[0], 1)
                        elif h == 0:
                            pe.wait_ge(s_ma[1], 1)
                        q = QROWS * (h % HPQ)
                        pe.matmul(bank[5][q:q + HD + 1, :], vsm[0:NK, h, :], p2[h % 2][0:NK, :], start=True,
                                  stop=True).then_inc(s_pv[1], 1)

                    def turn(k, g):
                        pe.wait_ge(s_ov[k], g + 1)
                        if g:
                            pe.wait_ge(s_o[k], g)
                        elif m:
                            pe.wait_ge(s_cat, 2)
                        if k == 0 and s:
                            if g == 0:
                                pe.wait_ge(s_xe[3], 1)
                            elif g == 1:
                                pe.wait_ge(s_gc[1], 2)
                            else:
                                pe.wait_ge(s_hid[1], 1)
                        for t in range(NT):
                            last = pe.transpose(bank[7][:, t * P:(t + 1) * P], ov[:, t * P:(t + 1) * P], identf[:, :])
                        last.then_inc(s_tv[k], 1)

                    def full_scores(n):
                        h, t = n // NT, n % NT
                        if n >= RN:
                            pe.wait_ge(s_bn, n - RN + 1)
                        elif RING[n] is bank[6]:
                            pe.wait_ge(s_vt[1], 2)
                        elif n == 0 and s:
                            pe.wait_ge(s_m1[1], H)
                        elif n == 0 and a:
                            pe.wait_ge(s_m1[0], 3 * (A1_PRE - 4))
                        pe.matmul(RING[n % RN][:, :], qst[1][0:B_SC, h, t * P:(t + 1) * P],
                                  kst[1][0:B_SC, h, :], start=True, stop=True).then_inc(s_bs, 1)

                    def transpose_out(k, ps):
                        pe.wait_ge(s_o[k], H // HPQ)
                        for t in range(NT):
                            last = pe.transpose(ps[:, t * P:(t + 1) * P], o[k][:, t, :], identf[:, :])
                        last.then_inc(s_ot[k], 1)

                    def project_out(k, w, ps):
                        pe.wait_ge(s_oe[k], 1)
                        for t in range(NT):
                            last = pe.matmul(ps[:, t * P:(t + 1) * P], oT[k][:, t * P:(t + 1) * P], w,
                                             start=True, stop=True)
                        last.then_inc(s_op[k], 1)

                    def gate(k, c, ps):
                        if c == 0:
                            pe.wait_ge(s_xe[2 * k + 1], 1)
                        elif k:
                            pe.wait_ge(s_gc[k], c)
                        pe.matmul(ps[:, :], wgT[:, c, :], xnT[k][:, :], start=True, stop=True).then_inc(s_g[k], 1)

                    def up(k, c, ps):
                        if c == 0:
                            pe.wait_ge(s_gc[k], FC)
                        pe.matmul(ps[:, :], wuT[:, c, :], xnT[k][:, :], start=True, stop=True).then_inc(s_g[k], 1)

                    def down(k, ps):
                        pe.wait_ge(s_hid[k], FC)
                        for t in range(NT):
                            for c in range(FC):
                                last = pe.matmul(ps[:, t * P:(t + 1) * P], gated[:, k, c, t * P:(t + 1) * P],
                                                 wdT[:, c, :], start=(c == 0), stop=(c == FC - 1))
                        last.then_inc(s_dn[k], 1)

                    def small_scores(h):
                        if h >= 3:
                            pe.wait_ge(s_m1[1], h - 2)
                        elif h == 0:
                            pe.wait_ge(s_kc, NPAIR * DMA)
                            pe.wait_ge(s_qsm, NPAIR * DMA)
                            if a:
                                pe.wait_ge(s_m1[0], 3 * (A1_PRE - 4))
                        for t in range(NT):
                            last = pe.matmul(bank[h % 3][:, t * NK:(t + 1) * NK],
                                             qsm[0:B_SC, h, t * P:(t + 1) * P], kcst[0:B_SC, h, :],
                                             start=True, stop=True)
                        last.then_inc(s_s1[1], 1)

                    for h in range(A1_PRE):
                        if a:
                            causal_scores(h)
                        if s:
                            for hs in s1_heads(h):
                                small_scores(hs)
                        if not m:
                            continue
                        if h == 1:
                            ln(2, bank[6])
                            pe.wait_ge(s_xe[2], 1)
                            channels_by(wqb[:, 0, :], 1, 2, bank[6])
                            channels_by(wqb[:, 1, :], 1, 2, bank[7])
                            tokens_by(wqb[:, 1, :], 1, 2, bank[5])
                        if h == 2:
                            pe.wait_ge(s_qf[1], 1)
                            tokens_by(wqb[:, 2, :], 1, 2, bank[6])
                    if m:
                        pe.wait_ge(s_stack[1], 2 * NPAIR * DMA)
                        for n in range(LEAD):
                            full_scores(n)
                    for n in range(STEPS):
                        if m and n + LEAD < NMAIN:
                            full_scores(n + LEAD)
                        if m:
                            if n == M_TAIL + 1:
                                pe.wait_ge(s_bi, LAST + 1)
                                pe.wait_ge(s_last, NT)
                                for t in range(NT):
                                    pe.matmul(bank[0][:, t:t + 1], psum[:, t * P:(t + 1) * P], onesf[:, 0:1],
                                              start=True, stop=False)
                                    last = pe.matmul(bank[0][:, t:t + 1], E[:, LAST % NE, t * P:(t + 1) * P],
                                                     onesf[:, 0:1], start=False, stop=True)
                                last.then_inc(s_ic, 1)
                            if n == M_TAIL + 3:
                                pe.wait_ge(s_dg, 1)
                                for t in range(NT):
                                    last = pe.matmul(bank[6][:, t * P:(t + 1) * P], onesf[:, :], wrep[:, t, :], start=True,
                                                     stop=True)
                                last.then_inc(s_rb, 1)
                            if n == M_TAIL + 5:
                                pe.wait_ge(s_sel, 1)
                                for t in range(NT):
                                    pe.matmul(bank[6][:, 0:HH], ktok[:, 0, t, :], sel[:, t, :], start=(t == 0),
                                              stop=(t == NT - 1))
                                for t in range(NT):
                                    last = pe.matmul(bank[6][L:NK, P:2 * P], sel[:, t, :], ktok[:, 1, t, :], start=(t == 0),
                                                     stop=(t == NT - 1))
                                last.then_inc(s_gat, 1)
                        if s and n == 0:
                            pe.wait_ge(s_m1[1], H)
                            if m:
                                pe.wait_ge(s_vt[1], 1)
                            transpose_max(1)
                        if a and n < H - A1_PRE:
                            causal_scores(A1_PRE + n)
                        if a and n == S2_AT:
                            pe.wait_ge(s_m1[0], 3 * H)
                            if s:
                                pe.wait_ge(s_ma[1], 1)
                            elif m:
                                pe.wait_ge(s_vt[1], 1)
                            transpose_max(0)
                        if m:
                            if n in (1, 3):
                                c = (n - 1) // 2
                                if c:
                                    pe.wait_ge(s_ew, 1)
                                else:
                                    pe.wait_ge(s_vt[1], 2)
                                    pe.wait_ge(s_nrm, 1)
                                for t in range(NT):
                                    last = pe.transpose(bank[7][0:H, t * P:(t + 1) * P], nrm[:, c, t, :], identf[:, :])
                                last.then_inc(s_nt, 1)
                            if n == 7:
                                pe.wait_ge(s_ew, 2)
                                pe.wait_ge(s_wn, 2)
                                for c in range(2):
                                    for t in range(NT):
                                        at = (c * NT + t) * H
                                        last = pe.matmul(bank[7][:, at:at + H], ew[:, c, t * P:(t + 1) * P],
                                                         identf[0:H, 0:H], start=True, stop=True)
                                last.then_inc(s_wt, 1)
                            if n == 10:
                                pe.wait_ge(s_wte, 1)
                                pe.wait_ge(s_kw, 1)
                                pe.wait_ge(s_wrep, 1)
                                for t in range(NT):
                                    own_g = group[:, t, t * GPT:(t + 1) * GPT]
                                    pe.matmul(bank[7][:, t * GPT:(t + 1) * GPT], kw[:, 0, t, :], own_g, start=True,
                                              stop=True)
                                    pe.matmul(bank[7][:, L + t * GPT:L + (t + 1) * GPT], wrep[:, t, :], own_g,
                                              start=True, stop=True)
                            if n == 11:
                                for t in range(NT):
                                    pe.matmul(bank[7][0:L, 2 * P:3 * P], group[:, t, :], kw[:, 1, t, :], start=(t == 0),
                                              stop=(t == NT - 1))
                                for t in range(NT):
                                    last = pe.matmul(bank[7][0:L, 3 * P:3 * P + H], group[:, t, :], wt[:, 1, t, :],
                                                     start=(t == 0), stop=(t == NT - 1))
                                last.then_inc(s_cmp, 1)
                        if s:
                            if n == S2_AT:
                                pe.wait_ge(s_mrow[1], DMA)
                                if a:
                                    pe.wait_ge(s_m1[0], 3 * H)
                            for h in s2_heads(n):
                                if h >= 2:
                                    pe.wait_ge(s_p[1], h - 1)
                                pe.matmul(bank[3 + h % 2][0:NK, :], kcst[0:B_MX, h, :], qsm[0:B_MX, h, :],
                                          start=True, stop=True).then_inc(s_s2[1], 1)
                            for h in s2_heads(n - 1):
                                weigh_hh(h)
                            if n in TURN_AT[1]:
                                turn(1, TURN_AT[1].index(n))
                            if n == S_TAIL:
                                transpose_out(1, bank[7])
                            if n == S_TAIL + 2:
                                project_out(1, wqb[:, 3, :], bank[7])
                            if n == S_TAIL + 6:
                                pe.wait_ge(s_xr[3], 1)
                                ln(3, bank[7])
                            if n in S_GATE_AT:
                                c = S_GATE_AT.index(n)
                                if a and c != 1:
                                    pe.wait_ge(s_o[0], 2 if c else 1)
                                gate(1, c, bank[7])
                            for c in range(FC):
                                if n == S_UP_AT[c]:
                                    if a and c == 0:
                                        pe.wait_ge(s_o[0], 2)
                                    if a and c == 1:
                                        pe.wait_ge(s_p[0], 3 * H)
                                    up(1, c, S_UP_BANK[c])
                            if n == S_DOWN_AT:
                                down(1, bank[4])
                        if a:
                            if n == A2_AT:
                                pe.wait_ge(s_mrow[0], DMA)
                            for u in a2_tiles(n):
                                causal_minus_max(u)
                                if u > 2:
                                    weigh(u - 3)
                            if n == A2_END:
                                for u in range(3 * H - 3, 3 * H):
                                    weigh(u)
                            if n in TURN_AT[0]:
                                turn(0, TURN_AT[0].index(n))
                            if n == A_TAIL:
                                transpose_out(0, bank[7])
                            if n == A_TAIL + 2:
                                project_out(0, woutT[:, :], bank[7])
                            if n == A_TAIL + 7:
                                pe.wait_ge(s_xr[1], 1)
                                ln(1, bank[7])
                            if n == A_TAIL + 9:
                                pe.wait_ge(s_p[0], 3 * H)
                                pe.wait_ge(s_ov[0], H // HPQ)
                                if s:
                                    pe.wait_ge(s_xr[4], 1)
                                if p:
                                    pe.wait_ge(s_vt[0], 1)
                                for c in range(FC):
                                    gate(0, c, bank[3 + c])
                            if n == A_TAIL + 11:
                                for c in range(FC):
                                    up(0, c, bank[3 + c])
                            if n == A_TAIL + 14:
                                down(0, bank[3])
                        if p:
                            if n == P_TAIL:
                                if a:
                                    pe.wait_ge(s_ov[0], H // HPQ)
                                ln(0, bank[5])
                            if n == P_TAIL + 2:
                                pe.wait_ge(s_xe[0], 1)
                                channels_by(wqkvT[:, 0:P], 0, 0, bank[5])
                            if n == P_TAIL + 4:
                                pe.wait_ge(s_qf[0], 1)
                                channels_by(wqkvT[:, P:2 * P], 0, 0, bank[5])
                            if n == P_TAIL + 6:
                                pe.wait_ge(s_qf[0], 2)
                                tokens_by(wqkvT[:, 2 * P:3 * P], 0, 0, bank[5])
            nc.sync.sem_clear(range(s_xin.num, s_kc.num + 1))
            nc.all_engine_barrier()

        one_pass(-1, False, True, False, False)
        one_pass(0, True, True, False, False)
        one_pass(1, True, True, True, False)
        with nc.Fori(2, B - 1) as batch:
            one_pass(batch, True, True, True, True)
        one_pass(B - 1, True, False, True, True)
        one_pass(B, False, False, True, True)
        one_pass(B + 1, False, False, False, True)


_INS = ['L0_attn_a_x', 'L0_attn_a_w_qkv', 'L0_attn_a_b_qkv', 'L0_attn_a_w_out', 'L0_attn_a_b_out',
        'L0_attn_b_Wq', 'L0_attn_b_Wk', 'L0_attn_b_Wv', 'L0_attn_b_Wo',
        'L0_ffn_w_gate', 'L0_ffn_w_up', 'L0_ffn_w_down']
_OUTS = [((8, 512, 128), 'float32')]


def kernel(**inputs):
    import numpy as _np
    import concourse.bacc as _bacc
    from concourse import mybir as _mybir
    from concourse.bass_utils import run_bass_kernel_spmd as _run

    nc = _bacc.Bacc("TRN2", target_bir_lowering=False, num_devices=1)
    arrays, args = {}, []
    for name in _INS:
        a = _np.ascontiguousarray(inputs[name])
        arrays[f"in_{name}_dram"] = a
        args.append(nc.dram_tensor(f"in_{name}_dram", a.shape, _mybir.dt.from_np(a.dtype), kind="ExternalInput").ap())
    for i, (shape, dtype) in enumerate(_OUTS):
        dt = _mybir.dt.from_np(_np.dtype(dtype))
        args.append(nc.dram_tensor(f"out_{i}_dram", shape, dt, kind="ExternalOutput").ap())
    hybrid_block(nc, *args)
    r = _run(nc, [arrays], core_ids=[0])
    got = tuple(r.results[0][f"out_{i}_dram"] for i in range(len(_OUTS)))
    return got[0]
```
